# Optimizing a Trainium2 kernel written in Bass

```python
import numpy as np
import jax
import jax.numpy as jnp

def _softmax(x, axis=-1):
    return jax.nn.softmax(x, axis=axis)

def _gelu(x):
    return jax.nn.gelu(x, approximate=True)

def _silu(x):
    return jax.nn.silu(x)

def _sigmoid(x):
    return jax.nn.sigmoid(x)

def _layernorm(x, axis=-1, eps=1e-05):
    m = jnp.mean(x, axis=axis, keepdims=True)
    v = jnp.var(x, axis=axis, keepdims=True)
    return (x - m) / jnp.sqrt(v + eps)

def _scatter_add(tgt, idx, src, axis=0):
    return tgt.at[idx].add(src)

def _segment_sum(src, seg, n):
    return jax.ops.segment_sum(src, seg, n)
kernel_name = 'mk_adaln_d2_jaxref_r8_ac14e2'

def setup_inputs(seed: int=0):
    np.random.seed(seed)
    _w = jnp.asarray

    def _L0_attn_setup():
        import jax, jax.numpy as jnp
        import numpy as np
        HEADS = 8
        BLOCK = 32
        key = jax.random.key(seed)
        ks = jax.random.split(key, 4)
        b, n, d, f = (4, 512, 128, 128)
        x = jax.random.normal(ks[0], (b, n, d), dtype=jnp.float32)
        w_qkv = jax.random.normal(ks[1], (3 * d, d), dtype=jnp.float32) * d ** (-0.5)
        w_out = jax.random.normal(ks[2], (d, d), dtype=jnp.float32) * d ** (-0.5)
        b_out = jnp.zeros((d,), dtype=jnp.float32)
        proj = jax.random.normal(ks[3], (HEADS, d // HEADS, f), dtype=jnp.float32) * (d // HEADS) ** (-0.5)
        return {'x': x, 'w_qkv': w_qkv, 'w_out': w_out, 'b_out': b_out, 'proj': proj}
    _L0_attn_in = _L0_attn_setup()

    def _L0_ffn_setup():
        import jax, jax.numpy as jnp
        import numpy as np
        B, SEQ, D, E, F = (4, 128, 128, 8, 512)
        CAPACITY = 2
        key = jax.random.key(seed)
        ks = jax.random.split(key, 8)
        x = jax.random.normal(ks[0], (B, SEQ, D), jnp.float32)
        gate_weight = jax.random.normal(ks[1], (E, D), jnp.float32) * 0.006
        W1 = jax.random.normal(ks[2], (E, D, F), jnp.float32) * (1.0 / np.sqrt(D))
        b1 = jnp.zeros((E, F), jnp.float32)
        W2 = jax.random.normal(ks[3], (E, F, D), jnp.float32) * (1.0 / np.sqrt(F))
        b2 = jnp.zeros((E, D), jnp.float32)
        Ws1 = jax.random.normal(ks[4], (D, F), jnp.float32) * (1.0 / np.sqrt(D))
        bs1 = jnp.zeros((F,), jnp.float32)
        Ws2 = jax.random.normal(ks[5], (F, D), jnp.float32) * (1.0 / np.sqrt(F))
        bs2 = jnp.zeros((D,), jnp.float32)
        return {'x': x, 'gate_weight': gate_weight, 'W1': W1, 'b1': b1, 'W2': W2, 'b2': b2, 'Ws1': Ws1, 'bs1': bs1, 'Ws2': Ws2, 'bs2': bs2}
    _L0_ffn_in = _L0_ffn_setup()
    _L0_c = _w((lambda *s: np.random.randn(*s).astype(np.float32) * 0.05)(2, 128))
    _L0_wmod = _w((lambda *s: np.random.randn(*s).astype(np.float32) * 0.05)(128, 6 * 128) * 128 ** (-0.5))

    def _L1_attn_setup():
        import jax, jax.numpy as jnp
        import numpy as np
        B, T, D, P, ALPHA, PR = (4, 512, 128, 64, 4, 64)
        key = jax.random.key(seed)
        ks = jax.random.split(key, 9)
        g = lambda k, shape, scale: jax.random.normal(k, shape, jnp.float32) * scale
        return {'x': jax.random.normal(ks[0], (B, T, D), jnp.float32), 'W_toP': g(ks[1], (D, P), D ** (-0.5)), 'W_U': g(ks[2], (D, P, ALPHA), D ** (-0.5)), 'W_F': g(ks[3], (D, P), D ** (-0.5)), 'W_V': g(ks[4], (P, ALPHA), 1.0), 'W_lam': g(ks[5], (P, PR), P ** (-0.5)), 'B_mat': g(ks[6], (P, PR), P ** (-0.5)), 'C_mat': g(ks[7], (PR, P), PR ** (-0.5)), 'W_fromP': g(ks[8], (P, D), P ** (-0.5))}
    _L1_attn_in = _L1_attn_setup()

    def _L1_ffn_setup():
        import jax, jax.numpy as jnp
        import numpy as np
        E, K, NG, TG = (64, 8, 8, 4)
        CAP = 128
        SCALE = 2.5

        def _route(x_flat, gate_weight, e_bias):
            T = x_flat.shape[0]
            logits = x_flat.astype(jnp.float32) @ gate_weight.astype(jnp.float32).T
            scores = jax.nn.sigmoid(logits)
            sfc = scores + e_bias[None, :]
            group_scores = jax.lax.top_k(sfc.reshape(T, NG, E // NG), 2)[0].sum(-1)
            _, gidx = jax.lax.top_k(group_scores, TG)
            gmask = jnp.zeros((T, NG), jnp.float32).at[jnp.arange(T)[:, None], gidx].set(1.0)
            smask = jnp.repeat(gmask, E // NG, axis=1)
            tmp = jnp.where(smask > 0, sfc, 0.0)
            _, topk_idx = jax.lax.top_k(tmp, K)
            topk_w = jnp.take_along_axis(scores, topk_idx, axis=1)
            topk_w = topk_w / (topk_w.sum(-1, keepdims=True) + 1e-20)
            return (topk_idx, topk_w * SCALE)

        def _moe_forward(hidden_states, gate_weight, e_bias, w1, w2, w3, shared_gate, shared_up, shared_down):
            B, S, H = hidden_states.shape
            T = B * S
            x = hidden_states.reshape(T, H)
            topk_idx, topk_w = _route(x, gate_weight, e_bias)
            Sk = T * K
            flat_e = topk_idx.reshape(-1)
            order = jnp.argsort(flat_e)
            sorted_e = flat_e[order]
            counts = jax.ops.segment_sum(jnp.ones((Sk,), jnp.int32), flat_e, num_segments=E)
            offsets = jnp.cumsum(counts) - counts
            pos = jnp.arange(Sk) - offsets[sorted_e]
            tok_sorted = x[order // K]
            xe = jnp.zeros((E, CAP, H), x.dtype).at[sorted_e, pos].set(tok_sorted, mode='drop')
            h = jax.nn.silu(jnp.einsum('ech,efh->ecf', xe, w1)) * jnp.einsum('ech,efh->ecf', xe, w3)
            ye = jnp.einsum('ecf,ehf->ech', h, w2)
            pos_c = jnp.minimum(pos, CAP - 1)
            vals = ye[sorted_e, pos_c]
            vals = jnp.where((pos < CAP)[:, None], vals, 0.0)
            flat_w = topk_w.reshape(-1)[order].astype(vals.dtype)
            flat_t = (jnp.arange(Sk) // K)[order]
            out = jax.ops.segment_sum(vals * flat_w[:, None], flat_t, num_segments=T)
            shared = jax.nn.silu(x @ shared_gate.T) * (x @ shared_up.T) @ shared_down.T
            return (out + shared).reshape(B, S, H)
        key = jax.random.key(seed)
        ks = jax.random.split(key, 9)
        B, S, H, F = (1, 256, 128, 64)
        bound = 1.0 / 32.0
        return {'hidden_states': jax.random.normal(ks[0], (B, S, H), jnp.float32), 'gate_weight': jax.random.uniform(ks[1], (E, H), jnp.float32, -bound, bound), 'e_bias': jnp.zeros((E,), jnp.float32), 'w1': jax.random.normal(ks[2], (E, F, H), jnp.float32) * 0.02, 'w2': jax.random.normal(ks[3], (E, H, F), jnp.float32) * 0.02, 'w3': jax.random.normal(ks[4], (E, F, H), jnp.float32) * 0.02, 'shared_gate': jax.random.normal(ks[5], (2 * F, H), jnp.float32) * 0.02, 'shared_up': jax.random.normal(ks[6], (2 * F, H), jnp.float32) * 0.02, 'shared_down': jax.random.normal(ks[7], (H, 2 * F), jnp.float32) * 0.02}
    _L1_ffn_in = _L1_ffn_setup()
    _L1_c = _w((lambda *s: np.random.randn(*s).astype(np.float32) * 0.05)(2, 128))
    _L1_wmod = _w((lambda *s: np.random.randn(*s).astype(np.float32) * 0.05)(128, 6 * 128) * 128 ** (-0.5))
    _d = {'L0_attn_x': _L0_attn_in['x'], 'L0_attn_w_qkv': _L0_attn_in['w_qkv'], 'L0_attn_w_out': _L0_attn_in['w_out'], 'L0_attn_b_out': _L0_attn_in['b_out'], 'L0_attn_proj': _L0_attn_in['proj'], 'L0_ffn_gate_weight': _L0_ffn_in['gate_weight'], 'L0_ffn_W1': _L0_ffn_in['W1'], 'L0_ffn_b1': _L0_ffn_in['b1'], 'L0_ffn_W2': _L0_ffn_in['W2'], 'L0_ffn_b2': _L0_ffn_in['b2'], 'L0_ffn_Ws1': _L0_ffn_in['Ws1'], 'L0_ffn_bs1': _L0_ffn_in['bs1'], 'L0_ffn_Ws2': _L0_ffn_in['Ws2'], 'L0_ffn_bs2': _L0_ffn_in['bs2'], 'L0_c': _L0_c, 'L0_wmod': _L0_wmod, 'L1_attn_W_toP': _L1_attn_in['W_toP'], 'L1_attn_W_U': _L1_attn_in['W_U'], 'L1_attn_W_F': _L1_attn_in['W_F'], 'L1_attn_W_V': _L1_attn_in['W_V'], 'L1_attn_W_lam': _L1_attn_in['W_lam'], 'L1_attn_B_mat': _L1_attn_in['B_mat'], 'L1_attn_C_mat': _L1_attn_in['C_mat'], 'L1_attn_W_fromP': _L1_attn_in['W_fromP'], 'L1_ffn_gate_weight': _L1_ffn_in['gate_weight'], 'L1_ffn_e_bias': _L1_ffn_in['e_bias'], 'L1_ffn_w1': _L1_ffn_in['w1'], 'L1_ffn_w2': _L1_ffn_in['w2'], 'L1_ffn_w3': _L1_ffn_in['w3'], 'L1_ffn_shared_gate': _L1_ffn_in['shared_gate'], 'L1_ffn_shared_up': _L1_ffn_in['shared_up'], 'L1_ffn_shared_down': _L1_ffn_in['shared_down'], 'L1_c': _L1_c, 'L1_wmod': _L1_wmod}
    _x0 = _d['L0_attn_x']
    _d['L0_attn_x'] = jax.random.normal(jax.random.fold_in(jax.random.key(seed), 1), (2, 2048, 128), dtype=_x0.dtype)
    del _x0
    return _d

def reference(L0_attn_x, L0_attn_w_qkv, L0_attn_w_out, L0_attn_b_out, L0_attn_proj, L0_ffn_gate_weight, L0_ffn_W1, L0_ffn_b1, L0_ffn_W2, L0_ffn_b2, L0_ffn_Ws1, L0_ffn_bs1, L0_ffn_Ws2, L0_ffn_bs2, L0_c, L0_wmod, L1_attn_W_toP, L1_attn_W_U, L1_attn_W_F, L1_attn_W_V, L1_attn_W_lam, L1_attn_B_mat, L1_attn_C_mat, L1_attn_W_fromP, L1_ffn_gate_weight, L1_ffn_e_bias, L1_ffn_w1, L1_ffn_w2, L1_ffn_w3, L1_ffn_shared_gate, L1_ffn_shared_up, L1_ffn_shared_down, L1_c, L1_wmod):

    def _L0_attn_ref(x, w_qkv, w_out, b_out, proj):
        import jax, jax.numpy as jnp
        import numpy as np
        HEADS = 8
        BLOCK = 32
        b, n, d = x.shape
        h = HEADS
        hd = d // h
        nb = n // BLOCK
        qkv = x @ w_qkv.T
        q, k, v = jnp.split(qkv, 3, axis=-1)

        def to_blocks(t):
            return t.reshape(b, n, h, hd).transpose(0, 2, 1, 3).reshape(b, h, nb, BLOCK, hd)
        q, k, v = (to_blocks(q), to_blocks(k), to_blocks(v))
        qp = jax.nn.elu(jnp.einsum('bhcsd,hdf->bhcsf', q, proj)) + 1.0
        kp = jax.nn.elu(jnp.einsum('bhcsd,hdf->bhcsf', k, proj)) + 1.0
        kv = jnp.einsum('bhcsf,bhcsd->bhcfd', kp, v)
        num = jnp.einsum('bhcsf,bhcfd->bhcsd', qp, kv)
        ksum = kp.sum(axis=3)
        z = 1.0 / (jnp.einsum('bhcsf,bhcf->bhcs', qp, ksum) + 1e-08)
        out = num * z[..., None]
        out = out.reshape(b, h, n, hd).transpose(0, 2, 1, 3).reshape(b, n, d)
        return out @ w_out.T + b_out

    def _L0_ffn_ref(x, gate_weight, W1, b1, W2, b2, Ws1, bs1, Ws2, bs2):
        import jax, jax.numpy as jnp
        import numpy as np
        B, SEQ, D, E, F = (4, 128, 128, 8, 512)
        CAPACITY = 2
        Bb, s, Dd = x.shape
        Ee = gate_weight.shape[0]
        xf = x.reshape(-1, Dd)
        S = xf.shape[0]
        logits = xf @ gate_weight.T
        scores = jax.nn.softmax(logits, axis=-1).T
        k = S * CAPACITY
        vals, idx = jax.lax.top_k(scores.reshape(-1), k)
        eidx = idx // S
        tidx = idx % S
        gate = jnp.zeros((Ee, S), x.dtype).at[eidx, tidx].add(vals)
        h = jax.nn.gelu(jnp.einsum('sd,edf->esf', xf, W1) + b1[:, None, :], approximate=True)
        y = jnp.einsum('esf,efd->esd', h, W2) + b2[:, None, :]
        out = jnp.einsum('es,esd->sd', gate, y)
        shared = jax.nn.gelu(xf @ Ws1 + bs1, approximate=True) @ Ws2 + bs2
        out = out + shared
        return out.reshape(Bb, s, Dd)

    def _L1_attn_ref(x, W_toP, W_U, W_F, W_V, W_lam, B_mat, C_mat, W_fromP):
        import jax, jax.numpy as jnp
        import numpy as np
        B, T, D, P, ALPHA, PR = (4, 512, 128, 64, 4, 64)
        pre = jnp.einsum('btd,dp->btp', x, W_toP)
        U = jnp.einsum('btd,dpa->btpa', x, W_U)
        Fg = jax.nn.sigmoid(jnp.einsum('btd,dp->btp', x, W_F))
        Y = U * W_V
        t = Y.sum(-1) + pre
        lam = jax.nn.sigmoid(jnp.einsum('btp,pr->btr', Fg, W_lam))
        u_in = jnp.einsum('btp,pr->btr', t, B_mat)

        def step(s, inp):
            l, u = inp
            s = l * s + u
            return (s, s)
        s0 = jnp.zeros((x.shape[0], PR), x.dtype)
        _, s_seq = jax.lax.scan(step, s0, (lam.transpose(1, 0, 2), u_in.transpose(1, 0, 2)))
        s_seq = s_seq.transpose(1, 0, 2)
        t_tilde = t + jnp.einsum('btr,rp->btp', s_seq, C_mat)
        h = jnp.einsum('btp,pd->btd', t_tilde, W_fromP)
        return h

    def _L1_ffn_ref(hidden_states, gate_weight, e_bias, w1, w2, w3, shared_gate, shared_up, shared_down):
        import jax, jax.numpy as jnp
        import numpy as np
        E, K, NG, TG = (64, 8, 8, 4)
        CAP = 128
        SCALE = 2.5

        def _route(x_flat, gate_weight, e_bias):
            T = x_flat.shape[0]
            logits = x_flat.astype(jnp.float32) @ gate_weight.astype(jnp.float32).T
            scores = jax.nn.sigmoid(logits)
            sfc = scores + e_bias[None, :]
            group_scores = jax.lax.top_k(sfc.reshape(T, NG, E // NG), 2)[0].sum(-1)
            _, gidx = jax.lax.top_k(group_scores, TG)
            gmask = jnp.zeros((T, NG), jnp.float32).at[jnp.arange(T)[:, None], gidx].set(1.0)
            smask = jnp.repeat(gmask, E // NG, axis=1)
            tmp = jnp.where(smask > 0, sfc, 0.0)
            _, topk_idx = jax.lax.top_k(tmp, K)
            topk_w = jnp.take_along_axis(scores, topk_idx, axis=1)
            topk_w = topk_w / (topk_w.sum(-1, keepdims=True) + 1e-20)
            return (topk_idx, topk_w * SCALE)

        def _moe_forward(hidden_states, gate_weight, e_bias, w1, w2, w3, shared_gate, shared_up, shared_down):
            B, S, H = hidden_states.shape
            T = B * S
            x = hidden_states.reshape(T, H)
            topk_idx, topk_w = _route(x, gate_weight, e_bias)
            Sk = T * K
            flat_e = topk_idx.reshape(-1)
            order = jnp.argsort(flat_e)
            sorted_e = flat_e[order]
            counts = jax.ops.segment_sum(jnp.ones((Sk,), jnp.int32), flat_e, num_segments=E)
            offsets = jnp.cumsum(counts) - counts
            pos = jnp.arange(Sk) - offsets[sorted_e]
            tok_sorted = x[order // K]
            xe = jnp.zeros((E, CAP, H), x.dtype).at[sorted_e, pos].set(tok_sorted, mode='drop')
            h = jax.nn.silu(jnp.einsum('ech,efh->ecf', xe, w1)) * jnp.einsum('ech,efh->ecf', xe, w3)
            ye = jnp.einsum('ecf,ehf->ech', h, w2)
            pos_c = jnp.minimum(pos, CAP - 1)
            vals = ye[sorted_e, pos_c]
            vals = jnp.where((pos < CAP)[:, None], vals, 0.0)
            flat_w = topk_w.reshape(-1)[order].astype(vals.dtype)
            flat_t = (jnp.arange(Sk) // K)[order]
            out = jax.ops.segment_sum(vals * flat_w[:, None], flat_t, num_segments=T)
            shared = jax.nn.silu(x @ shared_gate.T) * (x @ shared_up.T) @ shared_down.T
            return (out + shared).reshape(B, S, H)
        return _moe_forward(hidden_states, gate_weight, e_bias, w1, w2, w3, shared_gate, shared_up, shared_down)
    x = L0_attn_x
    mod = (_silu(L0_c) @ L0_wmod).reshape(L0_c.shape[0], 6, 1, -1)
    sa, ca, ga, sb, cb, gb = (mod[:, 0], mod[:, 1], mod[:, 2], mod[:, 3], mod[:, 4], mod[:, 5])
    ga = (2 * (ga >= 0) - 1) * jnp.maximum(jnp.abs(ga), 0.25)
    gb = (2 * (gb >= 0) - 1) * jnp.maximum(jnp.abs(gb), 0.25)
    h = _layernorm(x, axis=-1) * (1 + ca) + sa
    x = x + ga * _L0_attn_ref(h, L0_attn_w_qkv, L0_attn_w_out, L0_attn_b_out, L0_attn_proj)
    h = _layernorm(x, axis=-1) * (1 + cb) + sb
    x = x + gb * _L0_ffn_ref(h, L0_ffn_gate_weight, L0_ffn_W1, L0_ffn_b1, L0_ffn_W2, L0_ffn_b2, L0_ffn_Ws1, L0_ffn_bs1, L0_ffn_Ws2, L0_ffn_bs2)
    mod = (_silu(L1_c) @ L1_wmod).reshape(L1_c.shape[0], 6, 1, -1)
    sa, ca, ga, sb, cb, gb = (mod[:, 0], mod[:, 1], mod[:, 2], mod[:, 3], mod[:, 4], mod[:, 5])
    ga = (2 * (ga >= 0) - 1) * jnp.maximum(jnp.abs(ga), 0.25)
    gb = (2 * (gb >= 0) - 1) * jnp.maximum(jnp.abs(gb), 0.25)
    h = _layernorm(x, axis=-1) * (1 + ca) + sa
    x = x + ga * _L1_attn_ref(h, L1_attn_W_toP, L1_attn_W_U, L1_attn_W_F, L1_attn_W_V, L1_attn_W_lam, L1_attn_B_mat, L1_attn_C_mat, L1_attn_W_fromP)
    h = _layernorm(x, axis=-1) * (1 + cb) + sb
    x = x + gb * _L1_ffn_ref(h, L1_ffn_gate_weight, L1_ffn_e_bias, L1_ffn_w1, L1_ffn_w2, L1_ffn_w3, L1_ffn_shared_gate, L1_ffn_shared_up, L1_ffn_shared_down)
    return x

_drawn_inputs = setup_inputs


def setup_inputs(seed=0):
    import zlib

    import numpy as np

    out = dict(_drawn_inputs(seed))
    spreads = {'L0_attn_b_out': (0.0, 0.1),
     'L0_ffn_b1': (0.0, 0.8),
     'L0_ffn_b2': (0.0, 0.8),
     'L0_ffn_bs1': (0.0, 0.435),
     'L0_ffn_bs2': (0.0, 0.1),
     'L1_ffn_e_bias': (0.0, 0.8)}
    factors = {'L0_attn_proj': 8.0,
     'L1_ffn_gate_weight': 8.0,
     'L1_ffn_w1': 8.0,
     'L1_ffn_w2': 8.0,
     'L1_ffn_w3': 8.0,
     'L1_ffn_shared_gate': 8.0,
     'L1_ffn_shared_up': 8.0,
     'L1_ffn_shared_down': 8.0}
    for name, (base, spread) in spreads.items():
        noise = np.random.default_rng([zlib.crc32(name.encode()), seed]).standard_normal(out[name].shape)
        drawn = base * np.exp(spread * noise) if base else spread * noise
        out[name] = jnp.asarray(drawn.astype(out[name].dtype))
    for name, factor in factors.items():
        out[name] = (out[name] * factor).astype(out[name].dtype)
    return out
```

```python
from contextlib import ExitStack

import concourse.bass as bass
from concourse import mybir

F32 = mybir.dt.float32
BF16 = mybir.dt.bfloat16
I32 = mybir.dt.int32
ALU = mybir.AluOpType
ACT = mybir.ActivationFunctionType
AX = mybir.AxisListType.X
ds = bass.ds

P = 128
TILE = 128
CHUNK_TILES = 4
CHUNK = CHUNK_TILES * TILE
LN_EPS = 1e-5


class Chain:

    def __init__(self, engine, sem):
        self.engine, self.sem, self.past, self.k = engine, sem, 0, 0

    def body(self, i, n):
        self.base, self.n, self.k = self.past + i * n, n, 0

    def end(self, rounds):
        assert self.k == self.n, (self.k, self.n)
        self.past, self.k = self.past + rounds * self.n, 0

    def straight(self):
        self.base = self.past

    def __call__(self, ins):
        self.k += 1
        ins.then_inc(self.sem, 1)
        self.engine.wait_ge(self.sem, self.base + self.k)

    def close(self):
        self.past, self.k = self.past + self.k, 0


def build(nc, t, out):
    B, T1, D = t["L0_attn_x"].shape
    T = B * T1
    NT = T // TILE
    NC = T // CHUNK
    CPB = NC // B
    H, HD, FT = t["L0_attn_proj"].shape
    E0, _, FF = t["L0_ffn_W1"].shape
    FK = FF // P
    E1, F1, _ = t["L1_ffn_w1"].shape
    PR = t["L1_attn_W_lam"].shape[1]
    ALPHA = t["L1_attn_W_V"].shape[1]
    NPAIR = E1 // 2
    x_in = t["L0_attn_x"].rearrange("b (n p) d -> p (b n) d", p=P)
    out_v = out.rearrange("b (n p) d -> p (b n) d", p=P)

    with ExitStack() as ctx:
        def sb(name, shape, dt=F32):
            return ctx.enter_context(nc.sbuf_tensor(name, shape, dt))

        def sem(name):
            return ctx.enter_context(nc.semaphore(name))

        ps = ctx.enter_context(nc.psum_tensor("ps", [P, 8, 512], F32))

        def bank(k):
            return ps[:, k, :]

        ident = sb("ident", [P, P])
        ones = sb("ones", [P, P])
        ones_bf = sb("ones_bf", [P, P], BF16)
        before = sb("before", [P, P])
        before_bf = sb("before_bf", [P, P], BF16)
        x_sb = sb("x_sb", [P, NT, D])
        moments = sb("moments", [P, NT, 2])
        rstd = sb("rstd", [P, NT])
        scT = sb("scT", [P, 2 * B])
        shift = sb("shift", [P, 2, 4, NC])
        grow = sb("grow", [P, 2 * B, 2, D])
        schunk = sb("schunk", [P, NC, 2, D])
        gchunk = sb("gchunk", [P, 2, NC, D])
        wf = sb("wf", [P, 2, H, FT])
        wv = sb("wv", [P, D])
        wob = sb("wob", [P, NC, 2, D])
        bob = sb("bob", [1, NC, D])
        gw0 = sb("gw0", [P, E0])
        gw1 = sb("gw1", [P, E1])
        b1c = sb("b1c", [P, (E0 + 1) * FK])
        w_F = sb("w_F", [P, PR])
        w_u = sb("w_u", [P, PR])
        lam_bd = sb("lam_bd", [P, P])
        whx = sb("whx", [P, B, D])
        whs = sb("whs", [P, B, D])
        sgT = sb("sgT", [P, P])
        suT = sb("suT", [P, P])
        sdg = sb("sdg", [P, NC, D])
        dsel = sb("dsel", [P, P])
        blockmask = sb("blockmask", [P, P])
        stats6 = sb("stats6", [P, 4, 6])
        mom4 = sb("mom4", [P, 4, 2])

        ld_x = sem("ld_x")
        ld_mod = sem("ld_mod")
        ld_w = sem("ld_w")
        const_step = sem("const_step")
        dve_step = sem("dve_step")
        act_step = sem("act_step")
        pe_step = sem("pe_step")
        mod_c = sem("mod_c")
        c_turned = sem("c_turned")
        mod_b = sem("mod_b")
        mod_ps = sem("mod_ps")

        with ExitStack() as tmp:
            def st(name, shape, dt=F32):
                return tmp.enter_context(nc.sbuf_tensor(name, shape, dt))

            wmod = st("wmod", [P, 2, 6 * D])
            c_rows = st("c_rows", [2 * B, D])
            wqkv = st("wqkv", [P, 3, D])
            projblk = st("projblk", [P, H, FT])
            wo_n = st("wo_n", [P, D])
            wop = st("wop", [P, 2, 4, 32])
            bo_n = st("bo_n", [1, D])
            g0n = st("g0n", [E0, D])
            g1n = st("g1n", [E1, D])
            b1n = st("b1n", [(E0 + 1) * FK, P])
            toP = st("toP", [P, PR])
            wU = st("wU", [P, PR, ALPHA])
            wV = st("wV", [P, PR, ALPHA])
            wUV = st("wUV", [P, PR, ALPHA])
            wt = st("wt", [P, PR])
            wtT = st("wtT", [PR, P])
            Bm = st("Bm", [PR, PR])
            Cm = st("Cm", [PR, PR])
            CT = st("CT", [PR, 2, PR])
            fP = st("fP", [PR, D])
            sgn = st("sgn", [P, D])
            sun = st("sun", [P, D])
            sdn = st("sdn", [P, P])
            scb = st("scb", [P, 2 * B, P])
            modT = st("modT", [P, 2, 6, B])
            graw = st("graw", [P, 2 * B, 2, D])
            gsg = st("gsg", [P, 2 * B, 2, D])

            zeroed = sem("zeroed")
            wts_ps = sem("wts_ps")
            turned = sem("turned")
            fold_ps = sem("fold_ps")
            wt_done = sem("wt_done")
            N_LOADS = H + B + 17

            with nc.Block() as block:
                @block.sync
                def _(eng):
                    eng.dma_start(c_rows[0:B, :], t["L0_c"]).then_inc(ld_mod, 16)
                    eng.dma_start(c_rows[B:2 * B, :], t["L1_c"]).then_inc(ld_mod, 16)
                    eng.dma_start(wmod[:, 0, :], t["L0_wmod"]).then_inc(ld_mod, 16)
                    eng.dma_start(wmod[:, 1, :], t["L1_wmod"]).then_inc(ld_mod, 16)
                    for q in range(4):
                        n = NT // 4
                        eng.dma_start(x_sb[:, q * n:(q + 1) * n, :], x_in[:, q * n:(q + 1) * n, :]).then_inc(ld_x, 16)
                    eng.wait_ge(zeroed, 1)
                    for h in range(H):
                        eng.dma_start(projblk[h * HD:(h + 1) * HD, h, :], t["L0_attn_proj"][h]).then_inc(ld_w, 16)
                    for b in range(B):
                        eng.dma_start(lam_bd[b * PR:(b + 1) * PR, b * PR:(b + 1) * PR],
                                      t["L1_attn_W_lam"]).then_inc(ld_w, 16)
                    for dst, src in [
                        (wqkv[:, :, :], t["L0_attn_w_qkv"].rearrange("(g o) d -> o g d", o=P)),
                        (wo_n[:, :], t["L0_attn_w_out"]),
                        (bo_n[:, :], t["L0_attn_b_out"].rearrange("(a d) -> a d", a=1)),
                        (g0n[:, :], t["L0_ffn_gate_weight"]),
                        (g1n[:, :], t["L1_ffn_gate_weight"]),
                        (b1n[0:E0 * FK, :], t["L0_ffn_b1"].rearrange("e (k p) -> (e k) p", p=P)),
                        (b1n[E0 * FK:, :], t["L0_ffn_bs1"].rearrange("(k p) -> k p", p=P)),
                        (toP[:, :], t["L1_attn_W_toP"]),
                        (wU[:, :, :], t["L1_attn_W_U"]),
                        (wV[:, :, :], t["L1_attn_W_V"][None, :, :].to_broadcast([P, PR, ALPHA])),
                        (w_F[:, :], t["L1_attn_W_F"]),
                        (Bm[:, :], t["L1_attn_B_mat"]),
                        (Cm[:, :], t["L1_attn_C_mat"]),
                        (fP[:, :], t["L1_attn_W_fromP"]),
                        (sgn[:, :], t["L1_ffn_shared_gate"]),
                        (sun[:, :], t["L1_ffn_shared_up"]),
                        (sdn[:, :], t["L1_ffn_shared_down"]),
                    ]:
                        eng.dma_start(dst, src).then_inc(ld_w, 16)

                @block.gpsimd
                def _(eng):
                    step = Chain(eng, const_step)
                    step.straight()
                    eng.memset(projblk[:, :, :], 0.0)
                    step(eng.memset(lam_bd[:, :], 0.0))
                    eng.sem_inc(zeroed, 1)
                    eng.memset(ones[:, :], 1.0)
                    eng.memset(ones_bf[:, :], 1.0)
                    eng.memset(before[:, :], 1.0)
                    eng.memset(before_bf[:, :], 1.0)
                    eng.memset(dsel[:, :], 0.0)
                    eng.memset(blockmask[:, :], 0.0)
                    eng.memset(wop[:, :, :, :], 0.0)
                    eng.memset(whs[:, :, :], 0.0)
                    step(eng.memset(ident[:, :], 0.0))
                    step(eng.affine_select(out=before[:, :], in_=before[:, :], compare_op=ALU.is_gt, fill=0.0, base=0,
                                      pattern=[[1, P]], channel_multiplier=-1))
                    step(eng.affine_select(out=before_bf[:, :], in_=before_bf[:, :], compare_op=ALU.is_gt, fill=0.0, base=0,
                                      pattern=[[1, P]], channel_multiplier=-1))
                    for j in range(4):
                        step(eng.memset(blockmask[32 * j:32 * j + 32, 32 * j:32 * j + 32], 1.0))
                    step(eng.affine_select(out=dsel[:, :].rearrange("p (a b) -> p a b", a=4),
                                      in_=dsel[:, :].rearrange("p (a b) -> p a b", a=4),
                                      compare_op=ALU.not_equal, fill=1.0, base=-HD,
                                      pattern=[[-32, 4], [0, 32]], channel_multiplier=1))
                    step(eng.affine_select(out=ident[:, :], in_=ident[:, :], compare_op=ALU.not_equal, fill=1.0,
                                           base=0, pattern=[[-1, P]], channel_multiplier=1))
                    eng.sem_inc(zeroed, 1)

                @block.scalar
                def _(eng):
                    eng.wait_ge(c_turned, 1)
                    eng.activation(scT[:, :], ps[:, 5, 0:2 * B], ACT.Silu).then_inc(mod_c, 1)
                    step = Chain(eng, act_step)
                    step.straight()
                    eng.wait_ge(wts_ps, 1)
                    for qk in range(2):
                        for g in range(2):
                            eng.activation(wf[:, qk, 4 * g:4 * g + 4, :].rearrange("p a f -> p (a f)"),
                                           bank(2 * qk + g), ACT.Copy)
                    eng.wait_ge(wts_ps, 2)
                    eng.activation(wv[:, :], ps[:, 4, 0:128], ACT.Copy)
                    eng.activation(gw0[:, :], ps[:, 5, 128:128 + E0], ACT.Copy)
                    eng.activation(gw1[:, :], ps[:, 5, 0:E1], ACT.Copy)
                    eng.activation(b1c[:, :], ps[:, 5, 64:64 + (E0 + 1) * FK], ACT.Copy)
                    eng.activation(sgT[:, :], ps[:, 6, 0:128], ACT.Copy)
                    eng.activation(suT[:, :], ps[:, 6, 128:256], ACT.Copy)
                    eng.activation(wtT[:, :], ps[0:PR, 5, 256:384], ACT.Copy)
                    for b in range(2):
                        last = eng.activation(CT[:, b, :], ps[0:PR, 5, 384:384 + PR], ACT.Copy)
                    last.then_inc(turned, 1)
                    eng.wait_ge(fold_ps, 1)
                    eng.activation(w_u[:, :], ps[:, 7, 0:PR], ACT.Copy).then_inc(turned, 1)

                @block.tensor
                def _(eng):
                    eng.wait_ge(ld_mod, 64)
                    eng.wait_ge(zeroed, 2)
                    eng.transpose(ps[:, 5, 0:2 * B], c_rows[:, :], ident[0:2 * B, 0:2 * B]).then_inc(c_turned, 1)
                    eng.wait_ge(mod_b, 1)
                    for lb in range(2 * B):
                        eng.matmul(bank(lb), scb[:, lb, :], wmod[:, lb // B, 2 * D:6 * D], start=True, stop=True)
                    for l in range(2):
                        for j in range(6):
                            k = (l * 6 + j) * B
                            last = eng.matmul(ps[:, 4, k:k + B], wmod[:, l, j * D:(j + 1) * D],
                                              scT[:, l * B:(l + 1) * B], start=True, stop=True)
                    last.then_inc(mod_ps, 1)
                    eng.wait_ge(mod_b, 2)
                    eng.wait_ge(ld_w, 16 * N_LOADS)
                    eng.wait_ge(zeroed, 2)
                    for qk in range(2):
                        for g in range(2):
                            last = eng.matmul(bank(2 * qk + g), wqkv[:, qk, :],
                                              projblk[:, 4 * g:4 * g + 4, :].rearrange("p a f -> p (a f)"),
                                              start=True, stop=True)
                    last.then_inc(wts_ps, 1)
                    eng.transpose(ps[:, 4, 0:128], wqkv[:, 2, :], ident[:, :])
                    eng.wait_ge(wt_done, 1)
                    for g in range(2):
                        eng.transpose(ps[:, 4, 128 + 128 * g:256 + 128 * g],
                                      wop[:, g, :, :].rearrange("p a c -> p (a c)"), ident[:, :])
                    eng.transpose(ps[:, 5, 128:128 + E0], g0n[:, :], ident[0:E0, 0:E0])
                    eng.transpose(ps[:, 5, 0:E1], g1n[:, :], ident[0:E1, 0:E1])
                    nb = (E0 + 1) * FK
                    eng.transpose(ps[:, 5, 64:64 + nb], b1n[:, :], ident[0:nb, 0:nb])
                    eng.transpose(ps[0:PR, 5, 256:384], wt[:, :], ident[:, :])
                    eng.transpose(ps[0:PR, 5, 384:384 + PR], Cm[:, :], ident[0:PR, 0:PR])
                    eng.transpose(ps[:, 6, 0:128], sgn[:, :], ident[:, :])
                    eng.transpose(ps[:, 6, 128:256], sun[:, :], ident[:, :])
                    eng.transpose(ps[:, 6, 256:384], sdn[:, :], ident[:, :]).then_inc(wts_ps, 1)
                    eng.wait_ge(turned, 1)
                    eng.matmul(ps[:, 7, 0:PR], wtT[:, :], Bm[:, :], start=True, stop=True)
                    eng.matmul(ps[:, 7, 128:256], wtT[:, :], fP[:, :], start=True, stop=True)
                    eng.matmul(ps[:, 7, 256:384], CT[:, :, :].rearrange("p b r -> p (b r)"), fP[:, :],
                               start=True, stop=True).then_inc(fold_ps, 1)

                @block.vector
                def _(eng):
                    step = Chain(eng, dve_step)
                    step.straight()
                    eng.wait_ge(mod_c, 1)
                    eng.tensor_copy(scb[:, :, :], scT[:, :, None].to_broadcast([P, 2 * B, P])).then_inc(mod_b, 1)
                    eng.wait_ge(mod_ps, 1)
                    eng.tensor_copy(modT[:, :, :, :].rearrange("p l j b -> p (l j b)"), ps[:, 4, 0:12 * B])
                    for lb in range(2 * B):
                        r = bank(lb).rearrange("p (j d) -> p j d", j=4)
                        eng.tensor_copy(graw[:, lb, :, :], r[:, 0::3, :])
                        if lb >= B:
                            cs = slice((lb - B) * CPB, (lb - B + 1) * CPB)
                            eng.tensor_copy(schunk[:, cs, 0, :], r[:, 1:2, :].to_broadcast([P, CPB, D]))
                            eng.tensor_scalar(schunk[:, cs, 1, :], r[:, 2:3, :].to_broadcast([P, CPB, D]), 1.0, None,
                                              ALU.add)
                    step(eng.tensor_copy(moments[:, 0:1, 0], ps[:, 4, 0:1]))
                    eng.sem_inc(mod_b, 1)
                    for l in range(2):
                        for k, (j, add) in enumerate([(1, 1.0), (0, 0.0), (4, 1.0), (3, 0.0)]):
                            eng.tensor_scalar(shift[:, l, k, :].rearrange("p (b c) -> p b c", b=B),
                                              modT[:, l, j, :, None].to_broadcast([P, B, CPB]), add, None, ALU.add)
                    flat = graw[:, :, :, :].rearrange("p a b d -> p (a b d)")
                    gs = gsg[:, :, :, :].rearrange("p a b d -> p (a b d)")
                    gr = grow[:, :, :, :].rearrange("p a b d -> p (a b d)")
                    eng.tensor_scalar(gs, flat, 0.0, 2.0, ALU.is_ge, ALU.mult)
                    step(eng.scalar_tensor_tensor(gr, flat, -1.0, flat, ALU.mult, ALU.max))
                    step(eng.tensor_scalar(gr, gr, 0.25, None, ALU.max))
                    step(eng.scalar_tensor_tensor(gr, gs, -1.0, gr, ALU.add, ALU.mult))
                    for l in range(2):
                        for b in range(B):
                            eng.tensor_copy(gchunk[:, l, b * CPB:(b + 1) * CPB, :],
                                            grow[:, l * B + b, 1:2, :].to_broadcast([P, CPB, D]))
                    eng.wait_ge(ld_w, 16 * N_LOADS)
                    eng.wait_ge(zeroed, 2)
                    eng.tensor_copy(wop[:, :, :, 0:HD], wo_n[:, :].rearrange("p (g a c) -> p g a c", g=2, a=4))
                    step(eng.tensor_tensor(wUV[:, :, :], wU[:, :, :], wV[:, :, :], ALU.mult))
                    step(eng.tensor_reduce(wt[:, :], wUV[:, :, :], AX, ALU.add))
                    step(eng.tensor_tensor(wt[:, :], wt[:, :], toP[:, :], ALU.add))
                    eng.sem_inc(wt_done, 1)
                    eng.wait_ge(turned, 1)
                    for b in range(B):
                        cs = slice(b * CPB, (b + 1) * CPB)
                        for c in range(b * CPB, (b + 1) * CPB):
                            eng.tensor_tensor(wob[:, c, :, :], ps[:, 4, 128:384].rearrange("p (g d) -> p g d", g=2),
                                              grow[:, b, 0:1, :].to_broadcast([P, 2, D]), ALU.mult)
                        eng.tensor_tensor(bob[:, cs, :], bo_n[:, None, :].to_broadcast([1, CPB, D]),
                                          grow[0:1, b, 0:1, :].to_broadcast([1, CPB, D]), ALU.mult)
                        eng.tensor_tensor(sdg[:, cs, :], ps[:, 6, None, 256:384].to_broadcast([P, CPB, D]),
                                          grow[:, B + b, 1:2, :].to_broadcast([P, CPB, D]), ALU.mult)
                    eng.wait_ge(turned, 2)
                    for b in range(B):
                        rows = slice(b * PR, (b + 1) * PR)
                        eng.tensor_tensor(whx[:, b, :], ps[:, 7, 128:256], grow[:, B + b, 0, :], ALU.mult)
                        eng.tensor_tensor(whs[rows, b, :], ps[rows, 7, 256:384], grow[rows, B + b, 0, :], ALU.mult)

        def token_moments(eng, step, c):
            eng.nop(nofuse=True)
            for k in range(4):
                last = eng.bn_stats(stats6[:, k, :], x_sb[:, ds(c * 4 + k, 1), :])
            step(last)
            eng.nop(nofuse=True)
            for k in range(4):
                last = eng.bn_aggr(mom4[:, k, :], stats6[:, k, :])
            step(last)
            eng.nop(nofuse=True)
            step(eng.tensor_copy(moments[:, ds(c * 4, 4), :], mom4[:, :, :]))

        def normalized(eng, dst, c):
            for k in range(4):
                last = eng.tensor_scalar(dst[:, k, :], x_sb[:, ds(c * 4 + k, 1), :], moments[:, ds(c * 4 + k, 1), 0:1],
                                         rstd[:, ds(c * 4 + k, 1)], ALU.subtract, ALU.mult)
            return last

        def rstd_block(name):
            var_ready = sem(f"{name}_var_ready")
            std_ready = sem(f"{name}_std_ready")
            with nc.Block() as block:
                @block.vector
                def _(eng):
                    eng.tensor_scalar(rstd[:, :], moments[:, :, 1], LN_EPS, None, ALU.add).then_inc(var_ready, 1)
                    eng.wait_ge(std_ready, 1)
                    eng.reciprocal(rstd[:, :], rstd[:, :])

                @block.scalar
                def _(eng):
                    eng.wait_ge(var_ready, 1)
                    eng.activation(rstd[:, :], rstd[:, :], ACT.Sqrt).then_inc(std_ready, 1)

        mom_step = sem("mom_step")
        with nc.Block() as block:
            @block.vector
            def _(eng):
                step = Chain(eng, mom_step)
                eng.wait_ge(ld_x, 64)
                with eng.Fori(0, NC) as c:
                    step.body(c, 3)
                    token_moments(eng, step, c)
                step.end(NC)
        rstd_block("ln0")

        with ExitStack() as tmp:
            def st(name, shape, dt=F32):
                return tmp.enter_context(nc.sbuf_tensor(name, shape, dt))

            xn = st("xn", [P, 2, 4, D])
            hT = st("hT", [P, 2, CHUNK])
            vp = st("vp", [P, 2, 4, H, 32])
            ex = st("ex", [P, 2, 2, CHUNK])
            qk = st("qk", [P, 2, 2, CHUNK])
            am = st("am", [P, 2, CHUNK])
            osb = st("osb", [P, 2, CHUNK])
            den = st("den", [P, CHUNK])
            on = st("on", [P, 2, CHUNK])

            xn_ready = sem("xn_ready")
            xnT_ready = sem("xnT_ready")
            hT_ready = sem("hT_ready")
            v_ps = sem("v_ps")
            v_ready = sem("v_ready")
            x_ready = sem("x_ready")
            e_ready = sem("e_ready")
            r_ready = sem("r_ready")
            feat_ready = sem("feat_ready")
            a_ready = sem("a_ready")
            am_ready = sem("am_ready")
            o_ready = sem("o_ready")
            osb_ready = sem("osb_ready")
            den_ps = sem("den_ps")
            den_sb = sem("den_sb")
            den_inv = sem("den_inv")
            on_ready = sem("on_ready")
            out_ps = sem("out_ps")
            x_added = sem("x_added")
            v_set = sem("v_set")
            amom_step = sem("amom_step")

            def chunks(eng, body):
                body(0, 0, False, True)
                with eng.Fori(0, (NC - 2) // 2) as j:
                    body(j * 2 + 1, 1, True, True)
                    body(j * 2 + 2, 0, True, True)
                body(NC - 1, 1, True, False)

            with nc.Block() as block:
                @block.gpsimd
                def _(eng):
                    eng.memset(vp[:, :, :, :, HD + 1:32], 0.0)
                    eng.memset(vp[:, :, :, :, HD:HD + 1], 1.0).then_inc(v_set, 1)

                    def normalize(i, g):
                        n = i * 2 + g
                        eng.wait_ge(den_inv, n + 1)
                        eng.wait_ge(osb_ready, n + 1)
                        eng.wait_ge(out_ps, i)
                        eng.tensor_tensor(on[:, g, :], osb[:, g, :], den[:, :], ALU.mult).then_inc(on_ready, 1)

                    def body(i, u, prev, nxt):
                        for h in range(H):
                            if prev and h == 1:
                                normalize(i - 1, 0)
                            if prev and h == 4:
                                normalize(i - 1, 1)

                    chunks(eng, body)
                    normalize(NC - 1, 0)
                    normalize(NC - 1, 1)

                @block.scalar
                def _(eng):
                    def turn(i, u):
                        eng.wait_ge(xnT_ready, i + 1)
                        eng.activation(hT[:, u, :], bank(0), ACT.Identity, bias=shift[:, 0, 1, ds(i, 1)],
                                       scale=shift[:, 0, 0, ds(i, 1)]).then_inc(hT_ready, 1)

                    def keep_v(i, u):
                        eng.wait_ge(v_ps, i + 1)
                        eng.activation(vp[:, u, :, :, 0:HD].rearrange("p t h c -> p (t h) c"),
                                       bank(0).rearrange("p (a c) -> p a c", c=HD), ACT.Copy).then_inc(v_ready, 1)

                    def keep_o(i, g):
                        eng.wait_ge(o_ready, i * 2 + g + 1)
                        eng.wait_ge(on_ready, i * 2)
                        eng.activation(osb[:, g, :], bank(1), ACT.Copy).then_inc(osb_ready, 1)

                    def denominator(i, g):
                        eng.wait_ge(den_ps, i * 2 + g + 1)
                        eng.wait_ge(on_ready, i * 2 + g)
                        eng.activation(den[:, :], bank(0), ACT.Copy, bias=1e-8).then_inc(den_sb, 1)

                    def body(i, u, prev, nxt):
                        for h in range(H):
                            q = i * H + h
                            eng.wait_ge(x_ready, q + 1)
                            eng.wait_ge(feat_ready, q)
                            both = ex[:, h % 2, :, :].rearrange("p a n -> p (a n)")
                            eng.activation(both, ps[:, 2 + 2 * (h % 2):4 + 2 * (h % 2), :].rearrange("p a n -> p (a n)"),
                                           ACT.Relu, scale=-1.0).then_inc(r_ready, 1)
                            eng.wait_ge(r_ready, q + 1)
                            eng.activation(both, both, ACT.Exp, scale=-1.0).then_inc(e_ready, 1)
                            if prev and h == 0:
                                denominator(i - 1, 0)
                            if prev and h == 2:
                                keep_o(i - 1, 1)
                            if prev and h == 3:
                                denominator(i - 1, 1)
                            if h == 5:
                                keep_o(i, 0)
                            if nxt and h == 6:
                                turn(i + 1, 1 - u)
                            if nxt and h == 7:
                                keep_v(i + 1, 1 - u)

                    eng.wait_ge(v_set, 1)
                    turn(0, 0)
                    keep_v(0, 0)
                    chunks(eng, body)
                    denominator(NC - 1, 0)
                    keep_o(NC - 1, 1)
                    denominator(NC - 1, 1)

                @block.vector
                def _(eng):
                    step = Chain(eng, amom_step)
                    eng.sem_inc(feat_ready, 1)

                    def normalize(i, u):
                        eng.wait_ge(xnT_ready, i)
                        normalized(eng, xn[:, u, :, :], i).then_inc(xn_ready, 1)

                    def inside_blocks(q, par):
                        eng.wait_ge(a_ready, q + 2)
                        eng.tensor_tensor(am[:, par, :].rearrange("p (t m) -> p t m", t=4),
                                          bank(6).rearrange("p (t m) -> p t m", t=4),
                                          blockmask[:, None, :].to_broadcast([P, 4, P]), ALU.mult).then_inc(am_ready, 1)

                    def invert(i, g):
                        eng.wait_ge(den_sb, i * 2 + g + 1)
                        eng.reciprocal(den[:, :], den[:, :]).then_inc(den_inv, 1)

                    def add(i):
                        eng.wait_ge(out_ps, i + 1)
                        xs = x_sb[:, ds(i * 4, 4), :]
                        eng.tensor_tensor(xs, xs, bank(0).rearrange("p (t d) -> p t d", t=4), ALU.add).then_inc(x_added, 1)
                        eng.wait_ge(x_added, i + 1)
                        step.body(i, 3)
                        token_moments(eng, step, i)

                    def body(i, u, prev, nxt):
                        for h in range(H):
                            q = i * H + h
                            eng.wait_ge(e_ready, q + 1)
                            eng.wait_ge(a_ready, q)
                            eng.scalar_tensor_tensor(
                                qk[:, h % 2, :, :].rearrange("p a n -> p (a n)"),
                                ps[:, 2 + 2 * (h % 2):4 + 2 * (h % 2), :].rearrange("p a n -> p (a n)"), 0.0,
                                ex[:, h % 2, :, :].rearrange("p a n -> p (a n)"),
                                ALU.max, ALU.add).then_inc(feat_ready, 1)
                            if h or prev:
                                inside_blocks(q - 1, (h - 1) % 2)
                            if prev and h == 1:
                                invert(i - 1, 0)
                            if prev and h == 4:
                                invert(i - 1, 1)
                            if nxt and h == 4:
                                normalize(i + 1, 1 - u)
                            if prev and h == 6:
                                add(i - 1)

                    normalize(0, 0)
                    chunks(eng, body)
                    inside_blocks(NC * H - 1, 1)
                    invert(NC - 1, 0)
                    invert(NC - 1, 1)
                    add(NC - 1)
                    step.end(NC)

                @block.tensor
                def _(eng):
                    eng.sem_inc(a_ready, 1)

                    def turn(i, u):
                        eng.wait_ge(xn_ready, i + 1)
                        for k in range(4):
                            last = eng.transpose(bank(0)[:, k * P:(k + 1) * P], xn[:, u, k, :], ident[:, :])
                        last.then_inc(xnT_ready, 1)

                    def values(i, u):
                        eng.wait_ge(hT_ready, i + 1)
                        for k in range(4):
                            last = eng.matmul(bank(0)[:, k * P:(k + 1) * P], hT[:, u, k * P:(k + 1) * P], wv[:, :],
                                              start=True, stop=True)
                        last.then_inc(v_ps, 1)

                    def features(i, u, h):
                        q = i * H + h
                        eng.wait_ge(feat_ready, q)
                        eng.matmul(bank(2 + 2 * (h % 2)), wf[:, 0, h, :], hT[:, u, :], start=True, stop=True)
                        eng.matmul(bank(3 + 2 * (h % 2)), wf[:, 1, h, :], hT[:, u, :], start=True,
                                   stop=True).then_inc(x_ready, 1)

                    def products(q, h):
                        eng.wait_ge(feat_ready, q + 2)
                        eng.wait_ge(am_ready, q)
                        for k in range(4):
                            c = slice(k * P, (k + 1) * P)
                            last = eng.matmul(bank(6)[:, c], qk[:, h % 2, 1, c], qk[:, h % 2, 0, c], start=True, stop=True)
                        last.then_inc(a_ready, 1)

                    def outputs(q, i, u, h):
                        eng.wait_ge(am_ready, q + 1)
                        if h % 4 == 0:
                            eng.wait_ge(osb_ready, i * 2 + h // 4)
                            eng.wait_ge(v_ready, i + 1)
                        a = h % 4
                        for k in range(4):
                            last = eng.matmul(ps[32 * a:32 * a + 32, 1, k * P:(k + 1) * P], vp[:, u, k, h, :],
                                              am[:, h % 2, k * P:(k + 1) * P], start=True, stop=True)
                        if a == 3:
                            last.then_inc(o_ready, 1)

                    def denominator(i, g):
                        eng.wait_ge(osb_ready, i * 2 + g + 1)
                        eng.matmul(bank(0), dsel[:, :], osb[:, g, :], start=True, stop=True).then_inc(den_ps, 1)

                    def project(i):
                        eng.wait_ge(on_ready, i * 2 + 2)
                        for k in range(4):
                            c = slice(k * P, (k + 1) * P)
                            for g in range(2):
                                eng.matmul(bank(0)[:, c], on[:, g, c], wob[:, ds(i, 1), g, :].rearrange("p a d -> p (a d)"),
                                           start=(g == 0), stop=False)
                            last = eng.matmul(bank(0)[:, c], ones[0:1, :], bob[:, ds(i, 1), :].rearrange("p a d -> p (a d)"),
                                              start=False, stop=True)
                        last.then_inc(out_ps, 1)

                    def body(i, u, prev, nxt):
                        for h in range(H):
                            q = i * H + h
                            features(i, u, h)
                            if h >= 1 or prev:
                                products(q - 1, (h - 1) % H)
                            if h >= 2:
                                outputs(q - 2, i, u, h - 2)
                            elif prev:
                                outputs(q - 2, i - 1, 1 - u, h + H - 2)
                            if prev and h == 0:
                                eng.wait_ge(v_ready, i + 1)
                                denominator(i - 1, 0)
                            if prev and h == 3:
                                eng.wait_ge(den_sb, i * 2 - 1)
                                denominator(i - 1, 1)
                            if prev and h == 5:
                                eng.wait_ge(den_sb, i * 2)
                                project(i - 1)
                            if nxt and h == 6:
                                if prev:
                                    eng.wait_ge(x_added, i)
                                turn(i + 1, 1 - u)
                            if nxt and h == 7:
                                values(i + 1, 1 - u)

                    turn(0, 0)
                    values(0, 0)
                    chunks(eng, body)
                    last_q = NC * H - 1
                    products(last_q, H - 1)
                    outputs(last_q - 1, NC - 1, 1, H - 2)
                    eng.wait_ge(x_added, NC - 1)
                    denominator(NC - 1, 0)
                    outputs(last_q, NC - 1, 1, H - 1)
                    eng.wait_ge(den_sb, NC * 2 - 1)
                    denominator(NC - 1, 1)
                    eng.wait_ge(den_sb, NC * 2)
                    project(NC - 1)
        rstd_block("ln1")

        with ExitStack() as tmp:
            def st(name, shape, dt=F32):
                return tmp.enter_context(nc.sbuf_tensor(name, shape, dt))

            CAP0 = 2 * T
            NE = E0 + 1
            h2T = st("h2T", [P, T])
            w1s = st("w1s", [P, NE, FF])
            w2s = st("w2s", [P, NE, FK, D])
            b2m = st("b2m", [P, NT // 2, D])
            bs2 = st("bs2", [P, D])
            gateT = st("gateT", [P, E0, NT])
            gflat = st("gflat", [P, 2 * P])
            ld_f = sem("ld_f")
            N_LDF = 5 + E0
            with ExitStack() as tmp2:
                def st2(name, shape, dt=F32):
                    return tmp2.enter_context(nc.sbuf_tensor(name, shape, dt))

                xn = st2("xn2", [P, 2, 4, D])
                h2c = st2("h2c", [P, 2, CHUNK])
                scores = st2("scores", [P, NT, E0])
                smax = st2("smax", [P, NT])
                ssum = st2("ssum", [P, NT])
                sperm = st2("sperm", [P, 2, E0, NT // 2])
                sflat = st2("sflat", [P, 2 * P])
                above = st2("above", [P, 2 * P])
                equal = st2("equal", [P, 2 * P])
                rank = st2("rank", [P, 2 * P])
                b2r = st2("b2r", [P, D])
                cm3 = st2("cm3", [P, E0, NT // 2])
                cmask = st2("cmask", [P, NT // 2])
                cur = st2("cur", [P, 1], I32)
                cand = st2("cand", [P, 1], I32)
                bit = st2("bit", [P, 1], I32)
                bitf = st2("bitf", [P, 1])
                inc = st2("inc", [P, 1], I32)
                cnt = st2("cnt", [P, 1])
                n_above = st2("n_above", [P, 1])
                n_equal = st2("n_equal", [P, 1])
                need = st2("need", [P, 1])

                bxn_ready = sem("bxn_ready")
                bxnT_ready = sem("bxnT_ready")
                bh_ready = sem("bh_ready")
                bh_kept = sem("bh_kept")
                lg_ps = sem("lg_ps")
                lg_sb = sem("lg_sb")
                cm_step = sem("cm_step")
                cm_ready = sem("cm_ready")
                with nc.Block() as block:
                    @block.sync
                    def _(eng):
                        eng.dma_start(w1s[:, 0:E0, :], t["L0_ffn_W1"].rearrange("e d f -> d e f")).then_inc(ld_f, 16)
                        eng.dma_start(w1s[:, E0, :], t["L0_ffn_Ws1"]).then_inc(ld_f, 16)
                        eng.dma_start(w2s[:, 0:E0, :, :],
                                      t["L0_ffn_W2"].rearrange("e (k p) d -> p e k d", p=P)).then_inc(ld_f, 16)
                        eng.dma_start(w2s[:, E0, :, :],
                                      t["L0_ffn_Ws2"].rearrange("(k p) d -> p k d", p=P)).then_inc(ld_f, 16)
                        eng.dma_start(bs2[:, :], t["L0_ffn_bs2"][None, :].to_broadcast([P, D])).then_inc(ld_f, 16)
                        n = P // E0
                        for e in range(E0):
                            eng.dma_start(b2r[e * n:(e + 1) * n, :],
                                          t["L0_ffn_b2"][e:e + 1, :].to_broadcast([n, D])).then_inc(ld_f, 16)

                    @block.gpsimd
                    def _(eng):
                        step = Chain(eng, cm_step)
                        step.straight()
                        step(eng.memset(cm3[:, :, :], 0.0))
                        eng.affine_select(out=cm3[:, :, :], in_=cm3[:, :, :], compare_op=ALU.not_equal, fill=1.0, base=0,
                                          pattern=[[-NT // 2, E0], [-1, NT // 2]], channel_multiplier=1).then_inc(cm_ready, 1)
                        with eng.Fori(0, NC // 2) as j:
                            for u in range(2):
                                i = j * 2 + u
                                eng.wait_ge(bh_ready, i + 1)
                                eng.tensor_copy(h2T[:, ds(i * CHUNK, CHUNK)], h2c[:, u, :]).then_inc(bh_kept, 1)

                    @block.vector
                    def _(eng):
                        with eng.Fori(0, NC // 2) as j:
                            for u in range(2):
                                i = j * 2 + u
                                eng.wait_ge(bxnT_ready, i + 1)
                                normalized(eng, xn[:, u, :, :], i).then_inc(bxn_ready, 1)

                    @block.tensor
                    def _(eng):
                        eng.sem_inc(bxnT_ready, 2)
                        with eng.Fori(0, NC // 2) as j:
                            for u in range(2):
                                i = j * 2 + u
                                eng.wait_ge(bxn_ready, i + 1)
                                for k in range(4):
                                    last = eng.transpose(bank(u)[:, k * P:(k + 1) * P], xn[:, u, k, :], ident[:, :])
                                last.then_inc(bxnT_ready, 1)
                                eng.wait_ge(bh_ready, i + 1)
                                eng.wait_ge(lg_sb, i)
                                for k in range(4):
                                    last = eng.matmul(ps[:, 2 + u, k * E0:(k + 1) * E0], h2c[:, u, k * P:(k + 1) * P],
                                                      gw0[:, :], start=True, stop=True)
                                last.then_inc(lg_ps, 1)

                    @block.scalar
                    def _(eng):
                        with eng.Fori(0, NC // 2) as j:
                            for u in range(2):
                                i = j * 2 + u
                                eng.wait_ge(bxnT_ready, i + 3)
                                eng.wait_ge(lg_ps, i)
                                eng.wait_ge(bh_kept, i)
                                eng.activation(h2c[:, u, :], bank(u), ACT.Identity, bias=shift[:, 0, 3, ds(i, 1)],
                                               scale=shift[:, 0, 2, ds(i, 1)]).then_inc(bh_ready, 1)
                                eng.wait_ge(lg_ps, i + 1)
                                eng.activation(scores[:, ds(i * 4, 4), :],
                                               ps[:, 2 + u, 0:4 * E0].rearrange("p (k e) -> p k e", k=4),
                                               ACT.Copy).then_inc(lg_sb, 1)

                top_step = sem("top_step")
                ex_ready = sem("ex_ready")
                shifted = sem("shifted")
                perm_ready = sem("perm_ready")
                flat_ps = sem("flat_ps")
                cnt_ready = sem("cnt_ready")
                cnt_ps = sem("cnt_ps")
                gate_ready = sem("gate_ready")
                gate_ps = sem("gate_ps")
                BITS = 30
                with nc.Block() as block:
                    @block.scalar
                    def _(eng):
                        eng.wait_ge(shifted, 1)
                        eng.activation(scores[:, :, :], scores[:, :, :], ACT.Exp).then_inc(ex_ready, 1)

                    @block.vector
                    def _(eng):
                        step = Chain(eng, top_step)
                        step.straight()
                        step(eng.tensor_reduce(smax[:, :], scores[:, :, :], AX, ALU.max))
                        eng.tensor_tensor(scores[:, :, :], scores[:, :, :],
                                          smax[:, :, None].to_broadcast([P, NT, E0]), ALU.subtract).then_inc(shifted, 1)
                        eng.wait_ge(ex_ready, 1)
                        step(eng.tensor_reduce(ssum[:, :], scores[:, :, :], AX, ALU.add))
                        step(eng.reciprocal(ssum[:, :], ssum[:, :]))
                        for j in range(2):
                            last = eng.tensor_tensor(
                                sperm[:, j, :, :].rearrange("p e c -> p c e"),
                                scores[:, :, :].rearrange("p (c j) e -> p j c e", j=2)[:, j, :, :],
                                ssum[:, :].rearrange("p (c j) -> p j c", j=2)[:, j, :, None].to_broadcast([P, NT // 2, E0]),
                                ALU.mult)
                        last.then_inc(perm_ready, 1)
                        eng.memset(cur[:, :], 0)
                        eng.memset(bit[:, :], 1 << (BITS - 1))
                        eng.memset(cand[:, :], 1 << (BITS - 1))
                        step(eng.memset(bitf[:, :], float(1 << (BITS - 1))))
                        eng.wait_ge(flat_ps, 1)
                        step(eng.tensor_copy(sflat[:, :], ps[:, 0, 0:2 * P]))
                        step.close()
                        with eng.Fori(0, BITS) as k:
                            step.body(k, 5)
                            eng.tensor_scalar(above[:, :], sflat[:, :], cand[:, :].bitcast(F32), 0.0, ALU.is_ge, ALU.add,
                                              accum_out=cnt[:, :]).then_inc(cnt_ready, 1)
                            step(eng.tensor_scalar(bit[:, :], bit[:, :], 1, None, ALU.logical_shift_right))
                            eng.wait_ge(cnt_ps, k + 1)
                            step(eng.tensor_scalar(inc[:, :], ps[:, 1, 0:1], float(CAP0), bitf[:, :], ALU.is_ge, ALU.mult))
                            step(eng.tensor_tensor(cur[:, :], cur[:, :], inc[:, :], ALU.bitwise_or))
                            step(eng.tensor_tensor(cand[:, :], cur[:, :], bit[:, :], ALU.bitwise_or))
                            step(eng.tensor_scalar(bitf[:, :], bitf[:, :], 0.5, None, ALU.mult))
                        step.end(BITS)
                        step.straight()
                        thr = cur[:, :].bitcast(F32)
                        eng.tensor_scalar(above[:, :], sflat[:, :], thr, 0.0, ALU.is_gt, ALU.add, accum_out=n_above[:, :])
                        step(eng.tensor_scalar(equal[:, :], sflat[:, :], thr, 0.0, ALU.is_equal, ALU.add,
                                               accum_out=n_equal[:, :]))
                        eng.sem_inc(cnt_ready, 1)
                        step(eng.tensor_tensor_scan(rank[:, :], ones[:, 0:1].to_broadcast([P, 2 * P]), equal[:, :], 0.0,
                                                    ALU.mult, ALU.add))
                        eng.wait_ge(cnt_ps, BITS + 1)
                        step(eng.tensor_scalar(need[:, :], ps[:, 1, 0:1], -1.0, float(CAP0), ALU.mult, ALU.add))
                        step(eng.tensor_tensor(need[:, :], need[:, :], ps[:, 1, 1:2], ALU.subtract))
                        step(eng.scalar_tensor_tensor(rank[:, :], rank[:, :], need[:, :], equal[:, :], ALU.is_le, ALU.mult))
                        step(eng.tensor_tensor(above[:, :], above[:, :], rank[:, :], ALU.add))
                        eng.tensor_tensor(gflat[:, :], above[:, :], sflat[:, :], ALU.mult).then_inc(gate_ready, 1)
                        eng.wait_ge(cm_ready, 1)
                        eng.wait_ge(ld_f, 16 * N_LDF)
                        step(eng.tensor_reduce(cmask[:, :], cm3[:, :, :].rearrange("p e c -> p c e"), AX, ALU.add))
                        step(eng.tensor_tensor(b2m[:, :, :], b2r[:, None, :].to_broadcast([P, NT // 2, D]),
                                               cmask[:, :, None].to_broadcast([P, NT // 2, D]), ALU.mult))
                        eng.wait_ge(gate_ps, 1)
                        for j in range(2):
                            eng.tensor_copy(gateT[:, :, :].rearrange("p e (c j) -> p e c j", j=2)[:, :, :, j],
                                            ps[:, 0, j * P:(j + 1) * P].rearrange("p (e c) -> p e c", e=E0))

                    @block.tensor
                    def _(eng):
                        eng.wait_ge(perm_ready, 1)
                        for j in range(2):
                            last = eng.transpose(ps[:, 0, j * P:(j + 1) * P],
                                                 sperm[:, j, :, :].rearrange("p e c -> p (e c)"), ident[:, :])
                        last.then_inc(flat_ps, 1)
                        with eng.Fori(0, BITS) as k:
                            eng.wait_ge(cnt_ready, k + 1)
                            eng.matmul(ps[:, 1, 0:1], ones[:, :], cnt[:, :], start=True, stop=True).then_inc(cnt_ps, 1)
                        eng.wait_ge(cnt_ready, BITS + 1)
                        eng.matmul(ps[:, 1, 0:1], ones[:, :], n_above[:, :], start=True, stop=True)
                        eng.matmul(ps[:, 1, 1:2], before[:, :], n_equal[:, :], start=True, stop=True).then_inc(cnt_ps, 1)
                        eng.wait_ge(gate_ready, 1)
                        for j in range(2):
                            last = eng.transpose(ps[:, 0, j * P:(j + 1) * P], gflat[:, j * P:(j + 1) * P], ident[:, :])
                        last.then_inc(gate_ps, 1)

            hid = st("hid", [P, 2, FK, CHUNK])
            facc = st("facc", [P, 4, D])
            s1_ps = sem("s1_ps")
            hid_ready = sem("hid_ready")
            s2_ps = sem("s2_ps")
            y_used = sem("y_used")
            bias_ps = sem("bias_ps")
            f_step = sem("f_step")
            bx_added = sem("bx_added")
            order = [E0] + list(range(E0))
            with nc.Block() as block:
                @block.tensor
                def _(eng):
                    def up(i, u, n):
                        q = i * NE + n
                        for k in range(FK):
                            eng.wait_ge(hid_ready, q * FK + k)
                            eng.matmul(bank(k), w1s[:, order[n], k * P:(k + 1) * P], h2T[:, ds(i * CHUNK, CHUNK)],
                                       start=True, stop=True).then_inc(s1_ps, 1)

                    def down(i, par, n):
                        q = i * NE + n
                        eng.wait_ge(hid_ready, (q + 1) * FK + FK - 1)
                        eng.wait_ge(y_used, q)
                        for c in range(4):
                            for k in range(FK):
                                last = eng.matmul(bank(4 + par)[:, c * P:(c + 1) * P],
                                                  hid[:, par, k, c * P:(c + 1) * P], w2s[:, order[n], k, :],
                                                  start=(k == 0), stop=(k == FK - 1))
                        last.then_inc(s2_ps, 1)

                    eng.sem_inc(s2_ps, 1)
                    with eng.Fori(0, NC // 2) as j:
                        up(j * 2, 0, 0)
                        for s in range(2 * NE):
                            u, n = divmod(s, NE)
                            if s + 1 < 2 * NE:
                                up(j * 2 + (s + 1) // NE, u, (s + 1) % NE)
                            down(j * 2 + u, s % 2, n)
                            if n == NE - 1:
                                eng.wait_ge(bx_added, j * 2 + u)
                                for a in range(2):
                                    last = eng.matmul(ps[:, 6, a * 256:(a + 1) * 256], gflat[:, a * P:(a + 1) * P],
                                                      b2m[:, ds((j * 2 + u) * 2, 2), :].rearrange("p c d -> p (c d)"),
                                                      start=True, stop=True)
                                last.then_inc(bias_ps, 1)

                @block.scalar
                def _(eng):
                    eng.sem_inc(hid_ready, FK - 1)
                    with eng.Fori(0, NC // 2) as j:
                        for s in range(2 * NE):
                            n = s % NE
                            q = j * (2 * NE) + s
                            for k in range(FK):
                                eng.wait_ge(s1_ps, q * FK + k + 1)
                                if k == 0:
                                    eng.wait_ge(s2_ps, q)
                                col = order[n] * FK + k
                                eng.activation(hid[:, s % 2, k, :], bank(k), ACT.Gelu_apprx_tanh,
                                               bias=b1c[:, col:col + 1]).then_inc(hid_ready, 1)

                @block.vector
                def _(eng):
                    step = Chain(eng, f_step)
                    fa = facc[:, :, :]
                    eng.sem_inc(y_used, 1)
                    with eng.Fori(0, NC // 2) as jj:
                        for u in range(2):
                            i = jj * 2 + u
                            step.body(i, NE + 5)
                            for n in range(NE):
                                q = i * NE + n
                                y = bank(4 + (u * NE + n) % 2).rearrange("p (k d) -> p k d", k=4)
                                eng.wait_ge(s2_ps, q + 2)
                                if n == 0:
                                    last = eng.tensor_tensor(fa, y, bs2[:, None, :].to_broadcast([P, 4, D]), ALU.add)
                                else:
                                    for k in range(4):
                                        last = eng.scalar_tensor_tensor(facc[:, k, :], y[:, k, :],
                                                                        gateT[:, order[n], ds(i * 4 + k, 1)], facc[:, k, :],
                                                                        ALU.mult, ALU.add)
                                step(last)
                                eng.sem_inc(y_used, 1)
                            eng.wait_ge(bias_ps, i + 1)
                            step(eng.tensor_tensor(facc[:, :, :].rearrange("p (c j) d -> p j c d", j=2),
                                                   facc[:, :, :].rearrange("p (c j) d -> p j c d", j=2),
                                                   bank(6).rearrange("p (j c d) -> p j c d", j=2, c=2), ALU.add))
                            step(eng.tensor_tensor(fa, fa, gchunk[:, 0, ds(i, 1), :].to_broadcast([P, 4, D]), ALU.mult))
                            xs = x_sb[:, ds(i * 4, 4), :]
                            eng.tensor_tensor(xs, xs, fa, ALU.add).then_inc(bx_added, 1)
                            eng.wait_ge(bx_added, i + 1)
                            token_moments(eng, step, i)
                    step.end(NC)
        rstd_block("ln2")

        w13T = sb("w13T", [P, E1, 2, F1])
        w2b = sb("w2b", [P, NPAIR, 2, D])
        PG = 4
        with ExitStack() as tmp:
            def st(name, shape, dt=F32):
                return tmp.enter_context(nc.sbuf_tensor(name, shape, dt))

            w1n = st("w1n", [P, 2, PG, P])
            w3n = st("w3n", [P, 2, PG, P])
            w2n = st("w2n", [P, 2, 2 * PG, F1])
            wn_loaded = [sem(f"wn_loaded{u}") for u in range(2)]
            wn_turned = sem("wn_turned")
            wn_kept = sem("wn_kept")
            w2_zero = sem("w2_zero")
            ROUNDS = NPAIR // PG
            w1_v = t["L1_ffn_w1"].rearrange("(n e) f h -> (e f) n h", e=2)
            w3_v = t["L1_ffn_w3"].rearrange("(n e) f h -> (e f) n h", e=2)
            w2_v = t["L1_ffn_w2"].rearrange("e h f -> h e f")

            with nc.Block() as block:
                @block.sync
                def _(eng):
                    with eng.Fori(0, ROUNDS // 2) as j:
                        for u in range(2):
                            r = j * 2 + u
                            eng.wait_ge(wn_turned, r + 1)
                            eng.dma_start(w1n[:, u, :, :], w1_v[:, ds(r * PG, PG), :]).then_inc(wn_loaded[u], 16)
                            eng.dma_start(w3n[:, u, :, :], w3_v[:, ds(r * PG, PG), :]).then_inc(wn_loaded[u], 16)
                            eng.dma_start(w2n[:, u, :, :], w2_v[:, ds(r * 2 * PG, 2 * PG), :]).then_inc(wn_loaded[u], 16)

                @block.gpsimd
                def _(eng):
                    eng.memset(w2b[:, :, :, :], 0.0).then_inc(w2_zero, 1)

                @block.tensor
                def _(eng):
                    eng.sem_inc(wn_turned, 2)
                    with eng.Fori(0, ROUNDS // 2) as j:
                        for u in range(2):
                            r = j * 2 + u
                            eng.wait_ge(wn_loaded[u], 48 * (j + 1))
                            eng.wait_ge(wn_kept, r)
                            for q in range(PG):
                                c = slice(q * P, (q + 1) * P)
                                eng.transpose(bank(0)[:, c], w1n[:, u, q, :], ident[:, :])
                                eng.transpose(bank(1)[:, c], w3n[:, u, q, :], ident[:, :])
                                last = eng.transpose(bank(2)[:, c],
                                                     w2n[:, u, 2 * q:2 * q + 2, :].rearrange("p e f -> p (e f)"),
                                                     ident[:, :])
                            last.then_inc(wn_turned, 1)

                @block.scalar
                def _(eng):
                    eng.wait_ge(w2_zero, 1)
                    with eng.Fori(0, ROUNDS) as r:
                        eng.wait_ge(wn_turned, r + 3)
                        for a in range(2):
                            eng.activation(w13T[:, ds(r * 2 * PG, 2 * PG), a, :],
                                           bank(a).rearrange("p (e f) -> p e f", f=F1), ACT.Copy)
                        for e in range(2):
                            rows = slice(e * F1, (e + 1) * F1)
                            last = eng.activation(w2b[rows, ds(r * PG, PG), e, :],
                                                  ps[rows, 2, :].rearrange("p (q h) -> p q h", q=PG), ACT.Copy)
                        last.then_inc(wn_kept, 1)

        with ExitStack() as tmp:
            def st(name, shape, dt=F32):
                return tmp.enter_context(nc.sbuf_tensor(name, shape, dt))

            xn = st("xn3", [P, 2, B, 4, D])
            h3 = st("h3", [P, 2, B, CHUNK])
            fg = st("fg", [P, CHUNK])
            lam = st("lam", [P, CHUNK])
            state = st("state", [P, 2, CHUNK])
            cxn_ready = sem("cxn_ready")
            cxnT_ready = sem("cxnT_ready")
            ch_ready = sem("ch_ready")
            f_ps = sem("f_ps")
            fg_ready = sem("fg_ready")
            lam_ps = sem("lam_ps")
            lam_ready = sem("lam_ready")
            s_ready = sem("s_ready")
            c_out = sem("c_out")
            cx_added = sem("cx_added")
            c_step = sem("c_step")
            ROUNDS_C = CPB // 2
            with nc.Block() as block:
                @block.vector
                def _(eng):
                    step = Chain(eng, c_step)
                    step.straight()
                    step(eng.memset(state[:, 1, CHUNK - 1:CHUNK], 0.0))
                    step.close()
                    with eng.Fori(0, ROUNDS_C) as jj:
                        for u in range(2):
                            j = jj * 2 + u
                            for b in range(B):
                                last = normalized(eng, xn[:, u, b, :, :], j + b * CPB)
                            last.then_inc(cxn_ready, 1)
                            eng.wait_ge(lam_ready, j + 1)
                            eng.tensor_tensor_scan(state[:, u, :], lam[:, :], bank(3),
                                                   state[:, 1 - u, CHUNK - 1:CHUNK], ALU.mult, ALU.add).then_inc(s_ready, 1)
                            eng.wait_ge(c_out, j + 1)
                            for b in range(B):
                                xs = x_sb[:, ds((j + b * CPB) * 4, 4), :]
                                last = eng.tensor_tensor(xs, xs, bank(5 + b).rearrange("p (k d) -> p k d", k=4), ALU.add)
                            last.then_inc(cx_added, 1)
                            eng.wait_ge(cx_added, j + 1)
                            for b in range(B):
                                step.body(j * 2 + b, 3)
                                token_moments(eng, step, j + b * CPB)

                @block.tensor
                def _(eng):
                    with eng.Fori(0, ROUNDS_C) as jj:
                        for u in range(2):
                            j = jj * 2 + u
                            eng.wait_ge(cxn_ready, j + 1)
                            for b in range(B):
                                for k in range(4):
                                    last = eng.transpose(bank(b)[:, k * P:(k + 1) * P], xn[:, u, b, k, :], ident[:, :])
                            last.then_inc(cxnT_ready, 1)
                            eng.wait_ge(ch_ready, j + 1)
                            for w, k in ((w_F, 2), (w_u, 3)):
                                for b in range(B):
                                    last = eng.matmul(ps[b * PR:(b + 1) * PR, k, :], w[:, :], h3[:, u, b, :],
                                                      start=True, stop=True)
                            last.then_inc(f_ps, 1)
                            eng.wait_ge(fg_ready, j + 1)
                            eng.matmul(bank(4), lam_bd[:, :], fg[:, :], start=True, stop=True).then_inc(lam_ps, 1)
                            eng.wait_ge(s_ready, j + 1)
                            for b in range(B):
                                for k in range(4):
                                    c = slice(k * P, (k + 1) * P)
                                    eng.matmul(bank(5 + b)[:, c], h3[:, u, b, c], whx[:, b, :], start=True, stop=False)
                                    last = eng.matmul(bank(5 + b)[:, c], state[:, u, c], whs[:, b, :],
                                                      start=False, stop=True)
                            last.then_inc(c_out, 1)

                @block.scalar
                def _(eng):
                    with eng.Fori(0, ROUNDS_C) as jj:
                        for u in range(2):
                            j = jj * 2 + u
                            eng.wait_ge(cxnT_ready, j + 1)
                            for b in range(B):
                                last = eng.activation(h3[:, u, b, :], bank(b), ACT.Identity,
                                                      bias=shift[:, 1, 1, ds(j + b * CPB, 1)],
                                                      scale=shift[:, 1, 0, ds(j + b * CPB, 1)])
                            last.then_inc(ch_ready, 1)
                            eng.wait_ge(f_ps, j + 1)
                            eng.activation(fg[:, :], bank(2), ACT.Sigmoid).then_inc(fg_ready, 1)
                            eng.wait_ge(lam_ps, j + 1)
                            eng.activation(lam[:, :], bank(4), ACT.Sigmoid).then_inc(lam_ready, 1)
        rstd_block("ln3")

        NG = 8
        GE = E1 // NG
        TG = 4
        SCALE = 2.5
        CAP = P
        HXW = D + E1
        SPARE = P
        hx = nc.dram_tensor("hx", (T + SPARE, HXW), F32).ap()
        acc = [nc.dram_tensor(f"acc{a}", (T + SPARE, D), F32).ap() for a in range(2)]
        hx_v = hx[0:T, :].rearrange("(n p) c -> p n c", p=P)
        xe_sel = sb("xe_sel", [P, E1, NT], BF16)
        hx_stored = [sem(f"hx_stored{u}") for u in range(2)]
        acc_zeroed = sem("acc_zeroed")
        hx_spare = sem("hx_spare")
        with ExitStack() as tmp:
            def st(name, shape, dt=F32):
                return tmp.enter_context(nc.sbuf_tensor(name, shape, dt))

            zt = st("zt", [P, HXW])
            e_bias = st("e_bias", [P, E1])
            lower = st("lower", [P, NG, NG])
            xn = st("xn4", [P, 2, 4, D])
            rows = st("rows", [P, 2, 4, HXW])
            h4 = st("h4", [P, 2, CHUNK])
            sc = st("sc", [P, 2, 4, E1])
            sgm = st("sgm", [P, CHUNK])
            sgl = st("sgl", [P, CHUNK])
            hs = st("hs", [P, CHUNK])
            sfc = st("sfc", [P, 4, E1])
            tmpv = st("tmpv", [P, 4, E1])
            rep = st("rep", [P, 4, E1])
            sel = st("sel", [P, 2, 4, E1])
            top8 = st("top8", [P, 4, 8])
            hi = st("hi", [P, 4 * NG, GE // 2])
            lo = st("lo", [P, 4 * NG, GE // 2])
            mn = st("mn", [P, 4 * NG, GE // 4])
            gsum = st("gsum", [P, 4, NG])
            gt = st("gt", [P, 4, NG, NG])
            ge = st("ge", [P, 4, NG, NG])
            rank = st("rankg", [P, 4, NG])
            wsum = st("wsum", [P, 4])

            ld_b = sem("ld_b")
            z_ready = sem("z_ready")
            zt_ready = sem("zt_ready")
            dn_ready = sem("dn_ready")
            d_part = sem("d_part")
            h4_ready = sem("h4_ready")
            h4_ps = sem("h4_ps")
            h4T_ready = sem("h4T_ready")
            lg4_ps = sem("lg4_ps")
            sc_ready = sem("sc_ready")
            sh_ps = sem("sh_ps")
            sgm_ready = sem("sgm_ready")
            hs_ready = sem("hs_ready")
            dn_ps = sem("dn_ps")
            dx_added = sem("dx_added")
            sel_ready = sem("sel_ready")
            sel_kept = sem("sel_kept")
            w_ready = sem("w_ready")
            d_step = sem("d_step")
            NEVER = -3e38
            with nc.Block() as block:
                @block.sync
                def _(eng):
                    eng.dma_start(e_bias[:, :], t["L1_ffn_e_bias"][None, :].to_broadcast([P, E1])).then_inc(ld_b, 16)
                    eng.wait_ge(zt_ready, 1)
                    for a in range(2):
                        eng.dma_start(acc[a].rearrange("(n p) d -> p n d", p=P),
                                      zt[:, None, 0:D].to_broadcast([P, NT + 1, D])).then_inc(acc_zeroed, 16)
                    eng.dma_start(hx[T:T + SPARE, :], zt[:, :]).then_inc(hx_spare, 16)
                    with eng.Fori(0, NC // 2) as j:
                        for u in range(2):
                            i = j * 2 + u
                            eng.wait_ge(w_ready, i + 2)
                            eng.dma_start(hx_v[:, ds(i * 4, 4), :], rows[:, u, :, :]).then_inc(hx_stored[u], 16)
                    eng.wait_ge(hx_spare, 16)
                    eng.wait_ge(acc_zeroed, 32)
                    for u in range(2):
                        eng.wait_ge(hx_stored[u], 16 * (NC // 2))

                @block.gpsimd
                def _(eng):
                    eng.memset(zt[:, :], 0.0).then_inc(zt_ready, 1)
                    eng.memset(lower[:, :, :], 1.0).then_inc(z_ready, 1)
                    eng.wait_ge(z_ready, 1)
                    eng.affine_select(out=lower[:, :, :], in_=lower[:, :, :], compare_op=ALU.is_gt, fill=0.0, base=0,
                                      pattern=[[1, NG], [-1, NG]], channel_multiplier=0).then_inc(z_ready, 1)

                    def modulate(i, u):
                        eng.wait_ge(dn_ready, i + 1)
                        eng.wait_ge(hx_stored[u], (i - u) * 8)
                        r = rows[:, u, :, 0:D]
                        eng.tensor_tensor(r, xn[:, u, :, :], schunk[:, ds(i, 1), 1, :].to_broadcast([P, 4, D]),
                                          ALU.mult).then_inc(d_part, 1)
                        eng.wait_ge(d_part, i + 1)
                        eng.tensor_tensor(r, r, schunk[:, ds(i, 1), 0, :].to_broadcast([P, 4, D]),
                                          ALU.add).then_inc(h4_ready, 1)

                    def body(i, u, prev, nxt):
                        if nxt:
                            modulate(i + 1, 1 - u)
                        eng.wait_ge(sel_ready, i + 1)
                        eng.tensor_copy(xe_sel[:, :, ds(i * 4, 4)],
                                        sel[:, u, :, :].rearrange("p k e -> p e k")).then_inc(sel_kept, 1)

                    modulate(0, 0)
                    chunks(eng, body)

                @block.tensor
                def _(eng):
                    def score(i, u):
                        eng.wait_ge(h4_ready, i + 1)
                        eng.wait_ge(h4T_ready, i)
                        for k in range(4):
                            last = eng.transpose(bank(0)[:, k * P:(k + 1) * P], rows[:, u, k, 0:D], ident[:, :])
                        last.then_inc(h4_ps, 1)
                        eng.wait_ge(h4T_ready, i + 1)
                        eng.wait_ge(sc_ready, i)
                        for k in range(4):
                            last = eng.matmul(ps[:, 2, k * E1:(k + 1) * E1], h4[:, u, k * P:(k + 1) * P], gw1[:, :],
                                              start=True, stop=True)
                        last.then_inc(lg4_ps, 1)

                    def up(i, u):
                        eng.wait_ge(hs_ready, i)
                        eng.matmul(bank(4), sgT[:, :], h4[:, u, :], start=True, stop=True)
                        eng.matmul(bank(5), suT[:, :], h4[:, u, :], start=True, stop=True).then_inc(sh_ps, 1)

                    def body(i, u, prev, nxt):
                        if nxt:
                            score(i + 1, 1 - u)
                        eng.wait_ge(hs_ready, i + 1)
                        eng.wait_ge(dx_added, i)
                        for k in range(4):
                            last = eng.matmul(bank(6)[:, k * P:(k + 1) * P], hs[:, k * P:(k + 1) * P],
                                              sdg[:, ds(i, 1), :].rearrange("p a d -> p (a d)"), start=True, stop=True)
                        last.then_inc(dn_ps, 1)
                        if nxt:
                            up(i + 1, 1 - u)

                    score(0, 0)
                    up(0, 0)
                    chunks(eng, body)

                @block.scalar
                def _(eng):
                    with eng.Fori(0, NC // 2) as j:
                        for u in range(2):
                            i = j * 2 + u
                            eng.wait_ge(h4_ps, i + 1)
                            eng.wait_ge(lg4_ps, i)
                            eng.wait_ge(sh_ps, i)
                            eng.activation(h4[:, u, :], bank(0), ACT.Copy).then_inc(h4T_ready, 1)
                            eng.wait_ge(lg4_ps, i + 1)
                            eng.wait_ge(w_ready, i)
                            eng.activation(sc[:, u, :, :], ps[:, 2, 0:4 * E1].rearrange("p (k e) -> p k e", k=4),
                                           ACT.Sigmoid).then_inc(sc_ready, 1)
                            eng.wait_ge(sh_ps, i + 1)
                            eng.wait_ge(hs_ready, i)
                            eng.activation(sgm[:, :], bank(4), ACT.Sigmoid).then_inc(sgm_ready, 1)

                @block.vector
                def _(eng):
                    step = Chain(eng, d_step)
                    eng.sem_inc(w_ready, 1)
                    eng.wait_ge(ld_b, 16)
                    eng.wait_ge(z_ready, 2)
                    normalized(eng, xn[:, 0, :, :], 0).then_inc(dn_ready, 1)

                    def body(i, u, prev, nxt):
                        step.body(i, 22)
                        if nxt:
                            eng.wait_ge(h4_ready, i)
                            normalized(eng, xn[:, 1 - u, :, :], i + 1).then_inc(dn_ready, 1)
                        eng.wait_ge(sgm_ready, i + 1)
                        step(eng.tensor_tensor(sgl[:, :], sgm[:, :], bank(4), ALU.mult))
                        eng.tensor_tensor(hs[:, :], sgl[:, :], bank(5), ALU.mult).then_inc(hs_ready, 1)
                        eng.wait_ge(sc_ready, i + 1)
                        s = sc[:, u, :, :]
                        step(eng.tensor_tensor(sfc[:, :, :], s, e_bias[:, None, :].to_broadcast([P, 4, E1]), ALU.add))
                        v = sfc[:, :, :].rearrange("p k (g x) -> p (k g) x", g=NG)
                        q, r = GE // 2, GE // 4
                        eng.tensor_tensor(hi[:, :, :], v[:, :, 0:q], v[:, :, q:GE], ALU.max)
                        step(eng.tensor_tensor(lo[:, :, :], v[:, :, 0:q], v[:, :, q:GE], ALU.min))
                        for w in (r, r // 2):
                            eng.tensor_tensor(mn[:, :, 0:w], hi[:, :, 0:w], hi[:, :, w:2 * w], ALU.min)
                            step(eng.tensor_tensor(lo[:, :, 0:w], lo[:, :, 0:w], lo[:, :, w:2 * w], ALU.max))
                            eng.tensor_tensor(lo[:, :, 0:w], lo[:, :, 0:w], mn[:, :, 0:w], ALU.max)
                            step(eng.tensor_tensor(hi[:, :, 0:w], hi[:, :, 0:w], hi[:, :, w:2 * w], ALU.max))
                        step(eng.tensor_tensor(gsum[:, :, :].rearrange("p k g -> p (k g)"), hi[:, :, 0], lo[:, :, 0], ALU.add))
                        other = gsum[:, :, None, :].to_broadcast([P, 4, NG, NG])
                        mine = gsum[:, :, :, None].to_broadcast([P, 4, NG, NG])
                        eng.tensor_tensor(gt[:, :, :, :], other, mine, ALU.is_gt)
                        step(eng.tensor_tensor(ge[:, :, :, :], other, mine, ALU.is_equal))
                        step(eng.tensor_tensor(ge[:, :, :, :], ge[:, :, :, :],
                                               lower[:, None, :, :].to_broadcast([P, 4, NG, NG]), ALU.mult))
                        step(eng.tensor_tensor(gt[:, :, :, :], gt[:, :, :, :], ge[:, :, :, :], ALU.add))
                        step(eng.tensor_reduce(rank[:, :, :], gt[:, :, :, :], AX, ALU.add))
                        step(eng.tensor_scalar(rank[:, :, :], rank[:, :, :], float(TG), None, ALU.is_lt))
                        step(eng.tensor_tensor(tmpv[:, :, :].rearrange("p k (g x) -> p k g x", g=NG),
                                               sfc[:, :, :].rearrange("p k (g x) -> p k g x", g=NG),
                                               rank[:, :, :, None].to_broadcast([P, 4, NG, GE]), ALU.mult))
                        step(eng.tensor_scalar(tmpv[:, :, :], tmpv[:, :, :], 0.0, None, ALU.add))
                        eng.nop(nofuse=True)
                        for k in range(4):
                            last = eng.max(top8[:, k, :], tmpv[:, k, :])
                        step(last)
                        eng.nop(nofuse=True)
                        for k in range(4):
                            last = eng.match_replace(rep[:, k, :], top8[:, k, :], tmpv[:, k, :], NEVER)
                        step(last)
                        eng.wait_ge(sel_kept, i)
                        eng.tensor_scalar(sel[:, u, :, :], rep[:, :, :], NEVER, None, ALU.is_equal).then_inc(sel_ready, 1)
                        eng.wait_ge(sel_ready, i + 1)
                        step(eng.tensor_tensor(rep[:, :, :], sel[:, u, :, :], s, ALU.mult))
                        step(eng.tensor_reduce(wsum[:, :], rep[:, :, :], AX, ALU.add))
                        step(eng.tensor_scalar(wsum[:, :], wsum[:, :], 1e-20, None, ALU.add))
                        step(eng.reciprocal(wsum[:, :], wsum[:, :]))
                        step(eng.tensor_scalar(wsum[:, :], wsum[:, :], SCALE, None, ALU.mult))
                        eng.wait_ge(h4_ready, i + 1)
                        eng.tensor_tensor(rows[:, u, :, D:HXW], rep[:, :, :],
                                          wsum[:, :, None].to_broadcast([P, 4, E1]), ALU.mult).then_inc(w_ready, 1)
                        eng.wait_ge(dn_ps, i + 1)
                        xs = x_sb[:, ds(i * 4, 4), :]
                        eng.tensor_tensor(xs, xs, bank(6).rearrange("p (k d) -> p k d", k=4), ALU.add).then_inc(dx_added, 1)

                    chunks(eng, body)
                    step.end(NC)

        GROUPS = E1 * NT // P
        EG = E1 // GROUPS
        idx = sb("idx", [P, E1], I32)
        with ExitStack() as tmp:
            def st(name, shape, dt=F32):
                return tmp.enter_context(nc.sbuf_tensor(name, shape, dt))

            rinc = st("rinc", [P, E1, NT], BF16)
            keep = st("keep", [P, E1, NT], BF16)
            selR = st("selR", [P, P + 1], BF16)
            oneR = st("oneR", [P, P + 1], BF16)
            io_i = st("io_i", [P, P], I32)
            iota = st("iota", [P, P])
            cc_i = st("cc_i", [P, 1], I32)
            ccol = st("ccol", [P, 1])
            pay = st("pay", [P, EG, 2], BF16)
            inM = st("inM", [P, GROUPS, EG, P], BF16)
            edge = st("edge", [P, GROUPS, 2])
            oh = st("oh", [P, GROUPS, P])
            oh_b = st("oh_b", [P, GROUPS, P])
            ohb = st("ohb", [P, GROUPS, P], BF16)
            le = st("le", [P, EG, P])
            cnt = st("cnt4", [P, E1])
            nv = st("nv", [P, E1, 2])
            spare = st("spare", [P, 1])
            f1 = st("f1", [P, E1])
            k_step = sem("k_step")
            k_ready = sem("k_ready")
            r_done = sem("r_done")
            in_ps = sem("in_ps")
            in_act = sem("in_act")
            oh_ready = sem("oh_ready")
            slot_ps = sem("slot_ps")
            slot_used = sem("slot_used")
            idx_step = sem("idx_step")
            with nc.Block() as block:
                @block.gpsimd
                def _(eng):
                    step = Chain(eng, k_step)
                    step.straight()
                    eng.memset(keep[:, :, :], 1.0)
                    eng.memset(oneR[:, :], 1.0)
                    eng.memset(pay[:, :, :], 0.0)
                    eng.memset(inM[:, :, :, :], 0.0)
                    eng.iota(io_i[:, :], pattern=[[1, P]], base=0, channel_multiplier=0)
                    eng.iota(cc_i[:, :], pattern=[[1, 1]], base=0, channel_multiplier=1)
                    step(eng.memset(selR[:, :], -1.0))
                    eng.memset(keep[:, :, 0:1], 0.0)
                    step(eng.affine_select(out=selR[:, 0:P], in_=selR[:, 0:P], compare_op=ALU.is_gt, fill=0.0, base=0,
                                           pattern=[[-1, P]], channel_multiplier=1))
                    eng.tensor_copy(iota[:, :], io_i[:, :])
                    step(eng.tensor_copy(ccol[:, :], cc_i[:, :]))
                    for a in range(EG):
                        r = slice(a * NT, (a + 1) * NT)
                        eng.tensor_scalar(pay[r, a, 0:1], ccol[r, :], float(-a * NT), None, ALU.add)
                        last = eng.tensor_copy(pay[r, a, 1:2], ones[r, 0:1])
                    step(last)
                    eng.sem_inc(k_ready, 1)

                @block.tensor
                def _(eng):
                    eng.wait_ge(r_done, 1)
                    for g in range(GROUPS):
                        e = slice(g * EG, (g + 1) * EG)
                        o = ps[:, g // 2, (g % 2) * 256:(g % 2) * 256 + P + 1]
                        eng.matmul(o, xe_sel[:, e, :].rearrange("p e n -> p (e n)"), selR[:, :], start=True, stop=False)
                        last = eng.matmul(o, rinc[:, e, :].rearrange("p e n -> p (e n)"), oneR[:, :], start=False, stop=True)
                    last.then_inc(in_ps, 1)
                    eng.wait_ge(oh_ready, 1)
                    eng.wait_ge(in_act, 1)
                    for g in range(GROUPS):
                        if g >= 4:
                            eng.wait_ge(slot_used, g - 3)
                        eng.matmul(bank(g % 4), ohb[:, g, :], inM[:, g, :, :].rearrange("p e m -> p (e m)"),
                                   start=True, stop=True)
                        eng.matmul(ps[:, 4 + g % 4, 0:2 * EG], ohb[:, g, :], pay[:, :, :].rearrange("p e a -> p (e a)"),
                                   start=True, stop=True).then_inc(slot_ps, 1)

                @block.scalar
                def _(eng):
                    eng.wait_ge(in_ps, 1)
                    eng.wait_ge(k_ready, 1)
                    wide = ps[:, :, :].rearrange("p b (h c) -> p (b h) c", h=2)
                    for a in range(EG):
                        r = slice(a * NT, (a + 1) * NT)
                        last = eng.activation(inM[r, :, a, :], wide[r, :, 0:P], ACT.Copy)
                    last.then_inc(in_act, 1)

                @block.vector
                def _(eng):
                    step = Chain(eng, idx_step)
                    step.straight()
                    eng.wait_ge(k_ready, 1)
                    eng.tensor_tensor_scan(rinc[:, :, :].rearrange("p e n -> p (e n)"),
                                           keep[:, :, :].rearrange("p e n -> p (e n)"),
                                           xe_sel[:, :, :].rearrange("p e n -> p (e n)"), 0.0,
                                           ALU.mult, ALU.add).then_inc(r_done, 1)
                    eng.wait_ge(in_ps, 1)
                    eng.wait_ge(in_act, 1)
                    wide = ps[:, :, :].rearrange("p b (h c) -> p (b h) c", h=2)
                    eng.tensor_copy(edge[:, :, 0], wide[:, :, P])
                    step(eng.tensor_copy(edge[:, :, 1], wide[:, :, P - 1]))
                    io = iota[:, None, :].to_broadcast([P, GROUPS, P])
                    eng.tensor_tensor(oh[:, :, :], io, edge[:, :, 0:1].to_broadcast([P, GROUPS, P]), ALU.is_ge)
                    step(eng.tensor_tensor(oh_b[:, :, :], io, edge[:, :, 1:2].to_broadcast([P, GROUPS, P]), ALU.is_ge))
                    step(eng.tensor_tensor(ohb[:, :, :], oh[:, :, :], oh_b[:, :, :], ALU.subtract))
                    eng.sem_inc(oh_ready, 1)
                    for g in range(GROUPS):
                        eng.wait_ge(slot_ps, g + 1)
                        eng.tensor_copy(nv[:, g * EG:(g + 1) * EG, :].rearrange("p e a -> p (e a)"),
                                        ps[:, 4 + g % 4, 0:2 * EG])
                        for a in range(EG):
                            last = eng.tensor_scalar(le[:, a, :], bank(g % 4)[:, a * P:(a + 1) * P], ccol[:, :], 0.0,
                                                     ALU.is_le, ALU.add, accum_out=cnt[:, g * EG + a:g * EG + a + 1])
                        step(last)
                        eng.sem_inc(slot_used, 1)
                    step(eng.tensor_scalar(spare[:, :], ccol[:, :], float(T - P), None, ALU.add))
                    step(eng.scalar_tensor_tensor(f1[:, :], nv[:, :, 0], float(P), cnt[:, :], ALU.mult, ALU.add))
                    step(eng.tensor_scalar(f1[:, :], f1[:, :], spare[:, :], None, ALU.add))
                    step(eng.tensor_scalar(nv[:, :, 1], nv[:, :, 1], spare[:, :], None, ALU.mult))
                    step(eng.tensor_tensor(idx[:, :], f1[:, :], nv[:, :, 1], ALU.subtract))

        with ExitStack() as tmp:
            def st(name, shape, dt=F32):
                return tmp.enter_context(nc.sbuf_tensor(name, shape, dt))

            KE = 4
            RE = E1 // KE
            PER_ROUND = KE // 2 * 16
            ixs = st("ixs", [P, 4, KE], I32)
            gath = st("gath", [P, 2, KE, HXW])
            gT = st("gT", [P, 2, KE, P])
            sl = st("sl", [P, 2, KE, F1])
            hh = st("hh", [P, 2, KE, F1])
            hhT = st("hhT", [P, 2, KE // 2, P])
            ysc = st("ysc", [P, 2, KE, D])
            ix_ready = sem("ix_ready")
            gathered = [sem(f"gathered{u}") for u in range(2)]
            g_ps = sem("g_ps")
            gT_ready = sem("gT_ready")
            up_ps = sem("up_ps")
            sl_ready = sem("sl_ready")
            hh_ready = sem("hh_ready")
            hh_ps = sem("hh_ps")
            hhT_ready = sem("hhT_ready")
            y_ps = sem("y_ps")
            ysc_ready = sem("ysc_ready")
            added = [sem(f"added{a}") for a in range(2)]
            with nc.Block() as block:
                @block.gpsimd
                def _(eng):
                    def gather(r, s):
                        u = s % 2
                        if type(r) is not int or r >= 2:
                            eng.wait_ge(ysc_ready, r - 1)
                        if type(r) is not int or r >= 4:
                            for a in range(2):
                                eng.wait_ge(added[a], (r - 3) * PER_ROUND)
                        eng.tensor_copy(ixs[:, s, :], idx[:, ds(r * KE, KE)]).then_inc(ix_ready, 1)
                        eng.wait_ge(ix_ready, r + 1)
                        eng.nop(nofuse=True)
                        for k in range(KE):
                            eng.indirect_dma_start(out=gath[:, u, k, :], out_offset=None, in_=hx,
                                                   in_offset=bass.IndirectOffsetOnAxis(ap=ixs[:, s, k:k + 1], axis=0)
                                                   ).then_inc(gathered[u], 16)

                    def scatter(r, s):
                        eng.wait_ge(ysc_ready, r + 1)
                        for k in range(KE):
                            eng.wait_ge(added[k % 2], r * PER_ROUND + k // 2 * 16)
                            eng.nop(nofuse=True)
                            eng.indirect_dma_start(out=acc[k % 2],
                                                   out_offset=bass.IndirectOffsetOnAxis(ap=ixs[:, s, k:k + 1], axis=0),
                                                   in_=ysc[:, s % 2, k, :], in_offset=None,
                                                   compute_op=ALU.add).then_inc(added[k % 2], 16)

                    eng.wait_ge(hx_spare, 16)
                    eng.wait_ge(acc_zeroed, 32)
                    for u in range(2):
                        eng.wait_ge(hx_stored[u], 16 * (NC // 2))
                    gather(0, 0)
                    for s in range(4):
                        gather(s + 1, (s + 1) % 4)
                        scatter(s, s)
                    with eng.Fori(1, RE // 4 - 1) as j:
                        for s in range(4):
                            gather(j * 4 + s + 1, (s + 1) % 4)
                            scatter(j * 4 + s, s)
                    for s in range(4):
                        if s < 3:
                            gather(RE - 4 + s + 1, s + 1)
                        scatter(RE - 4 + s, s)

                @block.tensor
                def _(eng):
                    with eng.Fori(0, RE // 2) as j:
                        for u in range(2):
                            r = j * 2 + u
                            eng.wait_ge(gathered[u], (j + 1) * 16 * KE)
                            eng.wait_ge(gT_ready, r)
                            for k in range(KE):
                                last = eng.transpose(bank(0)[:, k * P:(k + 1) * P], gath[:, u, k, 0:D], ident[:, :])
                            last.then_inc(g_ps, 1)
                            eng.wait_ge(gT_ready, r + 1)
                            eng.wait_ge(hh_ready, r)
                            for k in range(KE):
                                last = eng.matmul(bank(1)[:, k * P:(k + 1) * P], gT[:, u, k, :],
                                                  w13T[:, ds(r * KE + k, 1), :, :].rearrange("p e a f -> p (e a f)"),
                                                  start=True, stop=True)
                            last.then_inc(up_ps, 1)
                            eng.wait_ge(hh_ready, r + 1)
                            eng.wait_ge(hhT_ready, r)
                            for q in range(KE // 2):
                                last = eng.transpose(ps[:, 2, q * P:(q + 1) * P],
                                                     hh[:, u, 2 * q:2 * q + 2, :].rearrange("p e f -> p (e f)"), ident[:, :])
                            last.then_inc(hh_ps, 1)
                            eng.wait_ge(hhT_ready, r + 1)
                            eng.wait_ge(ysc_ready, r)
                            for q in range(KE // 2):
                                last = eng.matmul(bank(3)[:, q * 256:(q + 1) * 256], hhT[:, u, q, :],
                                                  w2b[:, ds(r * (KE // 2) + q, 1), :, :].rearrange("p a e h -> p (a e h)"),
                                                  start=True, stop=True)
                            last.then_inc(y_ps, 1)

                @block.scalar
                def _(eng):
                    with eng.Fori(0, RE // 2) as j:
                        for u in range(2):
                            r = j * 2 + u
                            eng.wait_ge(g_ps, r + 1)
                            eng.wait_ge(up_ps, r)
                            eng.activation(gT[:, u, :, :].rearrange("p k c -> p (k c)"), bank(0), ACT.Copy).then_inc(gT_ready, 1)
                            eng.wait_ge(up_ps, r + 1)
                            eng.wait_ge(hh_ready, r)
                            eng.activation(sl[:, u, :, :], bank(1).rearrange("p (k a f) -> p k a f", k=KE, a=2)[:, :, 0, :],
                                           ACT.Silu).then_inc(sl_ready, 1)
                            eng.wait_ge(hh_ps, r + 1)
                            eng.wait_ge(y_ps, r)
                            eng.activation(hhT[:, u, :, :].rearrange("p q c -> p (q c)"), ps[:, 2, 0:2 * P],
                                           ACT.Copy).then_inc(hhT_ready, 1)

                @block.vector
                def _(eng):
                    def body(r, u):
                        eng.wait_ge(sl_ready, r + 1)
                        eng.wait_ge(hh_ps, r)
                        eng.tensor_tensor(hh[:, u, :, :], sl[:, u, :, :],
                                          bank(1).rearrange("p (k a f) -> p k a f", k=KE, a=2)[:, :, 1, :],
                                          ALU.mult).then_inc(hh_ready, 1)
                        eng.wait_ge(y_ps, r + 1)
                        if type(r) is not int or r >= 2:
                            for a in range(2):
                                eng.wait_ge(added[a], (r - 1) * PER_ROUND)
                        for k in range(KE):
                            last = eng.tensor_scalar(ysc[:, u, k, :], bank(3)[:, k * P:(k + 1) * P],
                                                     gath[:, u, k, ds(D + r * KE + k, 1)], None, ALU.mult)
                        last.then_inc(ysc_ready, 1)

                    body(0, 0)
                    body(1, 1)
                    with eng.Fori(1, RE // 2) as j:
                        for u in range(2):
                            body(j * 2 + u, u)

        with ExitStack() as tmp:
            accs = tmp.enter_context(nc.sbuf_tensor("accs", [P, 2, NT, D], F32))
            ld_acc = [sem(f"ld_acc{q}") for q in range(4)]
            f_part = sem("f_part")
            res_ready = sem("res_ready")
            st_out = sem("st_out")
            NQ = NT // 4
            with nc.Block() as block:
                @block.sync
                def _(eng):
                    for a in range(2):
                        eng.wait_ge(added[a], E1 // 2 * 16)
                    for q in range(4):
                        for a in range(2):
                            eng.dma_start(accs[:, a, q * NQ:(q + 1) * NQ, :],
                                          acc[a][0:T, :].rearrange("(n p) d -> p n d", p=P)[:, q * NQ:(q + 1) * NQ, :]
                                          ).then_inc(ld_acc[q], 16)
                    for q in range(4):
                        eng.wait_ge(res_ready, q + 1)
                        eng.dma_start(out_v[:, q * NQ:(q + 1) * NQ, :], x_sb[:, q * NQ:(q + 1) * NQ, :]).then_inc(st_out, 16)
                    eng.wait_ge(st_out, 64)

                @block.vector
                def _(eng):
                    step = Chain(eng, f_part)
                    step.straight()
                    for q in range(4):
                        eng.wait_ge(ld_acc[q], 32)
                        a0, a1 = (accs[:, a, q * NQ:(q + 1) * NQ, :] for a in range(2))
                        step(eng.tensor_tensor(a0, a0, a1, ALU.add))
                        step(eng.tensor_tensor(a0.rearrange("p (c k) d -> p c k d", k=4), a0.rearrange("p (c k) d -> p c k d", k=4),
                                               gchunk[:, 1, q * NQ // 4:(q + 1) * NQ // 4, None, :].to_broadcast([P, NQ // 4, 4, D]),
                                               ALU.mult))
                        xs = x_sb[:, q * NQ:(q + 1) * NQ, :]
                        eng.tensor_tensor(xs, xs, a0, ALU.add).then_inc(res_ready, 1)


_INS = [
    'L0_attn_x', 'L0_attn_w_qkv', 'L0_attn_w_out', 'L0_attn_b_out', 'L0_attn_proj', 'L0_ffn_gate_weight',
    'L0_ffn_W1', 'L0_ffn_b1', 'L0_ffn_W2', 'L0_ffn_b2', 'L0_ffn_Ws1', 'L0_ffn_bs1', 'L0_ffn_Ws2',
    'L0_ffn_bs2', 'L0_c', 'L0_wmod', 'L1_attn_W_toP', 'L1_attn_W_U', 'L1_attn_W_F', 'L1_attn_W_V',
    'L1_attn_W_lam', 'L1_attn_B_mat', 'L1_attn_C_mat', 'L1_attn_W_fromP', 'L1_ffn_gate_weight',
    'L1_ffn_e_bias', 'L1_ffn_w1', 'L1_ffn_w2', 'L1_ffn_w3', 'L1_ffn_shared_gate', 'L1_ffn_shared_up',
    'L1_ffn_shared_down', 'L1_c', 'L1_wmod',
]
_OUTS = [((2, 2048, 128), "float32")]


def kernel(**inputs):
    import numpy as _np
    import concourse.bacc as _bacc
    from concourse import mybir as _mybir
    from concourse.bass_utils import run_bass_kernel_spmd as _run

    nc = _bacc.Bacc("TRN2", target_bir_lowering=False, num_devices=1)
    arrays, args, outs = {}, {}, []
    for name in _INS:
        a = _np.ascontiguousarray(inputs[name])
        arrays[f"in_{name}_dram"] = a
        args[name] = nc.dram_tensor(f"in_{name}_dram", a.shape, _mybir.dt.from_np(a.dtype), kind="ExternalInput").ap()
    for i, (shape, dtype) in enumerate(_OUTS):
        dt = _mybir.dt.from_np(_np.dtype(dtype))
        outs.append(nc.dram_tensor(f"out_{i}_dram", shape, dt, kind="ExternalOutput").ap())
    build(nc, args, outs[0])
    r = _run(nc, [arrays], core_ids=[0])
    return r.results[0]["out_0_dram"]
```

```python
from contextlib import ExitStack

import concourse.bass as bass
from concourse import mybir

F32 = mybir.dt.float32
BF16 = mybir.dt.bfloat16
I32 = mybir.dt.int32
ALU = mybir.AluOpType
ACT = mybir.ActivationFunctionType
AX = mybir.AxisListType.X
ds = bass.ds

P = 128
TILE = 128
CHUNK_TILES = 4
CHUNK = CHUNK_TILES * TILE
LN_EPS = 1e-5


class Steps:

    def __init__(self, sem):
        self.sem, self.past = sem, 0


class Chain:

    def __init__(self, engine, steps):
        self.engine, self.steps, self.k = engine, steps, 0

    def body(self, i, n):
        self.base, self.n, self.k = self.steps.past + i * n, n, 0

    def end(self, rounds):
        assert self.k == self.n, (self.k, self.n)
        self.steps.past, self.k = self.steps.past + rounds * self.n, 0

    def straight(self):
        self.base = self.steps.past

    def __call__(self, ins):
        self.k += 1
        ins.then_inc(self.steps.sem, 1)
        self.engine.wait_ge(self.steps.sem, self.base + self.k)

    def close(self):
        self.steps.past, self.k = self.steps.past + self.k, 0


def build(nc, t, out):
    B, T1, D = t["L0_attn_x"].shape
    T = B * T1
    NT = T // TILE
    NC = T // CHUNK
    CPB = NC // B
    H, HD, FT = t["L0_attn_proj"].shape
    E0, _, FF = t["L0_ffn_W1"].shape
    FK = FF // P
    E1, F1, _ = t["L1_ffn_w1"].shape
    PR = t["L1_attn_W_lam"].shape[1]
    ALPHA = t["L1_attn_W_V"].shape[1]
    NPAIR = E1 // 2
    x_in = t["L0_attn_x"].rearrange("b (n p) d -> p (b n) d", p=P)
    out_v = out.rearrange("b (n p) d -> p (b n) d", p=P)

    with ExitStack() as ctx:
        def sb(name, shape, dt=F32):
            return ctx.enter_context(nc.sbuf_tensor(name, shape, dt))

        def sem(name):
            return ctx.enter_context(nc.semaphore(name))

        ps = ctx.enter_context(nc.psum_tensor("ps", [P, 8, 512], F32))

        def bank(k):
            return ps[:, k, :]

        ident = sb("ident", [P, P])
        ones = sb("ones", [P, P])
        ones_bf = sb("ones_bf", [P, P], BF16)
        before = sb("before", [P, P])
        before_bf = sb("before_bf", [P, P], BF16)
        x_sb = sb("x_sb", [P, NT, D])
        moments = sb("moments", [P, NT, 2])
        rstd = sb("rstd", [P, NT])
        scT = sb("scT", [P, 2 * B])
        shift = sb("shift", [P, 2, 4, NC])
        grow = sb("grow", [P, 2 * B, 2, D])
        schunk = sb("schunk", [P, 2, NC, 2, D])
        gchunk = sb("gchunk", [P, 2, NC, D])
        wf = sb("wf", [P, 2, H, FT])
        wv = sb("wv", [P, D])
        wob = sb("wob", [P, NC, 2, D])
        bob = sb("bob", [1, NC, D])
        gw0 = sb("gw0", [P, E0])
        gw1 = sb("gw1", [P, E1])
        b1c = sb("b1c", [P, (E0 + 1) * FK])
        w_F = sb("w_F", [P, PR])
        w_u = sb("w_u", [P, PR])
        lam_bd = sb("lam_bd", [P, P])
        whx = sb("whx", [P, B, D])
        whs = sb("whs", [P, B, D])
        sgT = sb("sgT", [P, P])
        suT = sb("suT", [P, P])
        sdg = sb("sdg", [P, NC, D])
        dsel = sb("dsel", [P, P])
        blockmask = sb("blockmask", [P, P])
        stats6 = sb("stats6", [P, 4, 6])
        mom4 = sb("mom4", [P, 4, 2])

        vector_steps = Steps(sem("vector_steps"))
        gpsimd_steps = Steps(sem("gpsimd_steps"))
        var_ready = sem("var_ready")
        std_ready = sem("std_ready")
        ld_acc = [sem(f"ld_acc{q}") for q in range(4)]
        ld_x = sem("ld_x")
        ld_mod = sem("ld_mod")
        ld_w = sem("ld_w")
        mod_c = sem("mod_c")
        c_turned = sem("c_turned")
        mod_b = sem("mod_b")
        mod_ps = sem("mod_ps")

        with ExitStack() as tmp:
            def st(name, shape, dt=F32):
                return tmp.enter_context(nc.sbuf_tensor(name, shape, dt))

            wmod = st("wmod", [P, 2, 6 * D])
            c_rows = st("c_rows", [2 * B, D])
            wqkv = st("wqkv", [P, 3, D])
            projblk = st("projblk", [P, H, FT])
            wo_n = st("wo_n", [P, D])
            wop = st("wop", [P, 2, 4, 32])
            bo_n = st("bo_n", [1, D])
            g0n = st("g0n", [E0, D])
            g1n = st("g1n", [E1, D])
            b1n = st("b1n", [(E0 + 1) * FK, P])
            toP = st("toP", [P, PR])
            wU = st("wU", [P, PR, ALPHA])
            wV = st("wV", [P, PR, ALPHA])
            wUV = st("wUV", [P, PR, ALPHA])
            wt = st("wt", [P, PR])
            wtT = st("wtT", [PR, P])
            Bm = st("Bm", [PR, PR])
            Cm = st("Cm", [PR, PR])
            CT = st("CT", [PR, 2, PR])
            fP = st("fP", [PR, D])
            sgn = st("sgn", [P, D])
            sun = st("sun", [P, D])
            sdn = st("sdn", [P, P])
            scb = st("scb", [P, 2 * B, P])
            modT = st("modT", [P, 2, 6, B])
            graw = st("graw", [P, 2 * B, 2, D])
            gsg = st("gsg", [P, 2 * B, 2, D])

            zeroed = sem("zeroed")
            wts_ps = sem("wts_ps")
            turned = sem("turned")
            fold_ps = sem("fold_ps")
            wt_done = sem("wt_done")
            N_LOADS = H + B + 17

            with nc.Block() as block:
                @block.sync
                def _(eng):
                    eng.dma_start(c_rows[0:B, :], t["L0_c"]).then_inc(ld_mod, 16)
                    eng.dma_start(c_rows[B:2 * B, :], t["L1_c"]).then_inc(ld_mod, 16)
                    eng.dma_start(wmod[:, 0, :], t["L0_wmod"]).then_inc(ld_mod, 16)
                    eng.dma_start(wmod[:, 1, :], t["L1_wmod"]).then_inc(ld_mod, 16)
                    for q in range(4):
                        n = NT // 4
                        eng.dma_start(x_sb[:, q * n:(q + 1) * n, :], x_in[:, q * n:(q + 1) * n, :]).then_inc(ld_x, 16)
                    eng.wait_ge(zeroed, 1)
                    for h in range(H):
                        eng.dma_start(projblk[h * HD:(h + 1) * HD, h, :], t["L0_attn_proj"][h]).then_inc(ld_w, 16)
                    for b in range(B):
                        eng.dma_start(lam_bd[b * PR:(b + 1) * PR, b * PR:(b + 1) * PR],
                                      t["L1_attn_W_lam"]).then_inc(ld_w, 16)
                    for dst, src in [
                        (wqkv[:, :, :], t["L0_attn_w_qkv"].rearrange("(g o) d -> o g d", o=P)),
                        (wo_n[:, :], t["L0_attn_w_out"]),
                        (bo_n[:, :], t["L0_attn_b_out"].rearrange("(a d) -> a d", a=1)),
                        (g0n[:, :], t["L0_ffn_gate_weight"]),
                        (g1n[:, :], t["L1_ffn_gate_weight"]),
                        (b1n[0:E0 * FK, :], t["L0_ffn_b1"].rearrange("e (k p) -> (e k) p", p=P)),
                        (b1n[E0 * FK:, :], t["L0_ffn_bs1"].rearrange("(k p) -> k p", p=P)),
                        (toP[:, :], t["L1_attn_W_toP"]),
                        (wU[:, :, :], t["L1_attn_W_U"]),
                        (wV[:, :, :], t["L1_attn_W_V"][None, :, :].to_broadcast([P, PR, ALPHA])),
                        (w_F[:, :], t["L1_attn_W_F"]),
                        (Bm[:, :], t["L1_attn_B_mat"]),
                        (Cm[:, :], t["L1_attn_C_mat"]),
                        (fP[:, :], t["L1_attn_W_fromP"]),
                        (sgn[:, :], t["L1_ffn_shared_gate"]),
                        (sun[:, :], t["L1_ffn_shared_up"]),
                        (sdn[:, :], t["L1_ffn_shared_down"]),
                    ]:
                        eng.dma_start(dst, src).then_inc(ld_w, 16)

                @block.gpsimd
                def _(eng):
                    step = Chain(eng, gpsimd_steps)
                    step.straight()
                    eng.memset(projblk[:, :, :], 0.0)
                    step(eng.memset(lam_bd[:, :], 0.0))
                    eng.sem_inc(zeroed, 1)
                    eng.memset(ones[:, :], 1.0)
                    eng.memset(ones_bf[:, :], 1.0)
                    eng.memset(before[:, :], 1.0)
                    eng.memset(before_bf[:, :], 1.0)
                    eng.memset(dsel[:, :], 0.0)
                    eng.memset(blockmask[:, :], 0.0)
                    eng.memset(wop[:, :, :, :], 0.0)
                    eng.memset(whs[:, :, :], 0.0)
                    step(eng.memset(ident[:, :], 0.0))
                    step(eng.affine_select(out=before[:, :], in_=before[:, :], compare_op=ALU.is_gt, fill=0.0, base=0,
                                      pattern=[[1, P]], channel_multiplier=-1))
                    step(eng.affine_select(out=before_bf[:, :], in_=before_bf[:, :], compare_op=ALU.is_gt, fill=0.0, base=0,
                                      pattern=[[1, P]], channel_multiplier=-1))
                    for j in range(4):
                        step(eng.memset(blockmask[32 * j:32 * j + 32, 32 * j:32 * j + 32], 1.0))
                    step(eng.affine_select(out=dsel[:, :].rearrange("p (a b) -> p a b", a=4),
                                      in_=dsel[:, :].rearrange("p (a b) -> p a b", a=4),
                                      compare_op=ALU.not_equal, fill=1.0, base=-HD,
                                      pattern=[[-32, 4], [0, 32]], channel_multiplier=1))
                    step(eng.affine_select(out=ident[:, :], in_=ident[:, :], compare_op=ALU.not_equal, fill=1.0,
                                           base=0, pattern=[[-1, P]], channel_multiplier=1))
                    step.close()
                    eng.sem_inc(zeroed, 1)

                @block.scalar
                def _(eng):
                    eng.wait_ge(c_turned, 1)
                    eng.activation(scT[:, :], ps[:, 5, 0:2 * B], ACT.Silu).then_inc(mod_c, 1)
                    eng.wait_ge(wts_ps, 1)
                    for qk in range(2):
                        for g in range(2):
                            eng.activation(wf[:, qk, 4 * g:4 * g + 4, :].rearrange("p a f -> p (a f)"),
                                           bank(2 * qk + g), ACT.Copy)
                    eng.wait_ge(wts_ps, 2)
                    eng.activation(wv[:, :], ps[:, 4, 0:128], ACT.Copy)
                    eng.activation(gw0[:, :], ps[:, 5, 128:128 + E0], ACT.Copy)
                    eng.activation(gw1[:, :], ps[:, 5, 0:E1], ACT.Copy)
                    eng.activation(b1c[:, :], ps[:, 5, 64:64 + (E0 + 1) * FK], ACT.Copy)
                    eng.activation(sgT[:, :], ps[:, 6, 0:128], ACT.Copy)
                    eng.activation(suT[:, :], ps[:, 6, 128:256], ACT.Copy)
                    eng.activation(wtT[:, :], ps[0:PR, 5, 256:384], ACT.Copy)
                    for b in range(2):
                        last = eng.activation(CT[:, b, :], ps[0:PR, 5, 384:384 + PR], ACT.Copy)
                    last.then_inc(turned, 1)
                    eng.wait_ge(fold_ps, 1)
                    eng.activation(w_u[:, :], ps[:, 7, 0:PR], ACT.Copy).then_inc(turned, 1)

                @block.tensor
                def _(eng):
                    eng.wait_ge(ld_mod, 64)
                    eng.wait_ge(zeroed, 2)
                    eng.transpose(ps[:, 5, 0:2 * B], c_rows[:, :], ident[0:2 * B, 0:2 * B]).then_inc(c_turned, 1)
                    eng.wait_ge(mod_b, 1)
                    for lb in range(2 * B):
                        eng.matmul(bank(lb), scb[:, lb, :], wmod[:, lb // B, 2 * D:6 * D], start=True, stop=True)
                    for l in range(2):
                        for j in range(6):
                            k = (l * 6 + j) * B
                            last = eng.matmul(ps[:, 4, k:k + B], wmod[:, l, j * D:(j + 1) * D],
                                              scT[:, l * B:(l + 1) * B], start=True, stop=True)
                    last.then_inc(mod_ps, 1)
                    eng.wait_ge(mod_b, 2)
                    eng.wait_ge(ld_w, 16 * N_LOADS)
                    eng.wait_ge(zeroed, 2)
                    for qk in range(2):
                        for g in range(2):
                            last = eng.matmul(bank(2 * qk + g), wqkv[:, qk, :],
                                              projblk[:, 4 * g:4 * g + 4, :].rearrange("p a f -> p (a f)"),
                                              start=True, stop=True)
                    last.then_inc(wts_ps, 1)
                    eng.transpose(ps[:, 4, 0:128], wqkv[:, 2, :], ident[:, :])
                    eng.wait_ge(wt_done, 1)
                    for g in range(2):
                        eng.transpose(ps[:, 4, 128 + 128 * g:256 + 128 * g],
                                      wop[:, g, :, :].rearrange("p a c -> p (a c)"), ident[:, :])
                    eng.transpose(ps[:, 5, 128:128 + E0], g0n[:, :], ident[0:E0, 0:E0])
                    eng.transpose(ps[:, 5, 0:E1], g1n[:, :], ident[0:E1, 0:E1])
                    nb = (E0 + 1) * FK
                    eng.transpose(ps[:, 5, 64:64 + nb], b1n[:, :], ident[0:nb, 0:nb])
                    eng.transpose(ps[0:PR, 5, 256:384], wt[:, :], ident[:, :])
                    eng.transpose(ps[0:PR, 5, 384:384 + PR], Cm[:, :], ident[0:PR, 0:PR])
                    eng.transpose(ps[:, 6, 0:128], sgn[:, :], ident[:, :])
                    eng.transpose(ps[:, 6, 128:256], sun[:, :], ident[:, :])
                    eng.transpose(ps[:, 6, 256:384], sdn[:, :], ident[:, :]).then_inc(wts_ps, 1)
                    eng.wait_ge(turned, 1)
                    eng.matmul(ps[:, 7, 0:PR], wtT[:, :], Bm[:, :], start=True, stop=True)
                    eng.matmul(ps[:, 7, 128:256], wtT[:, :], fP[:, :], start=True, stop=True)
                    eng.matmul(ps[:, 7, 256:384], CT[:, :, :].rearrange("p b r -> p (b r)"), fP[:, :],
                               start=True, stop=True).then_inc(fold_ps, 1)

                @block.vector
                def _(eng):
                    step = Chain(eng, vector_steps)
                    step.straight()
                    eng.wait_ge(mod_c, 1)
                    eng.tensor_copy(scb[:, :, :], scT[:, :, None].to_broadcast([P, 2 * B, P])).then_inc(mod_b, 1)
                    eng.wait_ge(mod_ps, 1)
                    eng.tensor_copy(modT[:, :, :, :].rearrange("p l j b -> p (l j b)"), ps[:, 4, 0:12 * B])
                    for lb in range(2 * B):
                        r = bank(lb).rearrange("p (j d) -> p j d", j=4)
                        eng.tensor_copy(graw[:, lb, :, :], r[:, 0::3, :])
                        cs = slice((lb % B) * CPB, (lb % B + 1) * CPB)
                        eng.tensor_copy(schunk[:, lb // B, cs, 0, :], r[:, 1:2, :].to_broadcast([P, CPB, D]))
                        eng.tensor_scalar(schunk[:, lb // B, cs, 1, :], r[:, 2:3, :].to_broadcast([P, CPB, D]), 1.0, None,
                                          ALU.add)
                    step(eng.tensor_copy(moments[:, 0:1, 0], ps[:, 4, 0:1]))
                    eng.sem_inc(mod_b, 1)
                    for l in range(2):
                        for k, (j, add) in enumerate([(1, 1.0), (0, 0.0), (4, 1.0), (3, 0.0)]):
                            eng.tensor_scalar(shift[:, l, k, :].rearrange("p (b c) -> p b c", b=B),
                                              modT[:, l, j, :, None].to_broadcast([P, B, CPB]), add, None, ALU.add)
                    flat = graw[:, :, :, :].rearrange("p a b d -> p (a b d)")
                    gs = gsg[:, :, :, :].rearrange("p a b d -> p (a b d)")
                    gr = grow[:, :, :, :].rearrange("p a b d -> p (a b d)")
                    eng.tensor_scalar(gs, flat, 0.0, 2.0, ALU.is_ge, ALU.mult)
                    step(eng.scalar_tensor_tensor(gr, flat, -1.0, flat, ALU.mult, ALU.max))
                    step(eng.tensor_scalar(gr, gr, 0.25, None, ALU.max))
                    step(eng.scalar_tensor_tensor(gr, gs, -1.0, gr, ALU.add, ALU.mult))
                    for l in range(2):
                        for b in range(B):
                            eng.tensor_copy(gchunk[:, l, b * CPB:(b + 1) * CPB, :],
                                            grow[:, l * B + b, 1:2, :].to_broadcast([P, CPB, D]))
                    eng.wait_ge(ld_w, 16 * N_LOADS)
                    eng.wait_ge(zeroed, 2)
                    eng.tensor_copy(wop[:, :, :, 0:HD], wo_n[:, :].rearrange("p (g a c) -> p g a c", g=2, a=4))
                    step(eng.tensor_tensor(wUV[:, :, :], wU[:, :, :], wV[:, :, :], ALU.mult))
                    step(eng.tensor_reduce(wt[:, :], wUV[:, :, :], AX, ALU.add))
                    step(eng.tensor_tensor(wt[:, :], wt[:, :], toP[:, :], ALU.add))
                    eng.sem_inc(wt_done, 1)
                    eng.wait_ge(turned, 1)
                    for b in range(B):
                        cs = slice(b * CPB, (b + 1) * CPB)
                        for c in range(b * CPB, (b + 1) * CPB):
                            eng.tensor_tensor(wob[:, c, :, :], ps[:, 4, 128:384].rearrange("p (g d) -> p g d", g=2),
                                              grow[:, b, 0:1, :].to_broadcast([P, 2, D]), ALU.mult)
                        eng.tensor_tensor(bob[:, cs, :], bo_n[:, None, :].to_broadcast([1, CPB, D]),
                                          grow[0:1, b, 0:1, :].to_broadcast([1, CPB, D]), ALU.mult)
                        eng.tensor_tensor(sdg[:, cs, :], ps[:, 6, None, 256:384].to_broadcast([P, CPB, D]),
                                          grow[:, B + b, 1:2, :].to_broadcast([P, CPB, D]), ALU.mult)
                    eng.wait_ge(turned, 2)
                    for b in range(B):
                        rows = slice(b * PR, (b + 1) * PR)
                        eng.tensor_tensor(whx[:, b, :], ps[:, 7, 128:256], grow[:, B + b, 0, :], ALU.mult)
                        eng.tensor_tensor(whs[rows, b, :], ps[rows, 7, 256:384], grow[rows, B + b, 0, :], ALU.mult)
                    step.close()

        def token_moments(eng, step, c):
            eng.nop(nofuse=True)
            for k in range(4):
                last = eng.bn_stats(stats6[:, k, :], x_sb[:, ds(c * 4 + k, 1), :])
            step(last)
            eng.nop(nofuse=True)
            for k in range(4):
                last = eng.bn_aggr(mom4[:, k, :], stats6[:, k, :])
            step(last)
            eng.nop(nofuse=True)
            step(eng.tensor_copy(moments[:, ds(c * 4, 4), :], mom4[:, :, :]))

        def normalized(eng, dst, c):
            for k in range(4):
                last = eng.tensor_scalar(dst[:, k, :], x_sb[:, ds(c * 4 + k, 1), :], moments[:, ds(c * 4 + k, 1), 0:1],
                                         rstd[:, ds(c * 4 + k, 1)], ALU.subtract, ALU.mult)
            return last

        def rstd_block(n):
            with nc.Block() as block:
                @block.vector
                def _(eng):
                    eng.tensor_scalar(rstd[:, :], moments[:, :, 1], LN_EPS, None, ALU.add).then_inc(var_ready, 1)
                    eng.wait_ge(std_ready, n + 1)
                    eng.reciprocal(rstd[:, :], rstd[:, :])

                @block.scalar
                def _(eng):
                    eng.wait_ge(var_ready, n + 1)
                    eng.activation(rstd[:, :], rstd[:, :], ACT.Sqrt).then_inc(std_ready, 1)

        with nc.Block() as block:
            @block.vector
            def _(eng):
                step = Chain(eng, vector_steps)
                eng.wait_ge(ld_x, 64)
                with eng.Fori(0, NC) as c:
                    step.body(c, 3)
                    token_moments(eng, step, c)
                step.end(NC)
        rstd_block(0)

        with ExitStack() as tmp:
            def st(name, shape, dt=F32):
                return tmp.enter_context(nc.sbuf_tensor(name, shape, dt))

            xn = st("xn", [P, 2, 4, D])
            hT = st("hT", [P, 2, CHUNK])
            vp = st("vp", [P, 2, 4, H, 32])
            ex = st("ex", [P, 2, 2, CHUNK])
            qk = st("qk", [P, 2, 2, CHUNK])
            am = st("am", [P, 2, CHUNK])
            osb = st("osb", [P, 2, CHUNK])
            den = st("den", [P, CHUNK])
            on = st("on", [P, 2, CHUNK])

            xn_ready = sem("xn_ready")
            xnT_ready = sem("xnT_ready")
            hT_ready = sem("hT_ready")
            v_ps = sem("v_ps")
            v_ready = sem("v_ready")
            x_ready = sem("x_ready")
            e_ready = sem("e_ready")
            r_ready = sem("r_ready")
            feat_ready = sem("feat_ready")
            a_ready = sem("a_ready")
            am_ready = sem("am_ready")
            o_ready = sem("o_ready")
            osb_ready = sem("osb_ready")
            den_ps = sem("den_ps")
            den_sb = sem("den_sb")
            den_inv = sem("den_inv")
            on_ready = sem("on_ready")
            out_ps = sem("out_ps")
            x_added = sem("x_added")
            v_set = sem("v_set")

            def chunks(eng, body):
                body(0, 0, False, True)
                with eng.Fori(0, (NC - 2) // 2) as j:
                    body(j * 2 + 1, 1, True, True)
                    body(j * 2 + 2, 0, True, True)
                body(NC - 1, 1, True, False)

            with nc.Block() as block:
                @block.gpsimd
                def _(eng):
                    eng.sem_inc(on_ready, 1)
                    eng.memset(vp[:, :, :, :, HD + 1:32], 0.0)
                    eng.memset(vp[:, :, :, :, HD:HD + 1], 1.0).then_inc(v_set, 1)

                    def normalize(i, g):
                        n = i * 2 + g
                        eng.wait_ge(den_inv, n + 1)
                        eng.wait_ge(osb_ready, n + 1)
                        eng.wait_ge(out_ps, i + 1)
                        eng.tensor_tensor(on[:, g, :], osb[:, g, :], den[:, :], ALU.mult).then_inc(on_ready, 1)

                    def body(i, u, prev, nxt):
                        for h in range(H):
                            if prev and h == 1:
                                normalize(i - 1, 0)
                            if prev and h == 4:
                                normalize(i - 1, 1)

                    chunks(eng, body)
                    normalize(NC - 1, 0)
                    normalize(NC - 1, 1)

                @block.scalar
                def _(eng):
                    def turn(i, u):
                        eng.wait_ge(xnT_ready, i + 1)
                        eng.activation(hT[:, u, :], bank(0), ACT.Identity, bias=shift[:, 0, 1, ds(i, 1)],
                                       scale=shift[:, 0, 0, ds(i, 1)]).then_inc(hT_ready, 1)

                    def keep_v(i, u):
                        eng.wait_ge(v_ps, i + 1)
                        eng.activation(vp[:, u, :, :, 0:HD].rearrange("p t h c -> p (t h) c"),
                                       bank(0).rearrange("p (a c) -> p a c", c=HD), ACT.Copy).then_inc(v_ready, 1)

                    def keep_o(i, g):
                        eng.wait_ge(o_ready, i * 2 + g + 1)
                        eng.wait_ge(on_ready, i * 2 + 1)
                        eng.activation(osb[:, g, :], bank(1), ACT.Copy).then_inc(osb_ready, 1)

                    def denominator(i, g):
                        eng.wait_ge(den_ps, i * 2 + g + 1)
                        eng.wait_ge(on_ready, i * 2 + g + 1)
                        eng.activation(den[:, :], bank(0), ACT.Copy, bias=1e-8).then_inc(den_sb, 1)

                    def body(i, u, prev, nxt):
                        for h in range(H):
                            q = i * H + h
                            eng.wait_ge(x_ready, q + 1)
                            eng.wait_ge(feat_ready, q)
                            both = ex[:, h % 2, :, :].rearrange("p a n -> p (a n)")
                            eng.activation(both, ps[:, 2 + 2 * (h % 2):4 + 2 * (h % 2), :].rearrange("p a n -> p (a n)"),
                                           ACT.Relu, scale=-1.0).then_inc(r_ready, 1)
                            eng.wait_ge(r_ready, q + 1)
                            eng.activation(both, both, ACT.Exp, scale=-1.0).then_inc(e_ready, 1)
                            if prev and h == 0:
                                denominator(i - 1, 0)
                            if prev and h == 2:
                                keep_o(i - 1, 1)
                            if prev and h == 3:
                                denominator(i - 1, 1)
                            if h == 5:
                                keep_o(i, 0)
                            if nxt and h == 6:
                                turn(i + 1, 1 - u)
                            if nxt and h == 7:
                                keep_v(i + 1, 1 - u)

                    eng.wait_ge(v_set, 1)
                    turn(0, 0)
                    keep_v(0, 0)
                    chunks(eng, body)
                    denominator(NC - 1, 0)
                    keep_o(NC - 1, 1)
                    denominator(NC - 1, 1)

                @block.vector
                def _(eng):
                    step = Chain(eng, vector_steps)
                    eng.sem_inc(feat_ready, 1)

                    def normalize(i, u):
                        eng.wait_ge(xnT_ready, i)
                        normalized(eng, xn[:, u, :, :], i).then_inc(xn_ready, 1)

                    def inside_blocks(q, par):
                        eng.wait_ge(a_ready, q + 2)
                        eng.tensor_tensor(am[:, par, :].rearrange("p (t m) -> p t m", t=4),
                                          bank(6).rearrange("p (t m) -> p t m", t=4),
                                          blockmask[:, None, :].to_broadcast([P, 4, P]), ALU.mult).then_inc(am_ready, 1)

                    def invert(i, g):
                        eng.wait_ge(den_sb, i * 2 + g + 1)
                        eng.reciprocal(den[:, :], den[:, :]).then_inc(den_inv, 1)

                    def add(i):
                        eng.wait_ge(out_ps, i + 2)
                        xs = x_sb[:, ds(i * 4, 4), :]
                        eng.tensor_tensor(xs, xs, bank(0).rearrange("p (t d) -> p t d", t=4), ALU.add).then_inc(x_added, 1)
                        eng.wait_ge(x_added, i + 1)
                        step.body(i, 3)
                        token_moments(eng, step, i)

                    def body(i, u, prev, nxt):
                        for h in range(H):
                            q = i * H + h
                            eng.wait_ge(e_ready, q + 1)
                            eng.wait_ge(a_ready, q)
                            eng.scalar_tensor_tensor(
                                qk[:, h % 2, :, :].rearrange("p a n -> p (a n)"),
                                ps[:, 2 + 2 * (h % 2):4 + 2 * (h % 2), :].rearrange("p a n -> p (a n)"), 0.0,
                                ex[:, h % 2, :, :].rearrange("p a n -> p (a n)"),
                                ALU.max, ALU.add).then_inc(feat_ready, 1)
                            if h or prev:
                                inside_blocks(q - 1, (h - 1) % 2)
                            if prev and h == 1:
                                invert(i - 1, 0)
                            if prev and h == 4:
                                invert(i - 1, 1)
                            if nxt and h == 4:
                                normalize(i + 1, 1 - u)
                            if prev and h == 6:
                                add(i - 1)

                    normalize(0, 0)
                    chunks(eng, body)
                    inside_blocks(NC * H - 1, 1)
                    invert(NC - 1, 0)
                    invert(NC - 1, 1)
                    add(NC - 1)
                    step.end(NC)

                @block.tensor
                def _(eng):
                    eng.sem_inc(out_ps, 1)
                    eng.sem_inc(a_ready, 1)

                    def turn(i, u):
                        eng.wait_ge(xn_ready, i + 1)
                        for k in range(4):
                            last = eng.transpose(bank(0)[:, k * P:(k + 1) * P], xn[:, u, k, :], ident[:, :])
                        last.then_inc(xnT_ready, 1)

                    def values(i, u):
                        eng.wait_ge(hT_ready, i + 1)
                        for k in range(4):
                            last = eng.matmul(bank(0)[:, k * P:(k + 1) * P], hT[:, u, k * P:(k + 1) * P], wv[:, :],
                                              start=True, stop=True)
                        last.then_inc(v_ps, 1)

                    def features(i, u, h):
                        q = i * H + h
                        eng.wait_ge(feat_ready, q)
                        eng.matmul(bank(2 + 2 * (h % 2)), wf[:, 0, h, :], hT[:, u, :], start=True, stop=True)
                        eng.matmul(bank(3 + 2 * (h % 2)), wf[:, 1, h, :], hT[:, u, :], start=True,
                                   stop=True).then_inc(x_ready, 1)

                    def products(q, h):
                        eng.wait_ge(feat_ready, q + 2)
                        eng.wait_ge(am_ready, q)
                        for k in range(4):
                            c = slice(k * P, (k + 1) * P)
                            last = eng.matmul(bank(6)[:, c], qk[:, h % 2, 1, c], qk[:, h % 2, 0, c], start=True, stop=True)
                        last.then_inc(a_ready, 1)

                    def outputs(q, i, u, h):
                        eng.wait_ge(am_ready, q + 1)
                        if h % 4 == 0:
                            eng.wait_ge(osb_ready, i * 2 + h // 4)
                            eng.wait_ge(v_ready, i + 1)
                        a = h % 4
                        for k in range(4):
                            last = eng.matmul(ps[32 * a:32 * a + 32, 1, k * P:(k + 1) * P], vp[:, u, k, h, :],
                                              am[:, h % 2, k * P:(k + 1) * P], start=True, stop=True)
                        if a == 3:
                            last.then_inc(o_ready, 1)

                    def denominator(i, g):
                        eng.wait_ge(osb_ready, i * 2 + g + 1)
                        eng.matmul(bank(0), dsel[:, :], osb[:, g, :], start=True, stop=True).then_inc(den_ps, 1)

                    def project(i):
                        eng.wait_ge(on_ready, i * 2 + 3)
                        for k in range(4):
                            c = slice(k * P, (k + 1) * P)
                            for g in range(2):
                                eng.matmul(bank(0)[:, c], on[:, g, c], wob[:, ds(i, 1), g, :].rearrange("p a d -> p (a d)"),
                                           start=(g == 0), stop=False)
                            last = eng.matmul(bank(0)[:, c], ones[0:1, :], bob[:, ds(i, 1), :].rearrange("p a d -> p (a d)"),
                                              start=False, stop=True)
                        last.then_inc(out_ps, 1)

                    def body(i, u, prev, nxt):
                        for h in range(H):
                            q = i * H + h
                            features(i, u, h)
                            if h >= 1 or prev:
                                products(q - 1, (h - 1) % H)
                            if h >= 2:
                                outputs(q - 2, i, u, h - 2)
                            elif prev:
                                outputs(q - 2, i - 1, 1 - u, h + H - 2)
                            if prev and h == 0:
                                eng.wait_ge(v_ready, i + 1)
                                denominator(i - 1, 0)
                            if prev and h == 3:
                                eng.wait_ge(den_sb, i * 2 - 1)
                                denominator(i - 1, 1)
                            if prev and h == 5:
                                eng.wait_ge(den_sb, i * 2)
                                project(i - 1)
                            if nxt and h == 6:
                                if prev:
                                    eng.wait_ge(x_added, i)
                                turn(i + 1, 1 - u)
                            if nxt and h == 7:
                                values(i + 1, 1 - u)

                    turn(0, 0)
                    values(0, 0)
                    chunks(eng, body)
                    last_q = NC * H - 1
                    products(last_q, H - 1)
                    outputs(last_q - 1, NC - 1, 1, H - 2)
                    eng.wait_ge(x_added, NC - 1)
                    denominator(NC - 1, 0)
                    outputs(last_q, NC - 1, 1, H - 1)
                    eng.wait_ge(den_sb, NC * 2 - 1)
                    denominator(NC - 1, 1)
                    eng.wait_ge(den_sb, NC * 2)
                    project(NC - 1)
        rstd_block(1)

        with ExitStack() as tmp:
            def st(name, shape, dt=F32):
                return tmp.enter_context(nc.sbuf_tensor(name, shape, dt))

            CAP0 = 2 * T
            NE = E0 + 1
            h2T = st("h2T", [P, T])
            w1s = st("w1s", [P, NE, FF])
            w2s = st("w2s", [P, NE, FK, D])
            b2m = st("b2m", [P, NT // 2, D])
            bs2 = st("bs2", [P, D])
            gateT = st("gateT", [P, NT, E0])
            flag = st("flag", [P, 2 * P])
            emask = st("emask", [P, E0])
            crow = st("crow", [P, 1])
            HW0 = D + E0
            hx0 = nc.dram_tensor("hx0", (T + P, HW0), F32).ap()
            hx0_v = hx0[0:T, :].rearrange("(n p) c -> p n c", p=P)
            acc0 = [nc.dram_tensor(f"acc0_{a}", (T + P, D), F32).ap() for a in range(2)]
            hx0_stored = [sem(f"hx0_stored{u}") for u in range(2)]
            hx0_spare = sem("hx0_spare")
            acc0_zeroed = sem("acc0_zeroed")
            gflat = st("gflat", [P, 2 * P])
            ld_f = sem("ld_f")
            N_LDF = 5 + E0
            with ExitStack() as tmp2:
                def st2(name, shape, dt=F32):
                    return tmp2.enter_context(nc.sbuf_tensor(name, shape, dt))

                xn = st2("xn2", [P, 2, 4, D])
                rows = st2("rows0", [P, 2, 4, D])
                zt = st2("zt0", [P, HW0])
                pi = st2("pi", [P, 1], I32)
                h2c = st2("h2c", [P, 2, CHUNK])
                scores = st2("scores", [P, NT, E0])
                smax = st2("smax", [P, NT])
                ssum = st2("ssum", [P, NT])
                sperm = st2("sperm", [P, 2, E0, NT // 2])
                sflat = st2("sflat", [P, 2 * P])
                above = st2("above", [P, 2 * P])
                equal = st2("equal", [P, 2 * P])
                rank = st2("rank", [P, 2 * P])
                b2r = st2("b2r", [P, D])
                cm3 = st2("cm3", [P, E0, NT // 2])
                cmask = st2("cmask", [P, NT // 2])
                cur = st2("cur", [P, 1], I32)
                cand = st2("cand", [P, 1], I32)
                bit = st2("bit", [P, 1], I32)
                bitf = st2("bitf", [P, 1])
                inc = st2("inc", [P, 1], I32)
                cnt = st2("cnt", [P, 1])
                n_above = st2("n_above", [P, 1])
                n_equal = st2("n_equal", [P, 1])
                need = st2("need", [P, 1])

                bxn_ready = sem("bxn_ready")
                zt0_ready = sem("zt0_ready")
                b_part = sem("b_part")
                rows_ready = sem("rows_ready")
                bxnT_ready = sem("bxnT_ready")
                bh_ready = sem("bh_ready")
                bh_kept = sem("bh_kept")
                lg_ps = sem("lg_ps")
                lg_sb = sem("lg_sb")
                cm_ready = sem("cm_ready")
                with nc.Block() as block:
                    @block.sync
                    def _(eng):
                        for u in range(2):
                            eng.sem_inc(hx0_stored[u], 16)
                        eng.dma_start(w1s[:, 0:E0, :], t["L0_ffn_W1"].rearrange("e d f -> d e f")).then_inc(ld_f, 16)
                        eng.dma_start(w1s[:, E0, :], t["L0_ffn_Ws1"]).then_inc(ld_f, 16)
                        eng.dma_start(w2s[:, 0:E0, :, :],
                                      t["L0_ffn_W2"].rearrange("e (k p) d -> p e k d", p=P)).then_inc(ld_f, 16)
                        eng.dma_start(w2s[:, E0, :, :],
                                      t["L0_ffn_Ws2"].rearrange("(k p) d -> p k d", p=P)).then_inc(ld_f, 16)
                        eng.dma_start(bs2[:, :], t["L0_ffn_bs2"][None, :].to_broadcast([P, D])).then_inc(ld_f, 16)
                        n = P // E0
                        for e in range(E0):
                            eng.dma_start(b2r[e * n:(e + 1) * n, :],
                                          t["L0_ffn_b2"][e:e + 1, :].to_broadcast([n, D])).then_inc(ld_f, 16)
                        eng.wait_ge(zt0_ready, 1)
                        for a in range(2):
                            eng.dma_start(acc0[a].rearrange("(n p) d -> p n d", p=P),
                                          zt[:, None, 0:D].to_broadcast([P, NT + 1, D])).then_inc(acc0_zeroed, 16)
                        eng.dma_start(hx0[T:T + P, :], zt[:, :]).then_inc(hx0_spare, 16)
                        with eng.Fori(0, NC // 2) as j:
                            for u in range(2):
                                i = j * 2 + u
                                eng.wait_ge(rows_ready, i + 3)
                                eng.dma_start(hx0_v[:, ds(i * 4, 4), 0:D], rows[:, u, :, :]).then_inc(hx0_stored[u], 16)
                        for u in range(2):
                            eng.wait_ge(hx0_stored[u], 16 * (NC // 2) + 16)
                        eng.wait_ge(acc0_zeroed, 32)
                        eng.wait_ge(hx0_spare, 16)

                    @block.gpsimd
                    def _(eng):
                        eng.sem_inc(bh_kept, 1)
                        eng.sem_inc(rows_ready, 2)
                        step = Chain(eng, gpsimd_steps)
                        step.straight()
                        eng.memset(zt[:, :], 0.0).then_inc(zt0_ready, 1)
                        eng.iota(pi[:, :], pattern=[[1, 1]], base=0, channel_multiplier=1)
                        step(eng.memset(cm3[:, :, :], 0.0))
                        eng.affine_select(out=cm3[:, :, :], in_=cm3[:, :, :], compare_op=ALU.not_equal, fill=1.0, base=0,
                                          pattern=[[-NT // 2, E0], [-1, NT // 2]], channel_multiplier=1).then_inc(cm_ready, 1)
                        step.close()
                        with eng.Fori(0, NC // 2) as j:
                            for u in range(2):
                                i = j * 2 + u
                                eng.wait_ge(bxn_ready, i + 1)
                                eng.wait_ge(hx0_stored[u], 16 * j + 16)
                                r = rows[:, u, :, :]
                                eng.tensor_tensor(r, xn[:, u, :, :], schunk[:, 0, ds(i, 1), 1, :].to_broadcast([P, 4, D]),
                                                  ALU.mult).then_inc(b_part, 1)
                                eng.wait_ge(b_part, i + 1)
                                eng.tensor_tensor(r, r, schunk[:, 0, ds(i, 1), 0, :].to_broadcast([P, 4, D]),
                                                  ALU.add).then_inc(rows_ready, 1)
                                eng.wait_ge(bh_ready, i + 1)
                                eng.tensor_copy(h2T[:, ds(i * CHUNK, CHUNK)], h2c[:, u, :]).then_inc(bh_kept, 1)

                    @block.vector
                    def _(eng):
                        with eng.Fori(0, NC // 2) as j:
                            for u in range(2):
                                i = j * 2 + u
                                eng.wait_ge(bxnT_ready, i + 1)
                                eng.wait_ge(rows_ready, i + 1)
                                normalized(eng, xn[:, u, :, :], i).then_inc(bxn_ready, 1)

                    @block.tensor
                    def _(eng):
                        eng.sem_inc(lg_ps, 1)
                        eng.sem_inc(bxnT_ready, 2)
                        with eng.Fori(0, NC // 2) as j:
                            for u in range(2):
                                i = j * 2 + u
                                eng.wait_ge(bxn_ready, i + 1)
                                for k in range(4):
                                    last = eng.transpose(bank(u)[:, k * P:(k + 1) * P], xn[:, u, k, :], ident[:, :])
                                last.then_inc(bxnT_ready, 1)
                                eng.wait_ge(bh_ready, i + 1)
                                eng.wait_ge(lg_sb, i + 1)
                                for k in range(4):
                                    last = eng.matmul(ps[:, 2 + u, k * E0:(k + 1) * E0], h2c[:, u, k * P:(k + 1) * P],
                                                      gw0[:, :], start=True, stop=True)
                                last.then_inc(lg_ps, 1)

                    @block.scalar
                    def _(eng):
                        eng.sem_inc(lg_sb, 1)
                        with eng.Fori(0, NC // 2) as j:
                            for u in range(2):
                                i = j * 2 + u
                                eng.wait_ge(bxnT_ready, i + 3)
                                eng.wait_ge(lg_ps, i + 1)
                                eng.wait_ge(bh_kept, i + 1)
                                eng.activation(h2c[:, u, :], bank(u), ACT.Identity, bias=shift[:, 0, 3, ds(i, 1)],
                                               scale=shift[:, 0, 2, ds(i, 1)]).then_inc(bh_ready, 1)
                                eng.wait_ge(lg_ps, i + 2)
                                eng.activation(scores[:, ds(i * 4, 4), :],
                                               ps[:, 2 + u, 0:4 * E0].rearrange("p (k e) -> p k e", k=4),
                                               ACT.Copy).then_inc(lg_sb, 1)

                ex_ready = sem("ex_ready")
                shifted = sem("shifted")
                perm_ready = sem("perm_ready")
                flat_ps = sem("flat_ps")
                cnt_ready = sem("cnt_ready")
                cnt_ps = sem("cnt_ps")
                gate_ready = sem("gate_ready")
                gate_ps = sem("gate_ps")
                BITS = 30
                with nc.Block() as block:
                    @block.scalar
                    def _(eng):
                        eng.wait_ge(shifted, 1)
                        eng.activation(scores[:, :, :], scores[:, :, :], ACT.Exp).then_inc(ex_ready, 1)

                    @block.vector
                    def _(eng):
                        step = Chain(eng, vector_steps)
                        step.straight()
                        step(eng.tensor_reduce(smax[:, :], scores[:, :, :], AX, ALU.max))
                        eng.tensor_tensor(scores[:, :, :], scores[:, :, :],
                                          smax[:, :, None].to_broadcast([P, NT, E0]), ALU.subtract).then_inc(shifted, 1)
                        eng.wait_ge(ex_ready, 1)
                        step(eng.tensor_reduce(ssum[:, :], scores[:, :, :], AX, ALU.add))
                        step(eng.reciprocal(ssum[:, :], ssum[:, :]))
                        for j in range(2):
                            last = eng.tensor_tensor(
                                sperm[:, j, :, :].rearrange("p e c -> p c e"),
                                scores[:, :, :].rearrange("p (c j) e -> p j c e", j=2)[:, j, :, :],
                                ssum[:, :].rearrange("p (c j) -> p j c", j=2)[:, j, :, None].to_broadcast([P, NT // 2, E0]),
                                ALU.mult)
                        last.then_inc(perm_ready, 1)
                        eng.memset(cur[:, :], 0)
                        eng.memset(bit[:, :], 1 << (BITS - 1))
                        eng.memset(cand[:, :], 1 << (BITS - 1))
                        step(eng.memset(bitf[:, :], float(1 << (BITS - 1))))
                        eng.wait_ge(flat_ps, 1)
                        step(eng.tensor_copy(sflat[:, :], ps[:, 0, 0:2 * P]))
                        step.close()
                        with eng.Fori(0, BITS) as k:
                            step.body(k, 5)
                            eng.tensor_scalar(above[:, :], sflat[:, :], cand[:, :].bitcast(F32), 0.0, ALU.is_ge, ALU.add,
                                              accum_out=cnt[:, :]).then_inc(cnt_ready, 1)
                            step(eng.tensor_scalar(bit[:, :], bit[:, :], 1, None, ALU.logical_shift_right))
                            eng.wait_ge(cnt_ps, k + 1)
                            step(eng.tensor_scalar(inc[:, :], ps[:, 1, 0:1], float(CAP0), bitf[:, :], ALU.is_ge, ALU.mult))
                            step(eng.tensor_tensor(cur[:, :], cur[:, :], inc[:, :], ALU.bitwise_or))
                            step(eng.tensor_tensor(cand[:, :], cur[:, :], bit[:, :], ALU.bitwise_or))
                            step(eng.tensor_scalar(bitf[:, :], bitf[:, :], 0.5, None, ALU.mult))
                        step.end(BITS)
                        step.straight()
                        thr = cur[:, :].bitcast(F32)
                        eng.tensor_scalar(above[:, :], sflat[:, :], thr, 0.0, ALU.is_gt, ALU.add, accum_out=n_above[:, :])
                        step(eng.tensor_scalar(equal[:, :], sflat[:, :], thr, 0.0, ALU.is_equal, ALU.add,
                                               accum_out=n_equal[:, :]))
                        eng.sem_inc(cnt_ready, 1)
                        step(eng.tensor_tensor_scan(rank[:, :], ones[:, 0:1].to_broadcast([P, 2 * P]), equal[:, :], 0.0,
                                                    ALU.mult, ALU.add))
                        eng.wait_ge(cnt_ps, BITS + 1)
                        step(eng.tensor_scalar(need[:, :], ps[:, 1, 0:1], -1.0, float(CAP0), ALU.mult, ALU.add))
                        step(eng.tensor_tensor(need[:, :], need[:, :], ps[:, 1, 1:2], ALU.subtract))
                        step(eng.scalar_tensor_tensor(rank[:, :], rank[:, :], need[:, :], equal[:, :], ALU.is_le, ALU.mult))
                        step(eng.tensor_tensor(flag[:, :], above[:, :], rank[:, :], ALU.add))
                        eng.tensor_tensor(gflat[:, :], flag[:, :], sflat[:, :], ALU.mult).then_inc(gate_ready, 1)
                        eng.wait_ge(cm_ready, 1)
                        eng.wait_ge(ld_f, 16 * N_LDF)
                        step(eng.tensor_reduce(cmask[:, :], cm3[:, :, :].rearrange("p e c -> p c e"), AX, ALU.add))
                        step(eng.tensor_tensor(b2m[:, :, :], b2r[:, None, :].to_broadcast([P, NT // 2, D]),
                                               cmask[:, :, None].to_broadcast([P, NT // 2, D]), ALU.mult))
                        step(eng.tensor_reduce(emask[:, :], cm3[:, :, :], AX, ALU.add))
                        step(eng.tensor_scalar(pi[:, :], pi[:, :], NT // 2 - 1, None, ALU.bitwise_and))
                        step(eng.tensor_copy(crow[:, :], pi[:, :]))
                        eng.wait_ge(gate_ps, 1)
                        for j in range(2):
                            eng.tensor_copy(gateT[:, :, :].rearrange("p (c j) e -> p e c j", j=2)[:, :, :, j],
                                            ps[:, 0, j * P:(j + 1) * P].rearrange("p (e c) -> p e c", e=E0))
                        step.close()

                    @block.tensor
                    def _(eng):
                        eng.wait_ge(perm_ready, 1)
                        for j in range(2):
                            last = eng.transpose(ps[:, 0, j * P:(j + 1) * P],
                                                 sperm[:, j, :, :].rearrange("p e c -> p (e c)"), ident[:, :])
                        last.then_inc(flat_ps, 1)
                        with eng.Fori(0, BITS) as k:
                            eng.wait_ge(cnt_ready, k + 1)
                            eng.matmul(ps[:, 1, 0:1], ones[:, :], cnt[:, :], start=True, stop=True).then_inc(cnt_ps, 1)
                        eng.wait_ge(cnt_ready, BITS + 1)
                        eng.matmul(ps[:, 1, 0:1], ones[:, :], n_above[:, :], start=True, stop=True)
                        eng.matmul(ps[:, 1, 1:2], before[:, :], n_equal[:, :], start=True, stop=True).then_inc(cnt_ps, 1)
                        eng.wait_ge(gate_ready, 1)
                        for j in range(2):
                            last = eng.transpose(ps[:, 0, j * P:(j + 1) * P], gflat[:, j * P:(j + 1) * P], ident[:, :])
                        last.then_inc(gate_ps, 1)

            TS = 256
            NTL = CAP0 // TS + E0
            NG0 = NTL * TS // P
            NBL = NTL * TS // CHUNK
            W = 4 + E0
            idx0 = st("idx0", [P, NG0], I32)
            info = st("info", [P, NG0, W])
            tile_e = st("tile_e", [P, NTL], I32)
            hx0_gates = sem("hx0_gates")
            with ExitStack() as tmp2:
                def st2(name, shape, dt=F32):
                    return tmp2.enter_context(nc.sbuf_tensor(name, shape, dt))

                hid = st2("hid_s", [P, 2, FK, CHUNK])
                facc = st2("facc", [P, 4, D])
                incl = st2("incl", [P, 2 * P], BF16)
                tot = st2("tot", [P, 1])
                tot_e = st2("tot_e", [P, E0])
                cnt_e = st2("cnt_e", [P, E0])
                tiles_i = st2("tiles_i", [P, E0], I32)
                tiles = st2("tiles", [P, E0])
                tiles_end = st2("tiles_end", [P, E0])
                cnt_end = st2("cnt_end", [P, E0])
                base = st2("base", [P, E0])
                row_start = st2("row_start", [P, 1])
                row_end = st2("row_end", [P, 1])
                rs_i = st2("rs_i", [P, 3], I32)
                blk_start = st2("blk_start", [P, NBL])
                blk_end = st2("blk_end", [P, NBL])
                pay = st2("pay0", [P, W], BF16)
                io_i = st2("io_i0", [P, CHUNK], I32)
                io512 = st2("io512", [P, CHUNK])
                bo_i = st2("bo_i", [P, NBL], I32)
                blk = st2("blk", [P, NBL])
                so_i = st2("so_i", [P, NG0 + 1], I32)
                slot = st2("slot", [P, NG0 + 1])
                inside = st2("inside", [P, 2, CHUNK])
                oh = st2("oh0", [P, NBL, CHUNK], BF16)
                past = st2("past", [P, NTL, E0])
                tile_f = st2("tile_f", [P, NTL])
                place = st2("place", [P, NG0])
                scr = st2("scr", [P, 2, 2 * P])
                fi = st2("fi", [P, NG0])

                io_ready = sem("io_ready")
                tot_ready = sem("tot_ready")
                tot_ps = sem("tot_ps")
                oh_ready = sem("oh0_ready")
                info_ps = sem("info_ps")
                info_ready = sem("info_ready")
                incl_ps = sem("incl_ps")
                incl_used = sem("incl_used")
                sh1_ps = sem("sh1_ps")
                shid_ready = sem("shid_ready")
                sy_ps = sem("sy_ps")
                sy_used = sem("sy_used")
                GPC = NG0 // 2 // (NC // 2)
                with nc.Block() as block:
                    @block.sync
                    def _(eng):
                        eng.dma_start(hx0_v[:, :, D:HW0], gateT[:, :, :]).then_inc(hx0_gates, 16)

                    @block.gpsimd
                    def _(eng):
                        step = Chain(eng, gpsimd_steps)
                        step.straight()
                        eng.iota(io_i[:, :], pattern=[[1, CHUNK]], base=0, channel_multiplier=0)
                        eng.iota(bo_i[:, :], pattern=[[CHUNK, NBL]], base=0, channel_multiplier=0)
                        step(eng.iota(so_i[:, 0:NG0], pattern=[[P, NG0]], base=0, channel_multiplier=1))
                        eng.tensor_copy(io512[:, :], io_i[:, :])
                        eng.tensor_copy(blk[:, :], bo_i[:, :])
                        step(eng.tensor_copy(slot[:, 0:NG0], so_i[:, 0:NG0]))
                        step.close()
                        eng.sem_inc(io_ready, 1)

                    @block.tensor
                    def _(eng):
                        def up(i):
                            for k in range(FK):
                                if i:
                                    eng.wait_ge(shid_ready, (i - 1) * FK + k + 1)
                                eng.matmul(bank(k), w1s[:, E0, k * P:(k + 1) * P], h2T[:, i * CHUNK:(i + 1) * CHUNK],
                                           start=True, stop=True).then_inc(sh1_ps, 1)

                        def down(i):
                            eng.wait_ge(shid_ready, (i + 1) * FK)
                            if i >= 2:
                                eng.wait_ge(sy_used, i - 1)
                            for c in range(4):
                                cols = bank(4 + i % 2)[:, c * P:(c + 1) * P]
                                for k in range(FK):
                                    eng.matmul(cols, hid[:, i % 2, k, c * P:(c + 1) * P], w2s[:, E0, k, :],
                                               start=(k == 0), stop=False)
                                last = eng.matmul(cols, gflat[:, (c % 2) * P:(c % 2 + 1) * P], b2m[:, 2 * i + c // 2, :],
                                                  start=False, stop=True)
                            last.then_inc(sy_ps, 1)

                        eng.wait_ge(tot_ready, 1)
                        eng.matmul(ps[:, 7, 0:E0], ones[:, :], tot_e[:, :], start=True, stop=True)
                        eng.matmul(ps[:, 7, E0:E0 + 1], before[:, :], tot[:, :], start=True, stop=True).then_inc(tot_ps, 1)
                        up(0)
                        for i in range(NC):
                            if i + 1 < NC:
                                up(i + 1)
                            down(i)
                            if i == NC // 2 - 1:
                                eng.wait_ge(oh_ready, 1)
                                for g in range(NG0):
                                    b, c = divmod(g, NG0 // 2)
                                    last = eng.matmul(ps[:, 6 + b, c * W:(c + 1) * W],
                                                      oh[:, g // 4, (g % 4) * P:(g % 4 + 1) * P], pay[:, :],
                                                      start=True, stop=True)
                                last.then_inc(info_ps, 1)
                            if i >= NC // 2 - 1 and i < NC - 1:
                                n0 = (i - NC // 2 + 1) * GPC
                                for n in range(n0, n0 + GPC if i < NC - 2 else NG0 // 2):
                                    if n < 2:
                                        eng.wait_ge(info_ready, 1)
                                    else:
                                        eng.wait_ge(incl_used, n - 1)
                                    for a in range(2):
                                        g = 2 * n + a
                                        last = eng.matmul(bank(6 + n % 2)[:, a * 256:(a + 1) * 256],
                                                          oh[:, g // 4, (g % 4) * P:(g % 4 + 1) * P], incl[:, :],
                                                          start=True, stop=True)
                                    last.then_inc(incl_ps, 1)

                    @block.scalar
                    def _(eng):
                        for i in range(NC):
                            for k in range(FK):
                                eng.wait_ge(sh1_ps, i * FK + k + 1)
                                if k == 0 and i >= 2:
                                    eng.wait_ge(sy_ps, i - 1)
                                col = E0 * FK + k
                                eng.activation(hid[:, i % 2, k, :], bank(k), ACT.Gelu_apprx_tanh,
                                               bias=b1c[:, col:col + 1]).then_inc(shid_ready, 1)

                    @block.vector
                    def _(eng):
                        step = Chain(eng, vector_steps)
                        step.straight()
                        eng.wait_ge(io_ready, 1)
                        step(eng.tensor_tensor_scan(incl[:, :], ones[:, 0:1].to_broadcast([P, 2 * P]), flag[:, :], 0.0,
                                                    ALU.mult, ALU.add))
                        step(eng.tensor_copy(tot[:, :], incl[:, 2 * P - 1:2 * P]))
                        step(eng.tensor_scalar(tot_e[:, :], emask[:, :], tot[:, :], None, ALU.mult))
                        eng.sem_inc(tot_ready, 1)
                        eng.wait_ge(tot_ps, 1)
                        step(eng.tensor_copy(cnt_e[:, :], ps[:, 7, 0:E0]))
                        step(eng.tensor_scalar(tiles_i[:, :], cnt_e[:, :], float(TS - 1), None, ALU.add))
                        step(eng.tensor_scalar(tiles_i[:, :], tiles_i[:, :], 8, None, ALU.logical_shift_right))
                        step(eng.tensor_copy(tiles[:, :], tiles_i[:, :]))
                        one8 = ones[:, 0:1].to_broadcast([P, E0])
                        eng.tensor_tensor_scan(tiles_end[:, :], one8, tiles[:, :], 0.0, ALU.mult, ALU.add)
                        step(eng.tensor_tensor_scan(cnt_end[:, :], one8, cnt_e[:, :], 0.0, ALU.mult, ALU.add))
                        eng.tensor_tensor(base[:, :], tiles_end[:, :], tiles[:, :], ALU.subtract)
                        step(eng.tensor_tensor(cnt_end[:, :], cnt_end[:, :], cnt_e[:, :], ALU.subtract))
                        step(eng.scalar_tensor_tensor(base[:, :], base[:, :], float(TS), cnt_end[:, :],
                                                      ALU.mult, ALU.subtract))
                        step(eng.tensor_tensor(base[:, :], base[:, :], emask[:, :], ALU.mult))
                        step(eng.tensor_reduce(row_start[:, :], base[:, :], AX, ALU.add))
                        step(eng.tensor_tensor(row_start[:, :], row_start[:, :], ps[:, 7, E0:E0 + 1], ALU.add))
                        step(eng.tensor_tensor(row_end[:, :], row_start[:, :], tot[:, :], ALU.add))
                        step(eng.tensor_copy(rs_i[:, 0:1], row_start[:, :]))
                        eng.tensor_scalar(rs_i[:, 1:2], rs_i[:, 0:1], 8, None, ALU.logical_shift_right)
                        step(eng.tensor_scalar(rs_i[:, 2:3], rs_i[:, 0:1], 255, None, ALU.bitwise_and))
                        eng.tensor_copy(pay[:, 0:1], crow[:, :])
                        eng.tensor_copy(pay[:, 1:3], rs_i[:, 1:3])
                        eng.tensor_copy(pay[:, 3:4], ones[:, 0:1])
                        eng.tensor_copy(pay[:, 4:W], emask[:, :])
                        eng.tensor_scalar(blk_start[:, :], blk[:, :], -1.0, row_start[:, :], ALU.mult, ALU.add)
                        step(eng.tensor_scalar(blk_end[:, :], blk[:, :], -1.0, row_end[:, :], ALU.mult, ALU.add))
                        step(eng.tensor_tensor(past[:, :, :], io512[:, 0:NTL, None].to_broadcast([P, NTL, E0]),
                                               tiles_end[:, None, :].to_broadcast([P, NTL, E0]), ALU.is_ge))
                        step(eng.tensor_reduce(tile_f[:, :], past[:, :, :], AX, ALU.add))
                        step(eng.tensor_scalar(tile_e[:, :], tile_f[:, :], float(E0 - 1), None, ALU.min))

                        def add_shared(i):
                            eng.wait_ge(sy_ps, i + 1)
                            fa = facc[:, :, :]
                            step(eng.tensor_tensor(fa, bank(4 + i % 2).rearrange("p (k d) -> p k d", k=4),
                                                   bs2[:, None, :].to_broadcast([P, 4, D]), ALU.add))
                            eng.sem_inc(sy_used, 1)
                            step(eng.tensor_tensor(fa, fa, gchunk[:, 0, i:i + 1, :].to_broadcast([P, 4, D]), ALU.mult))
                            xs = x_sb[:, i * 4:i * 4 + 4, :]
                            step(eng.tensor_tensor(xs, xs, fa, ALU.add))

                        for i in range(NC // 2):
                            for b in range(i * NBL // (NC // 2), (i + 1) * NBL // (NC // 2)):
                                step(eng.tensor_scalar(inside[:, b % 2, :], io512[:, :], blk_start[:, b:b + 1], None, ALU.is_ge))
                                last = eng.scalar_tensor_tensor(oh[:, b, :], io512[:, :], blk_end[:, b:b + 1],
                                                                inside[:, b % 2, :],
                                                                ALU.is_lt, ALU.mult)
                            step(last)
                            if i == NC // 2 - 1:
                                eng.sem_inc(oh_ready, 1)
                            if i < NC // 2 - 1:
                                add_shared(i)
                        add_shared(NC // 2 - 1)
                        eng.wait_ge(info_ps, 1)
                        for b in range(2):
                            last = eng.tensor_copy(info[:, b * (NG0 // 2):(b + 1) * (NG0 // 2), :].rearrange("p g w -> p (g w)"),
                                                   ps[:, 6 + b, 0:NG0 // 2 * W])
                        step(last)
                        eng.sem_inc(info_ready, 1)
                        step(eng.scalar_tensor_tensor(place[:, :], info[:, :, 1], -256.0, slot[:, 0:NG0], ALU.mult, ALU.add))
                        step(eng.tensor_tensor(place[:, :], place[:, :], info[:, :, 2], ALU.subtract))

                        def look_up(n):
                            eng.wait_ge(incl_ps, n + 1)
                            for a in range(2):
                                g = 2 * n + a
                                last = eng.tensor_scalar(scr[:, a, :], bank(6 + n % 2)[:, a * 256:(a + 1) * 256],
                                                         place[:, g:g + 1], 0.0, ALU.is_le, ALU.add,
                                                         accum_out=fi[:, g:g + 1])
                            step(last)
                            eng.sem_inc(incl_used, 1)

                        for i in range(NC // 2, NC - 1):
                            n0 = (i - NC // 2) * GPC
                            for n in range(n0, n0 + GPC):
                                look_up(n)
                            add_shared(i)
                        for n in range((NC // 2 - 1) * GPC, NG0 // 2):
                            look_up(n)
                        add_shared(NC - 1)
                        step(eng.scalar_tensor_tensor(fi[:, :], info[:, :, 0], 256.0, fi[:, :], ALU.mult, ALU.add))
                        step(eng.tensor_scalar(row_end[:, :], slot[:, 0:1], float(T - 256), None, ALU.add))
                        step(eng.tensor_scalar(place[:, :], info[:, :, 3], -1.0, 1.0, ALU.mult, ALU.add))
                        step(eng.tensor_scalar(place[:, :], place[:, :], row_end[:, :], None, ALU.mult))
                        step(eng.tensor_tensor(idx0[:, :], fi[:, :], place[:, :], ALU.add))
                        step.close()

            with ExitStack() as tmp2:
                def st2(name, shape, dt=F32):
                    return tmp2.enter_context(nc.sbuf_tensor(name, shape, dt))

                KT = TS // P
                ixg = st2("ixg", [P, 4, KT], I32)
                ixa = st2("ixa", [P, 4, KT], I32)
                cell = st2("cell", [P, 4], I32)
                gath = st2("gath0", [P, 4, KT, HW0])
                gT = st2("gT0", [P, 2, TS])
                w1t = st2("w1t", [P, 2, FF])
                b1t = st2("b1t", [P, 2, FK])
                hid = st2("hid_e", [P, 2, FK, TS])
                gm = st2("gm", [P, 2, KT, E0])
                gv = st2("gv", [P, 2, KT])
                ysc = st2("ysc0", [P, 2, KT, D])
                f_ix = sem("f_ix")
                f_gathered = [sem(f"f_gathered{s}") for s in range(4)]
                ft_ps = sem("ft_ps")
                fT_ready = sem("fT_ready")
                fw_cell = sem("fw_cell")
                fw_ready = sem("fw_ready")
                fu_ps = sem("fu_ps")
                fh_ready = sem("fh_ready")
                fy_ps = sem("fy_ps")
                fg_part = sem("fg_part")
                f_gated = sem("f_gated")
                fs_ready = sem("fs_ready")
                f_added = [sem(f"f_added{a}") for a in range(KT)]

                def early(n, k):
                    return type(n) is int and n < k

                def tile_rounds(eng, body):
                    for s in range(4):
                        body(s, s)
                    with eng.Fori(1, NTL // 4 - 1) as j:
                        for s in range(4):
                            body(j * 4 + s, s)
                    for s in range(4):
                        body(NTL - 4 + s, s)

                def late(n, k):
                    return type(n) is int and n + k >= NTL

                with nc.Block() as block:
                    @block.gpsimd
                    def _(eng):
                        def gather(n, s):
                            if not early(n, 4):
                                eng.wait_ge(ft_ps, n - 3)
                                eng.wait_ge(f_gated, n - 3)
                            eng.tensor_copy(ixg[:, s, :], idx0[:, ds(n * KT, KT)]).then_inc(f_ix, 1)

                        def fetch(n, s, count):
                            eng.wait_ge(f_ix, count)
                            eng.nop(nofuse=True)
                            for k in range(KT):
                                eng.indirect_dma_start(out=gath[:, s, k, :], out_offset=None, in_=hx0,
                                                       in_offset=bass.IndirectOffsetOnAxis(ap=ixg[:, s, k:k + 1], axis=0)
                                                       ).then_inc(f_gathered[s], 16)

                        def scatter(n, s, count):
                            eng.tensor_copy(ixa[:, s, :], idx0[:, ds(n * KT, KT)]).then_inc(f_ix, 1)
                            eng.wait_ge(f_ix, count)
                            eng.wait_ge(fs_ready, n + 1)
                            for k in range(KT):
                                if not early(n, 1):
                                    eng.wait_ge(f_added[k], n * 16)
                                eng.nop(nofuse=True)
                                eng.indirect_dma_start(out=acc0[k],
                                                       out_offset=bass.IndirectOffsetOnAxis(ap=ixa[:, s, k:k + 1], axis=0),
                                                       in_=ysc[:, s % 2, k, :], in_offset=None,
                                                       compute_op=ALU.add).then_inc(f_added[k], 16)

                        def body(n, s):
                            if not late(n, 3):
                                gather(n + 3, (s + 3) % 4)
                                fetch(n + 3, (s + 3) % 4, n * 2 + 4)
                                scatter(n, s, n * 2 + 5)
                            else:
                                scatter(n, s, n + NTL + 1)

                        eng.wait_ge(hx0_gates, 16)
                        for n in range(3):
                            gather(n, n)
                            fetch(n, n, n + 1)
                        tile_rounds(eng, body)

                    @block.tensor
                    def _(eng):
                        def turn(n, s):
                            eng.wait_ge(f_gathered[s], (n - s) * (KT * 4) + KT * 16)
                            if not early(n, 1):
                                eng.wait_ge(fT_ready, n)
                            for k in range(KT):
                                last = eng.transpose(bank(0)[:, k * P:(k + 1) * P], gath[:, s, k, 0:D], ident[:, :])
                            last.then_inc(ft_ps, 1)

                        def up(n, s):
                            eng.wait_ge(fT_ready, n + 1)
                            eng.wait_ge(fw_ready, n + 1)
                            for k in range(FK):
                                if not early(n, 1):
                                    eng.wait_ge(fh_ready, n * FK - (FK - 1 - k))
                                eng.matmul(ps[:, 1 + k, 0:TS], w1t[:, s % 2, k * P:(k + 1) * P], gT[:, s % 2, :],
                                           start=True, stop=True).then_inc(fu_ps, 1)

                        def down(n, s):
                            eng.wait_ge(fh_ready, (n + 1) * FK)
                            if not early(n, 2):
                                eng.wait_ge(fs_ready, n - 1)
                            eng.nop(nofuse=True)
                            e = eng.value_load(cell[0:1, s:s + 1], min_val=0, max_val=E0 - 1)
                            for c in range(KT):
                                for k in range(FK):
                                    last = eng.matmul(ps[:, 5 + s % 2, c * P:(c + 1) * P],
                                                      hid[:, s % 2, k, c * P:(c + 1) * P],
                                                      w2s[:, ds(e, 1), k, :].rearrange("p a d -> p (a d)"),
                                                      start=(k == 0), stop=(k == FK - 1))
                            last.then_inc(fy_ps, 1)

                        def body(n, s):
                            up(n, s)
                            if not late(n, 1):
                                turn(n + 1, (s + 1) % 4)
                            if not early(n, 1):
                                down(n - 1, (s + 3) % 4)

                        turn(0, 0)
                        tile_rounds(eng, body)
                        down(NTL - 1, 3)

                    @block.scalar
                    def _(eng):
                        def keep(n, s):
                            eng.wait_ge(ft_ps, n + 1)
                            if not early(n, 2):
                                eng.wait_ge(fu_ps, (n - 1) * FK)
                            eng.activation(gT[:, s % 2, :], ps[:, 0, 0:TS], ACT.Copy).then_inc(fT_ready, 1)

                        def body(n, s):
                            if not early(n, 2):
                                eng.wait_ge(fy_ps, n - 1)
                            for k in range(FK):
                                eng.wait_ge(fu_ps, n * FK + k + 1)
                                eng.activation(hid[:, s % 2, k, :], ps[:, 1 + k, 0:TS], ACT.Gelu_apprx_tanh,
                                               bias=b1t[:, s % 2, k:k + 1]).then_inc(fh_ready, 1)
                            if not late(n, 1):
                                keep(n + 1, (s + 1) % 4)

                        keep(0, 0)
                        tile_rounds(eng, body)

                    @block.vector
                    def _(eng):
                        def weights(n, s):
                            if not early(n, 2):
                                eng.wait_ge(fu_ps, (n - 1) * FK)
                                eng.wait_ge(fh_ready, (n - 1) * FK)
                            eng.nop(nofuse=True)
                            eng.tensor_copy(cell[0:1, s:s + 1], tile_e[0:1, ds(n, 1)]).then_inc(fw_cell, 1)
                            eng.wait_ge(fw_cell, n + 1)
                            eng.nop(nofuse=True)
                            e = eng.value_load(cell[0:1, s:s + 1], min_val=0, max_val=E0 - 1)
                            eng.tensor_copy(w1t[:, s % 2, :], w1s[:, ds(e, 1), :].rearrange("p a f -> p (a f)"))
                            eng.tensor_copy(b1t[:, s % 2, :], b1c[:, ds(e * FK, FK)]).then_inc(fw_ready, 1)

                        def gates(n, s):
                            eng.wait_ge(f_gathered[s], (n - s) * (KT * 4) + KT * 16)
                            eng.tensor_tensor(gm[:, s % 2, :, :], gath[:, s, :, D:HW0], info[:, ds(n * KT, KT), 4:W],
                                              ALU.mult).then_inc(fg_part, 1)
                            eng.wait_ge(fg_part, n + 1)
                            eng.tensor_reduce(gv[:, s % 2, :], gm[:, s % 2, :, :], AX, ALU.add).then_inc(f_gated, 1)

                        def weigh(n, s):
                            eng.wait_ge(fy_ps, n + 1)
                            eng.wait_ge(f_gated, n + 1)
                            if not early(n, 2):
                                for a in range(KT):
                                    eng.wait_ge(f_added[a], (n - 1) * 16)
                            for k in range(KT):
                                last = eng.tensor_scalar(ysc[:, s % 2, k, :], ps[:, 5 + s % 2, k * P:(k + 1) * P],
                                                         gv[:, s % 2, k:k + 1], None, ALU.mult)
                            last.then_inc(fs_ready, 1)

                        def body(n, s):
                            if not late(n, 1):
                                weights(n + 1, (s + 1) % 4)
                            gates(n, s)
                            if not early(n, 1):
                                weigh(n - 1, (s + 3) % 4)

                        weights(0, 0)
                        tile_rounds(eng, body)
                        weigh(NTL - 1, 3)

            with ExitStack() as tmp2:
                accs = tmp2.enter_context(nc.sbuf_tensor("accs0", [P, 2, NT, D], F32))
                NQ0 = NT // 4
                with nc.Block() as block:
                    @block.sync
                    def _(eng):
                        for a in range(2):
                            eng.wait_ge(f_added[a], NTL * 16)
                        for q in range(4):
                            for a in range(2):
                                eng.dma_start(accs[:, a, q * NQ0:(q + 1) * NQ0, :],
                                              acc0[a][0:T, :].rearrange("(n p) d -> p n d", p=P)[:, q * NQ0:(q + 1) * NQ0, :]
                                              ).then_inc(ld_acc[q], 16)

                    @block.vector
                    def _(eng):
                        step = Chain(eng, vector_steps)
                        step.straight()
                        for q in range(4):
                            eng.wait_ge(ld_acc[q], 32)
                            a0, a1 = (accs[:, a, q * NQ0:(q + 1) * NQ0, :] for a in range(2))
                            step(eng.tensor_tensor(a0, a0, a1, ALU.add))
                            a0c = a0.rearrange("p (c k) d -> p c k d", k=4)
                            step(eng.tensor_tensor(a0c, a0c,
                                                   gchunk[:, 0, q * NQ0 // 4:(q + 1) * NQ0 // 4, None, :].to_broadcast(
                                                       [P, NQ0 // 4, 4, D]), ALU.mult))
                            xs = x_sb[:, q * NQ0:(q + 1) * NQ0, :]
                            step(eng.tensor_tensor(xs, xs, a0, ALU.add))
                            for c in range(q * NQ0 // 4, (q + 1) * NQ0 // 4):
                                token_moments(eng, step, c)
                        step.close()
        rstd_block(2)

        w13T = sb("w13T", [P, E1, 2, F1])
        w2b = sb("w2b", [P, NPAIR, 2, D])
        PG = 4
        with ExitStack() as tmp:
            def st(name, shape, dt=F32):
                return tmp.enter_context(nc.sbuf_tensor(name, shape, dt))

            w1n = st("w1n", [P, 2, PG, P])
            w3n = st("w3n", [P, 2, PG, P])
            w2n = st("w2n", [P, 2, 2 * PG, F1])
            wn_loaded = [sem(f"wn_loaded{u}") for u in range(2)]
            wn_turned = sem("wn_turned")
            wn_kept = sem("wn_kept")
            w2_zero = sem("w2_zero")
            ROUNDS = NPAIR // PG
            w1_v = t["L1_ffn_w1"].rearrange("(n e) f h -> (e f) n h", e=2)
            w3_v = t["L1_ffn_w3"].rearrange("(n e) f h -> (e f) n h", e=2)
            w2_v = t["L1_ffn_w2"].rearrange("e h f -> h e f")

            with nc.Block() as block:
                @block.sync
                def _(eng):
                    with eng.Fori(0, ROUNDS // 2) as j:
                        for u in range(2):
                            r = j * 2 + u
                            eng.wait_ge(wn_turned, r + 1)
                            eng.dma_start(w1n[:, u, :, :], w1_v[:, ds(r * PG, PG), :]).then_inc(wn_loaded[u], 16)
                            eng.dma_start(w3n[:, u, :, :], w3_v[:, ds(r * PG, PG), :]).then_inc(wn_loaded[u], 16)
                            eng.dma_start(w2n[:, u, :, :], w2_v[:, ds(r * 2 * PG, 2 * PG), :]).then_inc(wn_loaded[u], 16)

                @block.gpsimd
                def _(eng):
                    eng.memset(w2b[:, :, :, :], 0.0).then_inc(w2_zero, 1)

                @block.tensor
                def _(eng):
                    eng.sem_inc(wn_turned, 2)
                    with eng.Fori(0, ROUNDS // 2) as j:
                        for u in range(2):
                            r = j * 2 + u
                            eng.wait_ge(wn_loaded[u], 48 * (j + 1))
                            eng.wait_ge(wn_kept, r + 1)
                            for q in range(PG):
                                c = slice(q * P, (q + 1) * P)
                                eng.transpose(bank(0)[:, c], w1n[:, u, q, :], ident[:, :])
                                eng.transpose(bank(1)[:, c], w3n[:, u, q, :], ident[:, :])
                                last = eng.transpose(bank(2)[:, c],
                                                     w2n[:, u, 2 * q:2 * q + 2, :].rearrange("p e f -> p (e f)"),
                                                     ident[:, :])
                            last.then_inc(wn_turned, 1)

                @block.scalar
                def _(eng):
                    eng.sem_inc(wn_kept, 1)
                    eng.wait_ge(w2_zero, 1)
                    with eng.Fori(0, ROUNDS) as r:
                        eng.wait_ge(wn_turned, r + 3)
                        for a in range(2):
                            eng.activation(w13T[:, ds(r * 2 * PG, 2 * PG), a, :],
                                           bank(a).rearrange("p (e f) -> p e f", f=F1), ACT.Copy)
                        for e in range(2):
                            rows = slice(e * F1, (e + 1) * F1)
                            last = eng.activation(w2b[rows, ds(r * PG, PG), e, :],
                                                  ps[rows, 2, :].rearrange("p (q h) -> p q h", q=PG), ACT.Copy)
                        last.then_inc(wn_kept, 1)

        with ExitStack() as tmp:
            def st(name, shape, dt=F32):
                return tmp.enter_context(nc.sbuf_tensor(name, shape, dt))

            xn = st("xn3", [P, 2, B, 4, D])
            h3 = st("h3", [P, 2, B, CHUNK])
            fg = st("fg", [P, CHUNK])
            lam = st("lam", [P, CHUNK])
            state = st("state", [P, 2, CHUNK])
            cxn_ready = sem("cxn_ready")
            cxnT_ready = sem("cxnT_ready")
            ch_ready = sem("ch_ready")
            f_ps = sem("f_ps")
            fg_ready = sem("fg_ready")
            lam_ps = sem("lam_ps")
            lam_ready = sem("lam_ready")
            s_ready = sem("s_ready")
            c_out = sem("c_out")
            cx_added = sem("cx_added")
            ROUNDS_C = CPB // 2
            with nc.Block() as block:
                @block.vector
                def _(eng):
                    step = Chain(eng, vector_steps)
                    step.straight()
                    step(eng.memset(state[:, 1, CHUNK - 1:CHUNK], 0.0))
                    step.close()
                    with eng.Fori(0, ROUNDS_C) as jj:
                        for u in range(2):
                            j = jj * 2 + u
                            for b in range(B):
                                last = normalized(eng, xn[:, u, b, :, :], j + b * CPB)
                            last.then_inc(cxn_ready, 1)
                            eng.wait_ge(lam_ready, j + 1)
                            eng.tensor_tensor_scan(state[:, u, :], lam[:, :], bank(3),
                                                   state[:, 1 - u, CHUNK - 1:CHUNK], ALU.mult, ALU.add).then_inc(s_ready, 1)
                            eng.wait_ge(c_out, j + 1)
                            for b in range(B):
                                xs = x_sb[:, ds((j + b * CPB) * 4, 4), :]
                                last = eng.tensor_tensor(xs, xs, bank(5 + b).rearrange("p (k d) -> p k d", k=4), ALU.add)
                            last.then_inc(cx_added, 1)
                            eng.wait_ge(cx_added, j + 1)
                            for b in range(B):
                                step.body(j * 2 + b, 3)
                                token_moments(eng, step, j + b * CPB)
                    step.end(B * CPB)

                @block.tensor
                def _(eng):
                    with eng.Fori(0, ROUNDS_C) as jj:
                        for u in range(2):
                            j = jj * 2 + u
                            eng.wait_ge(cxn_ready, j + 1)
                            for b in range(B):
                                for k in range(4):
                                    last = eng.transpose(bank(b)[:, k * P:(k + 1) * P], xn[:, u, b, k, :], ident[:, :])
                            last.then_inc(cxnT_ready, 1)
                            eng.wait_ge(ch_ready, j + 1)
                            for w, k in ((w_F, 2), (w_u, 3)):
                                for b in range(B):
                                    last = eng.matmul(ps[b * PR:(b + 1) * PR, k, :], w[:, :], h3[:, u, b, :],
                                                      start=True, stop=True)
                            last.then_inc(f_ps, 1)
                            eng.wait_ge(fg_ready, j + 1)
                            eng.matmul(bank(4), lam_bd[:, :], fg[:, :], start=True, stop=True).then_inc(lam_ps, 1)
                            eng.wait_ge(s_ready, j + 1)
                            for b in range(B):
                                for k in range(4):
                                    c = slice(k * P, (k + 1) * P)
                                    eng.matmul(bank(5 + b)[:, c], h3[:, u, b, c], whx[:, b, :], start=True, stop=False)
                                    last = eng.matmul(bank(5 + b)[:, c], state[:, u, c], whs[:, b, :],
                                                      start=False, stop=True)
                            last.then_inc(c_out, 1)

                @block.scalar
                def _(eng):
                    with eng.Fori(0, ROUNDS_C) as jj:
                        for u in range(2):
                            j = jj * 2 + u
                            eng.wait_ge(cxnT_ready, j + 1)
                            for b in range(B):
                                last = eng.activation(h3[:, u, b, :], bank(b), ACT.Identity,
                                                      bias=shift[:, 1, 1, ds(j + b * CPB, 1)],
                                                      scale=shift[:, 1, 0, ds(j + b * CPB, 1)])
                            last.then_inc(ch_ready, 1)
                            eng.wait_ge(f_ps, j + 1)
                            eng.activation(fg[:, :], bank(2), ACT.Sigmoid).then_inc(fg_ready, 1)
                            eng.wait_ge(lam_ps, j + 1)
                            eng.activation(lam[:, :], bank(4), ACT.Sigmoid).then_inc(lam_ready, 1)
        rstd_block(3)

        NG = 8
        GE = E1 // NG
        TG = 4
        SCALE = 2.5
        CAP = P
        HXW = D + E1
        SPARE = P
        hx = nc.dram_tensor("hx", (T + SPARE, HXW), F32).ap()
        acc = [nc.dram_tensor(f"acc{a}", (T + SPARE, D), F32).ap() for a in range(2)]
        hx_v = hx[0:T, :].rearrange("(n p) c -> p n c", p=P)
        xe_sel = sb("xe_sel", [P, E1, NT], BF16)
        hx_stored = [sem(f"hx_stored{u}") for u in range(2)]
        acc_zeroed = sem("acc_zeroed")
        hx_spare = sem("hx_spare")
        with ExitStack() as tmp:
            def st(name, shape, dt=F32):
                return tmp.enter_context(nc.sbuf_tensor(name, shape, dt))

            zt = st("zt", [P, HXW])
            e_bias = st("e_bias", [P, E1])
            lower = st("lower", [P, NG, NG])
            xn = st("xn4", [P, 2, 4, D])
            rows = st("rows", [P, 2, 4, HXW])
            h4 = st("h4", [P, 2, CHUNK])
            sc = st("sc", [P, 2, 4, E1])
            sgm = st("sgm", [P, CHUNK])
            sgl = st("sgl", [P, CHUNK])
            hs = st("hs", [P, CHUNK])
            sfc = st("sfc", [P, 4, E1])
            tmpv = st("tmpv", [P, 4, E1])
            rep = st("rep", [P, 4, E1])
            sel = st("sel", [P, 2, 4, E1])
            top8 = st("top8", [P, 4, 8])
            hi = st("hi", [P, 4 * NG, GE // 2])
            lo = st("lo", [P, 4 * NG, GE // 2])
            mn = st("mn", [P, 4 * NG, GE // 4])
            gsum = st("gsum", [P, 4, NG])
            gt = st("gt", [P, 4, NG, NG])
            ge = st("ge", [P, 4, NG, NG])
            rank = st("rankg", [P, 4, NG])
            wsum = st("wsum", [P, 4])

            ld_b = sem("ld_b")
            z_ready = sem("z_ready")
            zt_ready = sem("zt_ready")
            dn_ready = sem("dn_ready")
            d_part = sem("d_part")
            h4_ready = sem("h4_ready")
            h4_ps = sem("h4_ps")
            h4T_ready = sem("h4T_ready")
            lg4_ps = sem("lg4_ps")
            sc_ready = sem("sc_ready")
            sh_ps = sem("sh_ps")
            sgm_ready = sem("sgm_ready")
            hs_ready = sem("hs_ready")
            dn_ps = sem("dn_ps")
            dx_added = sem("dx_added")
            sel_ready = sem("sel_ready")
            sel_kept = sem("sel_kept")
            w_ready = sem("w_ready")
            NEVER = -3e38
            with nc.Block() as block:
                @block.sync
                def _(eng):
                    eng.dma_start(e_bias[:, :], t["L1_ffn_e_bias"][None, :].to_broadcast([P, E1])).then_inc(ld_b, 16)
                    eng.wait_ge(zt_ready, 1)
                    for a in range(2):
                        eng.dma_start(acc[a].rearrange("(n p) d -> p n d", p=P),
                                      zt[:, None, 0:D].to_broadcast([P, NT + 1, D])).then_inc(acc_zeroed, 16)
                    eng.dma_start(hx[T:T + SPARE, :], zt[:, :]).then_inc(hx_spare, 16)
                    with eng.Fori(0, NC // 2) as j:
                        for u in range(2):
                            i = j * 2 + u
                            eng.wait_ge(w_ready, i + 3)
                            eng.dma_start(hx_v[:, ds(i * 4, 4), :], rows[:, u, :, :]).then_inc(hx_stored[u], 16)
                    eng.wait_ge(hx_spare, 16)
                    eng.wait_ge(acc_zeroed, 32)
                    for u in range(2):
                        eng.wait_ge(hx_stored[u], 16 * (NC // 2))

                @block.gpsimd
                def _(eng):
                    eng.memset(zt[:, :], 0.0).then_inc(zt_ready, 1)
                    eng.memset(lower[:, :, :], 1.0).then_inc(z_ready, 1)
                    eng.wait_ge(z_ready, 1)
                    eng.affine_select(out=lower[:, :, :], in_=lower[:, :, :], compare_op=ALU.is_gt, fill=0.0, base=0,
                                      pattern=[[1, NG], [-1, NG]], channel_multiplier=0).then_inc(z_ready, 1)

                    def modulate(i, u):
                        eng.wait_ge(dn_ready, i + 1)
                        eng.wait_ge(hx_stored[u], (i - u) * 8)
                        r = rows[:, u, :, 0:D]
                        eng.tensor_tensor(r, xn[:, u, :, :], schunk[:, 1, ds(i, 1), 1, :].to_broadcast([P, 4, D]),
                                          ALU.mult).then_inc(d_part, 1)
                        eng.wait_ge(d_part, i + 1)
                        eng.tensor_tensor(r, r, schunk[:, 1, ds(i, 1), 0, :].to_broadcast([P, 4, D]),
                                          ALU.add).then_inc(h4_ready, 1)

                    def body(i, u, prev, nxt):
                        if nxt:
                            modulate(i + 1, 1 - u)
                        eng.wait_ge(sel_ready, i + 1)
                        eng.tensor_copy(xe_sel[:, :, ds(i * 4, 4)],
                                        sel[:, u, :, :].rearrange("p k e -> p e k")).then_inc(sel_kept, 1)

                    modulate(0, 0)
                    chunks(eng, body)

                @block.tensor
                def _(eng):
                    eng.sem_inc(sh_ps, 1)
                    eng.sem_inc(lg4_ps, 1)
                    def score(i, u):
                        eng.wait_ge(h4_ready, i + 1)
                        eng.wait_ge(h4T_ready, i)
                        for k in range(4):
                            last = eng.transpose(bank(0)[:, k * P:(k + 1) * P], rows[:, u, k, 0:D], ident[:, :])
                        last.then_inc(h4_ps, 1)
                        eng.wait_ge(h4T_ready, i + 1)
                        eng.wait_ge(sc_ready, i)
                        for k in range(4):
                            last = eng.matmul(ps[:, 2, k * E1:(k + 1) * E1], h4[:, u, k * P:(k + 1) * P], gw1[:, :],
                                              start=True, stop=True)
                        last.then_inc(lg4_ps, 1)

                    def up(i, u):
                        eng.wait_ge(hs_ready, i + 1)
                        eng.matmul(bank(4), sgT[:, :], h4[:, u, :], start=True, stop=True)
                        eng.matmul(bank(5), suT[:, :], h4[:, u, :], start=True, stop=True).then_inc(sh_ps, 1)

                    def body(i, u, prev, nxt):
                        if nxt:
                            score(i + 1, 1 - u)
                        eng.wait_ge(hs_ready, i + 2)
                        eng.wait_ge(dx_added, i)
                        for k in range(4):
                            last = eng.matmul(bank(6)[:, k * P:(k + 1) * P], hs[:, k * P:(k + 1) * P],
                                              sdg[:, ds(i, 1), :].rearrange("p a d -> p (a d)"), start=True, stop=True)
                        last.then_inc(dn_ps, 1)
                        if nxt:
                            up(i + 1, 1 - u)

                    score(0, 0)
                    up(0, 0)
                    chunks(eng, body)

                @block.scalar
                def _(eng):
                    with eng.Fori(0, NC // 2) as j:
                        for u in range(2):
                            i = j * 2 + u
                            eng.wait_ge(h4_ps, i + 1)
                            eng.wait_ge(lg4_ps, i + 1)
                            eng.wait_ge(sh_ps, i + 1)
                            eng.activation(h4[:, u, :], bank(0), ACT.Copy).then_inc(h4T_ready, 1)
                            eng.wait_ge(lg4_ps, i + 2)
                            eng.wait_ge(w_ready, i + 1)
                            eng.activation(sc[:, u, :, :], ps[:, 2, 0:4 * E1].rearrange("p (k e) -> p k e", k=4),
                                           ACT.Sigmoid).then_inc(sc_ready, 1)
                            eng.wait_ge(sh_ps, i + 2)
                            eng.wait_ge(hs_ready, i + 1)
                            eng.activation(sgm[:, :], bank(4), ACT.Sigmoid).then_inc(sgm_ready, 1)

                @block.vector
                def _(eng):
                    eng.sem_inc(hs_ready, 1)
                    step = Chain(eng, vector_steps)
                    eng.sem_inc(w_ready, 2)
                    eng.wait_ge(ld_b, 16)
                    eng.wait_ge(z_ready, 2)
                    normalized(eng, xn[:, 0, :, :], 0).then_inc(dn_ready, 1)

                    def body(i, u, prev, nxt):
                        step.body(i, 22)
                        if nxt:
                            eng.wait_ge(h4_ready, i)
                            normalized(eng, xn[:, 1 - u, :, :], i + 1).then_inc(dn_ready, 1)
                        eng.wait_ge(sgm_ready, i + 1)
                        step(eng.tensor_tensor(sgl[:, :], sgm[:, :], bank(4), ALU.mult))
                        eng.tensor_tensor(hs[:, :], sgl[:, :], bank(5), ALU.mult).then_inc(hs_ready, 1)
                        eng.wait_ge(sc_ready, i + 1)
                        s = sc[:, u, :, :]
                        step(eng.tensor_tensor(sfc[:, :, :], s, e_bias[:, None, :].to_broadcast([P, 4, E1]), ALU.add))
                        v = sfc[:, :, :].rearrange("p k (g x) -> p (k g) x", g=NG)
                        q, r = GE // 2, GE // 4
                        eng.tensor_tensor(hi[:, :, :], v[:, :, 0:q], v[:, :, q:GE], ALU.max)
                        step(eng.tensor_tensor(lo[:, :, :], v[:, :, 0:q], v[:, :, q:GE], ALU.min))
                        for w in (r, r // 2):
                            eng.tensor_tensor(mn[:, :, 0:w], hi[:, :, 0:w], hi[:, :, w:2 * w], ALU.min)
                            step(eng.tensor_tensor(lo[:, :, 0:w], lo[:, :, 0:w], lo[:, :, w:2 * w], ALU.max))
                            eng.tensor_tensor(lo[:, :, 0:w], lo[:, :, 0:w], mn[:, :, 0:w], ALU.max)
                            step(eng.tensor_tensor(hi[:, :, 0:w], hi[:, :, 0:w], hi[:, :, w:2 * w], ALU.max))
                        step(eng.tensor_tensor(gsum[:, :, :].rearrange("p k g -> p (k g)"), hi[:, :, 0], lo[:, :, 0], ALU.add))
                        other = gsum[:, :, None, :].to_broadcast([P, 4, NG, NG])
                        mine = gsum[:, :, :, None].to_broadcast([P, 4, NG, NG])
                        eng.tensor_tensor(gt[:, :, :, :], other, mine, ALU.is_gt)
                        step(eng.tensor_tensor(ge[:, :, :, :], other, mine, ALU.is_equal))
                        step(eng.tensor_tensor(ge[:, :, :, :], ge[:, :, :, :],
                                               lower[:, None, :, :].to_broadcast([P, 4, NG, NG]), ALU.mult))
                        step(eng.tensor_tensor(gt[:, :, :, :], gt[:, :, :, :], ge[:, :, :, :], ALU.add))
                        step(eng.tensor_reduce(rank[:, :, :], gt[:, :, :, :], AX, ALU.add))
                        step(eng.tensor_scalar(rank[:, :, :], rank[:, :, :], float(TG), None, ALU.is_lt))
                        step(eng.tensor_tensor(tmpv[:, :, :].rearrange("p k (g x) -> p k g x", g=NG),
                                               sfc[:, :, :].rearrange("p k (g x) -> p k g x", g=NG),
                                               rank[:, :, :, None].to_broadcast([P, 4, NG, GE]), ALU.mult))
                        step(eng.tensor_scalar(tmpv[:, :, :], tmpv[:, :, :], 0.0, None, ALU.add))
                        eng.nop(nofuse=True)
                        for k in range(4):
                            last = eng.max(top8[:, k, :], tmpv[:, k, :])
                        step(last)
                        eng.nop(nofuse=True)
                        for k in range(4):
                            last = eng.match_replace(rep[:, k, :], top8[:, k, :], tmpv[:, k, :], NEVER)
                        step(last)
                        eng.wait_ge(sel_kept, i)
                        eng.tensor_scalar(sel[:, u, :, :], rep[:, :, :], NEVER, None, ALU.is_equal).then_inc(sel_ready, 1)
                        eng.wait_ge(sel_ready, i + 1)
                        step(eng.tensor_tensor(rep[:, :, :], sel[:, u, :, :], s, ALU.mult))
                        step(eng.tensor_reduce(wsum[:, :], rep[:, :, :], AX, ALU.add))
                        step(eng.tensor_scalar(wsum[:, :], wsum[:, :], 1e-20, None, ALU.add))
                        step(eng.reciprocal(wsum[:, :], wsum[:, :]))
                        step(eng.tensor_scalar(wsum[:, :], wsum[:, :], SCALE, None, ALU.mult))
                        eng.wait_ge(h4_ready, i + 1)
                        eng.tensor_tensor(rows[:, u, :, D:HXW], rep[:, :, :],
                                          wsum[:, :, None].to_broadcast([P, 4, E1]), ALU.mult).then_inc(w_ready, 1)
                        eng.wait_ge(dn_ps, i + 1)
                        xs = x_sb[:, ds(i * 4, 4), :]
                        eng.tensor_tensor(xs, xs, bank(6).rearrange("p (k d) -> p k d", k=4), ALU.add).then_inc(dx_added, 1)

                    chunks(eng, body)
                    step.end(NC)

        GROUPS = E1 * NT // P
        EG = E1 // GROUPS
        idx = sb("idx", [P, E1], I32)
        with ExitStack() as tmp:
            def st(name, shape, dt=F32):
                return tmp.enter_context(nc.sbuf_tensor(name, shape, dt))

            rinc = st("rinc", [P, E1, NT], BF16)
            keep = st("keep", [P, E1, NT], BF16)
            selR = st("selR", [P, P + 1], BF16)
            oneR = st("oneR", [P, P + 1], BF16)
            io_i = st("io_i", [P, P], I32)
            iota = st("iota", [P, P])
            cc_i = st("cc_i", [P, 1], I32)
            ccol = st("ccol", [P, 1])
            pay = st("pay", [P, EG, 2], BF16)
            inM = st("inM", [P, GROUPS, EG, P], BF16)
            edge = st("edge", [P, GROUPS, 2])
            oh = st("oh", [P, GROUPS, P])
            oh_b = st("oh_b", [P, GROUPS, P])
            ohb = st("ohb", [P, GROUPS, P], BF16)
            le = st("le", [P, EG, P])
            cnt = st("cnt4", [P, E1])
            nv = st("nv", [P, E1, 2])
            spare = st("spare", [P, 1])
            f1 = st("f1", [P, E1])
            k_ready = sem("k_ready")
            r_done = sem("r_done")
            in_ps = sem("in_ps")
            in_act = sem("in_act")
            oh_ready = sem("oh_ready")
            slot_ps = sem("slot_ps")
            slot_used = sem("slot_used")
            with nc.Block() as block:
                @block.gpsimd
                def _(eng):
                    step = Chain(eng, gpsimd_steps)
                    step.straight()
                    eng.memset(keep[:, :, :], 1.0)
                    eng.memset(oneR[:, :], 1.0)
                    eng.memset(pay[:, :, :], 0.0)
                    eng.memset(inM[:, :, :, :], 0.0)
                    eng.iota(io_i[:, :], pattern=[[1, P]], base=0, channel_multiplier=0)
                    eng.iota(cc_i[:, :], pattern=[[1, 1]], base=0, channel_multiplier=1)
                    step(eng.memset(selR[:, :], -1.0))
                    eng.memset(keep[:, :, 0:1], 0.0)
                    step(eng.affine_select(out=selR[:, 0:P], in_=selR[:, 0:P], compare_op=ALU.is_gt, fill=0.0, base=0,
                                           pattern=[[-1, P]], channel_multiplier=1))
                    eng.tensor_copy(iota[:, :], io_i[:, :])
                    step(eng.tensor_copy(ccol[:, :], cc_i[:, :]))
                    for a in range(EG):
                        r = slice(a * NT, (a + 1) * NT)
                        eng.tensor_scalar(pay[r, a, 0:1], ccol[r, :], float(-a * NT), None, ALU.add)
                        last = eng.tensor_copy(pay[r, a, 1:2], ones[r, 0:1])
                    step(last)
                    step.close()
                    eng.sem_inc(k_ready, 1)

                @block.tensor
                def _(eng):
                    eng.wait_ge(r_done, 1)
                    for g in range(GROUPS):
                        e = slice(g * EG, (g + 1) * EG)
                        o = ps[:, g // 2, (g % 2) * 256:(g % 2) * 256 + P + 1]
                        eng.matmul(o, xe_sel[:, e, :].rearrange("p e n -> p (e n)"), selR[:, :], start=True, stop=False)
                        last = eng.matmul(o, rinc[:, e, :].rearrange("p e n -> p (e n)"), oneR[:, :], start=False, stop=True)
                    last.then_inc(in_ps, 1)
                    eng.wait_ge(oh_ready, 1)
                    eng.wait_ge(in_act, 1)
                    for g in range(GROUPS):
                        if g >= 4:
                            eng.wait_ge(slot_used, g - 3)
                        eng.matmul(bank(g % 4), ohb[:, g, :], inM[:, g, :, :].rearrange("p e m -> p (e m)"),
                                   start=True, stop=True)
                        eng.matmul(ps[:, 4 + g % 4, 0:2 * EG], ohb[:, g, :], pay[:, :, :].rearrange("p e a -> p (e a)"),
                                   start=True, stop=True).then_inc(slot_ps, 1)

                @block.scalar
                def _(eng):
                    eng.wait_ge(in_ps, 1)
                    eng.wait_ge(k_ready, 1)
                    wide = ps[:, :, :].rearrange("p b (h c) -> p (b h) c", h=2)
                    for a in range(EG):
                        r = slice(a * NT, (a + 1) * NT)
                        last = eng.activation(inM[r, :, a, :], wide[r, :, 0:P], ACT.Copy)
                    last.then_inc(in_act, 1)

                @block.vector
                def _(eng):
                    step = Chain(eng, vector_steps)
                    step.straight()
                    eng.wait_ge(k_ready, 1)
                    eng.tensor_tensor_scan(rinc[:, :, :].rearrange("p e n -> p (e n)"),
                                           keep[:, :, :].rearrange("p e n -> p (e n)"),
                                           xe_sel[:, :, :].rearrange("p e n -> p (e n)"), 0.0,
                                           ALU.mult, ALU.add).then_inc(r_done, 1)
                    eng.wait_ge(in_ps, 1)
                    eng.wait_ge(in_act, 1)
                    wide = ps[:, :, :].rearrange("p b (h c) -> p (b h) c", h=2)
                    eng.tensor_copy(edge[:, :, 0], wide[:, :, P])
                    step(eng.tensor_copy(edge[:, :, 1], wide[:, :, P - 1]))
                    io = iota[:, None, :].to_broadcast([P, GROUPS, P])
                    eng.tensor_tensor(oh[:, :, :], io, edge[:, :, 0:1].to_broadcast([P, GROUPS, P]), ALU.is_ge)
                    step(eng.tensor_tensor(oh_b[:, :, :], io, edge[:, :, 1:2].to_broadcast([P, GROUPS, P]), ALU.is_ge))
                    step(eng.tensor_tensor(ohb[:, :, :], oh[:, :, :], oh_b[:, :, :], ALU.subtract))
                    eng.sem_inc(oh_ready, 1)
                    for g in range(GROUPS):
                        eng.wait_ge(slot_ps, g + 1)
                        eng.tensor_copy(nv[:, g * EG:(g + 1) * EG, :].rearrange("p e a -> p (e a)"),
                                        ps[:, 4 + g % 4, 0:2 * EG])
                        for a in range(EG):
                            last = eng.tensor_scalar(le[:, a, :], bank(g % 4)[:, a * P:(a + 1) * P], ccol[:, :], 0.0,
                                                     ALU.is_le, ALU.add, accum_out=cnt[:, g * EG + a:g * EG + a + 1])
                        step(last)
                        eng.sem_inc(slot_used, 1)
                    step(eng.tensor_scalar(spare[:, :], ccol[:, :], float(T - P), None, ALU.add))
                    step(eng.scalar_tensor_tensor(f1[:, :], nv[:, :, 0], float(P), cnt[:, :], ALU.mult, ALU.add))
                    step(eng.tensor_scalar(f1[:, :], f1[:, :], spare[:, :], None, ALU.add))
                    step(eng.tensor_scalar(nv[:, :, 1], nv[:, :, 1], spare[:, :], None, ALU.mult))
                    step(eng.tensor_tensor(idx[:, :], f1[:, :], nv[:, :, 1], ALU.subtract))
                    step.close()

        with ExitStack() as tmp:
            def st(name, shape, dt=F32):
                return tmp.enter_context(nc.sbuf_tensor(name, shape, dt))

            KE = 4
            RE = E1 // KE
            PER_ROUND = KE // 2 * 16
            ixs = st("ixs", [P, 4, KE], I32)
            gath = st("gath", [P, 2, KE, HXW])
            gT = st("gT", [P, 2, KE, P])
            sl = st("sl", [P, 2, KE, F1])
            hh = st("hh", [P, 2, KE, F1])
            hhT = st("hhT", [P, 2, KE // 2, P])
            ysc = st("ysc", [P, 2, KE, D])
            ix_ready = sem("ix_ready")
            gathered = [sem(f"gathered{u}") for u in range(2)]
            g_ps = sem("g_ps")
            gT_ready = sem("gT_ready")
            up_ps = sem("up_ps")
            sl_ready = sem("sl_ready")
            hh_ready = sem("hh_ready")
            hh_ps = sem("hh_ps")
            hhT_ready = sem("hhT_ready")
            y_ps = sem("y_ps")
            ysc_ready = sem("ysc_ready")
            added = [sem(f"added{a}") for a in range(2)]
            with nc.Block() as block:
                @block.gpsimd
                def _(eng):
                    def gather(r, s):
                        u = s % 2
                        if type(r) is not int or r >= 2:
                            eng.wait_ge(ysc_ready, r)
                        if type(r) is not int or r >= 4:
                            for a in range(2):
                                eng.wait_ge(added[a], (r - 3) * PER_ROUND)
                        eng.tensor_copy(ixs[:, s, :], idx[:, ds(r * KE, KE)]).then_inc(ix_ready, 1)
                        eng.wait_ge(ix_ready, r + 1)
                        eng.nop(nofuse=True)
                        for k in range(KE):
                            eng.indirect_dma_start(out=gath[:, u, k, :], out_offset=None, in_=hx,
                                                   in_offset=bass.IndirectOffsetOnAxis(ap=ixs[:, s, k:k + 1], axis=0)
                                                   ).then_inc(gathered[u], 16)

                    def scatter(r, s):
                        eng.wait_ge(ysc_ready, r + 2)
                        for k in range(KE):
                            eng.wait_ge(added[k % 2], r * PER_ROUND + k // 2 * 16)
                            eng.nop(nofuse=True)
                            eng.indirect_dma_start(out=acc[k % 2],
                                                   out_offset=bass.IndirectOffsetOnAxis(ap=ixs[:, s, k:k + 1], axis=0),
                                                   in_=ysc[:, s % 2, k, :], in_offset=None,
                                                   compute_op=ALU.add).then_inc(added[k % 2], 16)

                    eng.wait_ge(hx_spare, 16)
                    eng.wait_ge(acc_zeroed, 32)
                    for u in range(2):
                        eng.wait_ge(hx_stored[u], 16 * (NC // 2))
                    gather(0, 0)
                    for s in range(4):
                        gather(s + 1, (s + 1) % 4)
                        scatter(s, s)
                    with eng.Fori(1, RE // 4 - 1) as j:
                        for s in range(4):
                            gather(j * 4 + s + 1, (s + 1) % 4)
                            scatter(j * 4 + s, s)
                    for s in range(4):
                        if s < 3:
                            gather(RE - 4 + s + 1, s + 1)
                        scatter(RE - 4 + s, s)

                @block.tensor
                def _(eng):
                    eng.sem_inc(y_ps, 1)
                    eng.sem_inc(up_ps, 1)
                    with eng.Fori(0, RE // 2) as j:
                        for u in range(2):
                            r = j * 2 + u
                            eng.wait_ge(gathered[u], (j + 1) * 16 * KE)
                            eng.wait_ge(gT_ready, r + 1)
                            for k in range(KE):
                                last = eng.transpose(bank(0)[:, k * P:(k + 1) * P], gath[:, u, k, 0:D], ident[:, :])
                            last.then_inc(g_ps, 1)
                            eng.wait_ge(gT_ready, r + 2)
                            eng.wait_ge(hh_ready, r + 1)
                            for k in range(KE):
                                last = eng.matmul(bank(1)[:, k * P:(k + 1) * P], gT[:, u, k, :],
                                                  w13T[:, ds(r * KE + k, 1), :, :].rearrange("p e a f -> p (e a f)"),
                                                  start=True, stop=True)
                            last.then_inc(up_ps, 1)
                            eng.wait_ge(hh_ready, r + 2)
                            eng.wait_ge(hhT_ready, r + 1)
                            for q in range(KE // 2):
                                last = eng.transpose(ps[:, 2, q * P:(q + 1) * P],
                                                     hh[:, u, 2 * q:2 * q + 2, :].rearrange("p e f -> p (e f)"), ident[:, :])
                            last.then_inc(hh_ps, 1)
                            eng.wait_ge(hhT_ready, r + 2)
                            eng.wait_ge(ysc_ready, r + 1)
                            for q in range(KE // 2):
                                last = eng.matmul(bank(3)[:, q * 256:(q + 1) * 256], hhT[:, u, q, :],
                                                  w2b[:, ds(r * (KE // 2) + q, 1), :, :].rearrange("p a e h -> p (a e h)"),
                                                  start=True, stop=True)
                            last.then_inc(y_ps, 1)

                @block.scalar
                def _(eng):
                    eng.sem_inc(hhT_ready, 1)
                    eng.sem_inc(gT_ready, 1)
                    with eng.Fori(0, RE // 2) as j:
                        for u in range(2):
                            r = j * 2 + u
                            eng.wait_ge(g_ps, r + 1)
                            eng.wait_ge(up_ps, r + 1)
                            eng.activation(gT[:, u, :, :].rearrange("p k c -> p (k c)"), bank(0), ACT.Copy).then_inc(gT_ready, 1)
                            eng.wait_ge(up_ps, r + 2)
                            eng.wait_ge(hh_ready, r + 1)
                            eng.activation(sl[:, u, :, :], bank(1).rearrange("p (k a f) -> p k a f", k=KE, a=2)[:, :, 0, :],
                                           ACT.Silu).then_inc(sl_ready, 1)
                            eng.wait_ge(hh_ps, r + 1)
                            eng.wait_ge(y_ps, r + 1)
                            eng.activation(hhT[:, u, :, :].rearrange("p q c -> p (q c)"), ps[:, 2, 0:2 * P],
                                           ACT.Copy).then_inc(hhT_ready, 1)

                @block.vector
                def _(eng):
                    eng.sem_inc(ysc_ready, 1)
                    eng.sem_inc(hh_ready, 1)
                    def body(r, u):
                        eng.wait_ge(sl_ready, r + 1)
                        eng.wait_ge(hh_ps, r)
                        eng.tensor_tensor(hh[:, u, :, :], sl[:, u, :, :],
                                          bank(1).rearrange("p (k a f) -> p k a f", k=KE, a=2)[:, :, 1, :],
                                          ALU.mult).then_inc(hh_ready, 1)
                        eng.wait_ge(y_ps, r + 2)
                        if type(r) is not int or r >= 2:
                            for a in range(2):
                                eng.wait_ge(added[a], (r - 1) * PER_ROUND)
                        for k in range(KE):
                            last = eng.tensor_scalar(ysc[:, u, k, :], bank(3)[:, k * P:(k + 1) * P],
                                                     gath[:, u, k, ds(D + r * KE + k, 1)], None, ALU.mult)
                        last.then_inc(ysc_ready, 1)

                    body(0, 0)
                    body(1, 1)
                    with eng.Fori(1, RE // 2) as j:
                        for u in range(2):
                            body(j * 2 + u, u)

        with ExitStack() as tmp:
            accs = tmp.enter_context(nc.sbuf_tensor("accs", [P, 2, NT, D], F32))
            res_ready = sem("res_ready")
            st_out = sem("st_out")
            NQ = NT // 4
            with nc.Block() as block:
                @block.sync
                def _(eng):
                    for a in range(2):
                        eng.wait_ge(added[a], E1 // 2 * 16)
                    for q in range(4):
                        for a in range(2):
                            eng.dma_start(accs[:, a, q * NQ:(q + 1) * NQ, :],
                                          acc[a][0:T, :].rearrange("(n p) d -> p n d", p=P)[:, q * NQ:(q + 1) * NQ, :]
                                          ).then_inc(ld_acc[q], 16)
                    for q in range(4):
                        eng.wait_ge(res_ready, q + 1)
                        eng.dma_start(out_v[:, q * NQ:(q + 1) * NQ, :], x_sb[:, q * NQ:(q + 1) * NQ, :]).then_inc(st_out, 16)
                    eng.wait_ge(st_out, 64)

                @block.vector
                def _(eng):
                    step = Chain(eng, vector_steps)
                    step.straight()
                    for q in range(4):
                        eng.wait_ge(ld_acc[q], 64)
                        a0, a1 = (accs[:, a, q * NQ:(q + 1) * NQ, :] for a in range(2))
                        step(eng.tensor_tensor(a0, a0, a1, ALU.add))
                        step(eng.tensor_tensor(a0.rearrange("p (c k) d -> p c k d", k=4), a0.rearrange("p (c k) d -> p c k d", k=4),
                                               gchunk[:, 1, q * NQ // 4:(q + 1) * NQ // 4, None, :].to_broadcast([P, NQ // 4, 4, D]),
                                               ALU.mult))
                        xs = x_sb[:, q * NQ:(q + 1) * NQ, :]
                        eng.tensor_tensor(xs, xs, a0, ALU.add).then_inc(res_ready, 1)


_INS = [
    'L0_attn_x', 'L0_attn_w_qkv', 'L0_attn_w_out', 'L0_attn_b_out', 'L0_attn_proj', 'L0_ffn_gate_weight',
    'L0_ffn_W1', 'L0_ffn_b1', 'L0_ffn_W2', 'L0_ffn_b2', 'L0_ffn_Ws1', 'L0_ffn_bs1', 'L0_ffn_Ws2',
    'L0_ffn_bs2', 'L0_c', 'L0_wmod', 'L1_attn_W_toP', 'L1_attn_W_U', 'L1_attn_W_F', 'L1_attn_W_V',
    'L1_attn_W_lam', 'L1_attn_B_mat', 'L1_attn_C_mat', 'L1_attn_W_fromP', 'L1_ffn_gate_weight',
    'L1_ffn_e_bias', 'L1_ffn_w1', 'L1_ffn_w2', 'L1_ffn_w3', 'L1_ffn_shared_gate', 'L1_ffn_shared_up',
    'L1_ffn_shared_down', 'L1_c', 'L1_wmod',
]
_OUTS = [((2, 2048, 128), "float32")]


def kernel(**inputs):
    import numpy as _np
    import concourse.bacc as _bacc
    from concourse import mybir as _mybir
    from concourse.bass_utils import run_bass_kernel_spmd as _run

    nc = _bacc.Bacc("TRN2", target_bir_lowering=False, num_devices=1)
    arrays, args, outs = {}, {}, []
    for name in _INS:
        a = _np.ascontiguousarray(inputs[name])
        arrays[f"in_{name}_dram"] = a
        args[name] = nc.dram_tensor(f"in_{name}_dram", a.shape, _mybir.dt.from_np(a.dtype), kind="ExternalInput").ap()
    for i, (shape, dtype) in enumerate(_OUTS):
        dt = _mybir.dt.from_np(_np.dtype(dtype))
        outs.append(nc.dram_tensor(f"out_{i}_dram", shape, dt, kind="ExternalOutput").ap())
    build(nc, args, outs[0])
    r = _run(nc, [arrays], core_ids=[0])
    return r.results[0]["out_0_dram"]
```

```python
from contextlib import ExitStack

import concourse.bass as bass
from concourse import mybir

F32 = mybir.dt.float32
BF16 = mybir.dt.bfloat16
I32 = mybir.dt.int32
ALU = mybir.AluOpType
ACT = mybir.ActivationFunctionType
AX = mybir.AxisListType.X
ds = bass.ds

P = 128
TILE = 128
CHUNK_TILES = 4
CHUNK = CHUNK_TILES * TILE
LN_EPS = 1e-5


class Steps:

    def __init__(self, sem):
        self.sem, self.past = sem, 0


class Chain:

    def __init__(self, engine, steps):
        self.engine, self.steps, self.k = engine, steps, 0

    def body(self, i, n):
        self.base, self.n, self.k = self.steps.past + i * n, n, 0

    def end(self, rounds):
        assert self.k == self.n, (self.k, self.n)
        self.steps.past, self.k = self.steps.past + rounds * self.n, 0

    def straight(self):
        self.base = self.steps.past

    def __call__(self, ins):
        self.k += 1
        ins.then_inc(self.steps.sem, 1)
        self.engine.wait_ge(self.steps.sem, self.base + self.k)

    def close(self):
        self.steps.past, self.k = self.steps.past + self.k, 0


def build(nc, t, out):
    B, T1, D = t["L0_attn_x"].shape
    T = B * T1
    NT = T // TILE
    NC = T // CHUNK
    CPB = NC // B
    H, HD, FT = t["L0_attn_proj"].shape
    E0, _, FF = t["L0_ffn_W1"].shape
    FK = FF // P
    E1, F1, _ = t["L1_ffn_w1"].shape
    PR = t["L1_attn_W_lam"].shape[1]
    ALPHA = t["L1_attn_W_V"].shape[1]
    NPAIR = E1 // 2
    x_in = t["L0_attn_x"].rearrange("b (n p) d -> p (b n) d", p=P)
    out_v = out.rearrange("b (n p) d -> p (b n) d", p=P)

    with ExitStack() as ctx:
        def sb(name, shape, dt=F32):
            return ctx.enter_context(nc.sbuf_tensor(name, shape, dt))

        def sem(name):
            return ctx.enter_context(nc.semaphore(name))

        ps = ctx.enter_context(nc.psum_tensor("ps", [P, 8, 512], F32))

        def bank(k):
            return ps[:, k, :]

        ident = sb("ident", [P, P])
        ones = sb("ones", [P, P])
        ones_bf = sb("ones_bf", [P, P], BF16)
        before = sb("before", [P, P])
        before_bf = sb("before_bf", [P, P], BF16)
        x_sb = sb("x_sb", [P, NT, D])
        moments = sb("moments", [P, NT, 2])
        rstd = sb("rstd", [P, NT])
        nmr = sb("nmr", [P, NT])
        scT = sb("scT", [P, 2 * B])
        shift = sb("shift", [P, 2, 4, NC])
        grow = sb("grow", [P, 2 * B, 2, D])
        schunk = sb("schunk", [P, 2, NC, 2, D])
        gchunk = sb("gchunk", [P, 2, NC, D])
        wf = sb("wf", [P, 2, H, FT])
        wv = sb("wv", [P, D])
        wob = sb("wob", [P, NC, 2, D])
        bob = sb("bob", [1, NC, D])
        gw0 = sb("gw0", [P, E0])
        gw1 = sb("gw1", [P, E1])
        b1c = sb("b1c", [P, (E0 + 1) * FK])
        w_F = sb("w_F", [P, PR])
        w_u = sb("w_u", [P, PR])
        lam_bd = sb("lam_bd", [P, P])
        whx = sb("whx", [P, B, D])
        whs = sb("whs", [P, B, D])
        sgT = sb("sgT", [P, P])
        suT = sb("suT", [P, P])
        sdg = sb("sdg", [P, NC, D])
        dsel = sb("dsel", [P, P])
        blockmask = sb("blockmask", [P, P])
        stats_all = sb("stats_all", [P, NT, 6])
        stats6 = sb("stats6", [P, 4, 6])
        mom4 = sb("mom4", [P, 4, 2])

        vector_steps = Steps(sem("vector_steps"))
        gpsimd_steps = Steps(sem("gpsimd_steps"))
        var_ready = sem("var_ready")
        std_ready = sem("std_ready")
        ld_acc = [sem(f"ld_acc{q}") for q in range(4)]
        SPARE = P
        HW0, HXW = D + E0, D + E1
        hx0 = nc.dram_tensor("hx0", (T + SPARE, HW0), F32).ap()
        hx0_v = hx0[0:T, :].rearrange("(n p) c -> p n c", p=P)
        acc0 = [nc.dram_tensor(f"acc0_{a}", (T + SPARE, D), F32).ap() for a in range(2)]
        hx = nc.dram_tensor("hx", (T + SPARE, HXW), F32).ap()
        acc = [nc.dram_tensor(f"acc{a}", (T + SPARE, D), F32).ap() for a in range(2)]
        hx_v = hx[0:T, :].rearrange("(n p) c -> p n c", p=P)
        zt = sb("zt", [P, HXW])
        acc0_zeroed = sem("acc0_zeroed")
        acc_zeroed = sem("acc_zeroed")
        ld_x = sem("ld_x")
        ld_mod = sem("ld_mod")
        ld_w = sem("ld_w")
        mod_c = sem("mod_c")
        c_turned = sem("c_turned")
        mod_b = sem("mod_b")
        mod_ps = sem("mod_ps")

        def token_moments(eng, step, c):
            eng.nop(nofuse=True)
            for k in range(4):
                last = eng.bn_stats(stats6[:, k, :], x_sb[:, ds(c * 4 + k, 1), :])
            step(last)
            eng.nop(nofuse=True)
            for k in range(4):
                last = eng.bn_aggr(mom4[:, k, :], stats6[:, k, :])
            step(last)
            eng.nop(nofuse=True)
            step(eng.tensor_copy(moments[:, ds(c * 4, 4), :], mom4[:, :, :]))

        def moments_of(eng, step, tiles):
            for n in tiles:
                last = eng.bn_stats(stats_all[:, n, :], x_sb[:, n, :])
            step(last)
            for n in tiles:
                last = eng.bn_aggr(moments[:, n, :], stats_all[:, n, :])
            step(last)

        with ExitStack() as tmp:
            def st(name, shape, dt=F32):
                return tmp.enter_context(nc.sbuf_tensor(name, shape, dt))

            wmod = st("wmod", [P, 2, 6 * D])
            c_rows = st("c_rows", [2 * B, D])
            wqkv = st("wqkv", [P, 3, D])
            projblk = st("projblk", [P, H, FT])
            wo_n = st("wo_n", [P, D])
            wop = st("wop", [P, 2, 4, 32])
            bo_n = st("bo_n", [1, D])
            g0n = st("g0n", [E0, D])
            g1n = st("g1n", [E1, D])
            b1n = st("b1n", [(E0 + 1) * FK, P])
            toP = st("toP", [P, PR])
            wU = st("wU", [P, PR, ALPHA])
            wV = st("wV", [P, PR, ALPHA])
            wUV = st("wUV", [P, PR, ALPHA])
            wt = st("wt", [P, PR])
            wtT = st("wtT", [PR, P])
            Bm = st("Bm", [PR, PR])
            Cm = st("Cm", [PR, PR])
            CT = st("CT", [PR, 2, PR])
            fP = st("fP", [PR, D])
            sgn = st("sgn", [P, D])
            sun = st("sun", [P, D])
            sdn = st("sdn", [P, P])
            scb = st("scb", [P, 2 * B, P])
            modT = st("modT", [P, 2, 6, B])
            graw = st("graw", [P, 2 * B, 2, D])
            gsg = st("gsg", [P, 2 * B, 2, D])

            zeroed = sem("zeroed")
            wts_ps = sem("wts_ps")
            turned = sem("turned")
            fold_ps = sem("fold_ps")
            wt_done = sem("wt_done")
            N_LOADS = H + B + 17

            with nc.Block() as block:
                @block.sync
                def _(eng):
                    eng.dma_start(c_rows[0:B, :], t["L0_c"]).then_inc(ld_mod, 16)
                    eng.dma_start(c_rows[B:2 * B, :], t["L1_c"]).then_inc(ld_mod, 16)
                    eng.dma_start(wmod[:, 0, :], t["L0_wmod"]).then_inc(ld_mod, 16)
                    eng.dma_start(wmod[:, 1, :], t["L1_wmod"]).then_inc(ld_mod, 16)
                    eng.wait_ge(zeroed, 1)
                    for h in range(H):
                        eng.dma_start(projblk[h * HD:(h + 1) * HD, h, :], t["L0_attn_proj"][h]).then_inc(ld_w, 16)
                    for b in range(B):
                        eng.dma_start(lam_bd[b * PR:(b + 1) * PR, b * PR:(b + 1) * PR],
                                      t["L1_attn_W_lam"]).then_inc(ld_w, 16)
                    for dst, src in [
                        (wqkv[:, :, :], t["L0_attn_w_qkv"].rearrange("(g o) d -> o g d", o=P)),
                        (wo_n[:, :], t["L0_attn_w_out"]),
                        (bo_n[:, :], t["L0_attn_b_out"].rearrange("(a d) -> a d", a=1)),
                        (g0n[:, :], t["L0_ffn_gate_weight"]),
                        (g1n[:, :], t["L1_ffn_gate_weight"]),
                        (b1n[0:E0 * FK, :], t["L0_ffn_b1"].rearrange("e (k p) -> (e k) p", p=P)),
                        (b1n[E0 * FK:, :], t["L0_ffn_bs1"].rearrange("(k p) -> k p", p=P)),
                        (toP[:, :], t["L1_attn_W_toP"]),
                        (wU[:, :, :], t["L1_attn_W_U"]),
                        (wV[:, :, :], t["L1_attn_W_V"][None, :, :].to_broadcast([P, PR, ALPHA])),
                        (w_F[:, :], t["L1_attn_W_F"]),
                        (Bm[:, :], t["L1_attn_B_mat"]),
                        (Cm[:, :], t["L1_attn_C_mat"]),
                        (fP[:, :], t["L1_attn_W_fromP"]),
                        (sgn[:, :], t["L1_ffn_shared_gate"]),
                        (sun[:, :], t["L1_ffn_shared_up"]),
                        (sdn[:, :], t["L1_ffn_shared_down"]),
                    ]:
                        eng.dma_start(dst, src).then_inc(ld_w, 16)
                    for rows, zeroed_rows in ((hx0, acc0_zeroed), (hx, acc_zeroed)):
                        eng.dma_start(rows[T:T + SPARE, :], zt[:, 0:rows.shape[1]]).then_inc(zeroed_rows, 16)
                    for targets, zeroed_targets in ((acc0, acc0_zeroed), (acc, acc_zeroed)):
                        for a in targets:
                            eng.dma_start(a.rearrange("(n p) d -> p n d", p=P),
                                          zt[:, None, 0:D].to_broadcast([P, NT + 1, D])).then_inc(zeroed_targets, 16)

                @block.gpsimd
                def _(eng):
                    step = Chain(eng, gpsimd_steps)
                    step.straight()
                    eng.memset(projblk[:, :, :], 0.0)
                    eng.memset(zt[:, :], 0.0)
                    step(eng.memset(lam_bd[:, :], 0.0))
                    eng.sem_inc(zeroed, 1)
                    eng.memset(ones[:, :], 1.0)
                    eng.memset(ones_bf[:, :], 1.0)
                    eng.memset(before[:, :], 1.0)
                    eng.memset(before_bf[:, :], 1.0)
                    eng.memset(dsel[:, :], 0.0)
                    eng.memset(blockmask[:, :], 0.0)
                    eng.memset(wop[:, :, :, :], 0.0)
                    eng.memset(whs[:, :, :], 0.0)
                    step(eng.memset(ident[:, :], 0.0))
                    step(eng.affine_select(out=before[:, :], in_=before[:, :], compare_op=ALU.is_gt, fill=0.0, base=0,
                                      pattern=[[1, P]], channel_multiplier=-1))
                    step(eng.affine_select(out=before_bf[:, :], in_=before_bf[:, :], compare_op=ALU.is_gt, fill=0.0, base=0,
                                      pattern=[[1, P]], channel_multiplier=-1))
                    for j in range(4):
                        step(eng.memset(blockmask[32 * j:32 * j + 32, 32 * j:32 * j + 32], 1.0))
                    step(eng.affine_select(out=dsel[:, :].rearrange("p (a b) -> p a b", a=4),
                                      in_=dsel[:, :].rearrange("p (a b) -> p a b", a=4),
                                      compare_op=ALU.not_equal, fill=1.0, base=-HD,
                                      pattern=[[-32, 4], [0, 32]], channel_multiplier=1))
                    step(eng.affine_select(out=ident[:, :], in_=ident[:, :], compare_op=ALU.not_equal, fill=1.0,
                                           base=0, pattern=[[-1, P]], channel_multiplier=1))
                    step.close()
                    eng.sem_inc(zeroed, 1)

                @block.scalar
                def _(eng):
                    for q in range(4):
                        n = NT // 4
                        eng.dma_start(x_sb[:, q * n:(q + 1) * n, :], x_in[:, q * n:(q + 1) * n, :]).then_inc(ld_x, 16)
                    eng.wait_ge(c_turned, 1)
                    eng.activation(scT[:, :], ps[:, 5, 0:2 * B], ACT.Silu).then_inc(mod_c, 1)
                    eng.wait_ge(wts_ps, 1)
                    for qk in range(2):
                        for g in range(2):
                            eng.activation(wf[:, qk, 4 * g:4 * g + 4, :].rearrange("p a f -> p (a f)"),
                                           bank(2 * qk + g), ACT.Copy)
                    eng.wait_ge(wts_ps, 2)
                    eng.activation(wv[:, :], ps[:, 4, 0:128], ACT.Copy)
                    eng.activation(gw0[:, :], ps[:, 5, 128:128 + E0], ACT.Copy)
                    eng.activation(gw1[:, :], ps[:, 5, 0:E1], ACT.Copy)
                    eng.activation(b1c[:, :], ps[:, 5, 64:64 + (E0 + 1) * FK], ACT.Copy)
                    eng.activation(sgT[:, :], ps[:, 6, 0:128], ACT.Copy)
                    eng.activation(suT[:, :], ps[:, 6, 128:256], ACT.Copy)
                    eng.activation(wtT[:, :], ps[0:PR, 5, 256:384], ACT.Copy)
                    for b in range(2):
                        last = eng.activation(CT[:, b, :], ps[0:PR, 5, 384:384 + PR], ACT.Copy)
                    last.then_inc(turned, 1)
                    eng.wait_ge(fold_ps, 1)
                    eng.activation(w_u[:, :], ps[:, 7, 0:PR], ACT.Copy).then_inc(turned, 1)

                @block.tensor
                def _(eng):
                    eng.wait_ge(ld_mod, 64)
                    eng.wait_ge(zeroed, 2)
                    eng.transpose(ps[:, 5, 0:2 * B], c_rows[:, :], ident[0:2 * B, 0:2 * B]).then_inc(c_turned, 1)
                    eng.wait_ge(mod_b, 1)
                    for lb in range(2 * B):
                        eng.matmul(bank(lb), scb[:, lb, :], wmod[:, lb // B, 2 * D:6 * D], start=True, stop=True)
                    for l in range(2):
                        for j in range(6):
                            k = (l * 6 + j) * B
                            last = eng.matmul(ps[:, 4, k:k + B], wmod[:, l, j * D:(j + 1) * D],
                                              scT[:, l * B:(l + 1) * B], start=True, stop=True)
                    last.then_inc(mod_ps, 1)
                    eng.wait_ge(mod_b, 2)
                    eng.wait_ge(ld_w, 16 * N_LOADS)
                    eng.wait_ge(zeroed, 2)
                    for qk in range(2):
                        for g in range(2):
                            last = eng.matmul(bank(2 * qk + g), wqkv[:, qk, :],
                                              projblk[:, 4 * g:4 * g + 4, :].rearrange("p a f -> p (a f)"),
                                              start=True, stop=True)
                    last.then_inc(wts_ps, 1)
                    eng.transpose(ps[:, 4, 0:128], wqkv[:, 2, :], ident[:, :])
                    eng.wait_ge(wt_done, 1)
                    for g in range(2):
                        eng.transpose(ps[:, 4, 128 + 128 * g:256 + 128 * g],
                                      wop[:, g, :, :].rearrange("p a c -> p (a c)"), ident[:, :])
                    eng.transpose(ps[:, 5, 128:128 + E0], g0n[:, :], ident[0:E0, 0:E0])
                    eng.transpose(ps[:, 5, 0:E1], g1n[:, :], ident[0:E1, 0:E1])
                    nb = (E0 + 1) * FK
                    eng.transpose(ps[:, 5, 64:64 + nb], b1n[:, :], ident[0:nb, 0:nb])
                    eng.transpose(ps[0:PR, 5, 256:384], wt[:, :], ident[:, :])
                    eng.transpose(ps[0:PR, 5, 384:384 + PR], Cm[:, :], ident[0:PR, 0:PR])
                    eng.transpose(ps[:, 6, 0:128], sgn[:, :], ident[:, :])
                    eng.transpose(ps[:, 6, 128:256], sun[:, :], ident[:, :])
                    eng.transpose(ps[:, 6, 256:384], sdn[:, :], ident[:, :]).then_inc(wts_ps, 1)
                    eng.wait_ge(turned, 1)
                    eng.matmul(ps[:, 7, 0:PR], wtT[:, :], Bm[:, :], start=True, stop=True)
                    eng.matmul(ps[:, 7, 128:256], wtT[:, :], fP[:, :], start=True, stop=True)
                    eng.matmul(ps[:, 7, 256:384], CT[:, :, :].rearrange("p b r -> p (b r)"), fP[:, :],
                               start=True, stop=True).then_inc(fold_ps, 1)

                @block.vector
                def _(eng):
                    step = Chain(eng, vector_steps)
                    eng.wait_ge(mod_c, 1)
                    eng.tensor_copy(scb[:, :, :], scT[:, :, None].to_broadcast([P, 2 * B, P])).then_inc(mod_b, 1)
                    eng.wait_ge(ld_x, 64)
                    step.straight()
                    moments_of(eng, step, range(NT))
                    eng.wait_ge(mod_ps, 1)
                    eng.tensor_copy(modT[:, :, :, :].rearrange("p l j b -> p (l j b)"), ps[:, 4, 0:12 * B])
                    for lb in range(2 * B):
                        r = bank(lb).rearrange("p (j d) -> p j d", j=4)
                        eng.tensor_copy(graw[:, lb, :, :], r[:, 0::3, :])
                        cs = slice((lb % B) * CPB, (lb % B + 1) * CPB)
                        eng.tensor_copy(schunk[:, lb // B, cs, 0, :], r[:, 1:2, :].to_broadcast([P, CPB, D]))
                        eng.tensor_scalar(schunk[:, lb // B, cs, 1, :], r[:, 2:3, :].to_broadcast([P, CPB, D]), 1.0, None,
                                          ALU.add)
                    step(eng.tensor_copy(mom4[:, 0, 0:1], ps[:, 4, 0:1]))
                    eng.sem_inc(mod_b, 1)
                    for l in range(2):
                        for k, (j, add) in enumerate([(1, 1.0), (0, 0.0), (4, 1.0), (3, 0.0)]):
                            eng.tensor_scalar(shift[:, l, k, :].rearrange("p (b c) -> p b c", b=B),
                                              modT[:, l, j, :, None].to_broadcast([P, B, CPB]), add, None, ALU.add)
                    flat = graw[:, :, :, :].rearrange("p a b d -> p (a b d)")
                    gs = gsg[:, :, :, :].rearrange("p a b d -> p (a b d)")
                    gr = grow[:, :, :, :].rearrange("p a b d -> p (a b d)")
                    eng.tensor_scalar(gs, flat, 0.0, 2.0, ALU.is_ge, ALU.mult)
                    step(eng.scalar_tensor_tensor(gr, flat, -1.0, flat, ALU.mult, ALU.max))
                    step(eng.tensor_scalar(gr, gr, 0.25, None, ALU.max))
                    step(eng.scalar_tensor_tensor(gr, gs, -1.0, gr, ALU.add, ALU.mult))
                    for l in range(2):
                        for b in range(B):
                            eng.tensor_copy(gchunk[:, l, b * CPB:(b + 1) * CPB, :],
                                            grow[:, l * B + b, 1:2, :].to_broadcast([P, CPB, D]))
                    eng.wait_ge(ld_w, 16 * N_LOADS)
                    eng.wait_ge(zeroed, 2)
                    eng.tensor_copy(wop[:, :, :, 0:HD], wo_n[:, :].rearrange("p (g a c) -> p g a c", g=2, a=4))
                    step(eng.tensor_tensor(wUV[:, :, :], wU[:, :, :], wV[:, :, :], ALU.mult))
                    step(eng.tensor_reduce(wt[:, :], wUV[:, :, :], AX, ALU.add))
                    step(eng.tensor_tensor(wt[:, :], wt[:, :], toP[:, :], ALU.add))
                    eng.sem_inc(wt_done, 1)
                    eng.wait_ge(turned, 1)
                    for b in range(B):
                        cs = slice(b * CPB, (b + 1) * CPB)
                        for c in range(b * CPB, (b + 1) * CPB):
                            eng.tensor_tensor(wob[:, c, :, :], ps[:, 4, 128:384].rearrange("p (g d) -> p g d", g=2),
                                              grow[:, b, 0:1, :].to_broadcast([P, 2, D]), ALU.mult)
                        eng.tensor_tensor(bob[:, cs, :], bo_n[:, None, :].to_broadcast([1, CPB, D]),
                                          grow[0:1, b, 0:1, :].to_broadcast([1, CPB, D]), ALU.mult)
                        eng.tensor_tensor(sdg[:, cs, :], ps[:, 6, None, 256:384].to_broadcast([P, CPB, D]),
                                          grow[:, B + b, 1:2, :].to_broadcast([P, CPB, D]), ALU.mult)
                    eng.wait_ge(turned, 2)
                    for b in range(B):
                        rows = slice(b * PR, (b + 1) * PR)
                        eng.tensor_tensor(whx[:, b, :], ps[:, 7, 128:256], grow[:, B + b, 0, :], ALU.mult)
                        eng.tensor_tensor(whs[rows, b, :], ps[rows, 7, 256:384], grow[rows, B + b, 0, :], ALU.mult)
                    step.close()

        def normalized(eng, dst, c):
            for k in range(4):
                last = eng.tensor_scalar(dst[:, k, :], x_sb[:, ds(c * 4 + k, 1), :], moments[:, ds(c * 4 + k, 1), 0:1],
                                         rstd[:, ds(c * 4 + k, 1)], ALU.subtract, ALU.mult)
            return last

        def rstd_block(n):
            with nc.Block() as block:
                @block.vector
                def _(eng):
                    eng.tensor_scalar(rstd[:, :], moments[:, :, 1], LN_EPS, None, ALU.add).then_inc(var_ready, 1)
                    eng.wait_ge(std_ready, n + 1)
                    step = Chain(eng, vector_steps)
                    step.straight()
                    step(eng.reciprocal(rstd[:, :], rstd[:, :]))
                    step(eng.scalar_tensor_tensor(nmr[:, :], moments[:, :, 0], -1.0, rstd[:, :], ALU.mult, ALU.mult))
                    step.close()

                @block.scalar
                def _(eng):
                    eng.wait_ge(var_ready, n + 1)
                    eng.activation(rstd[:, :], rstd[:, :], ACT.Sqrt).then_inc(std_ready, 1)

        rstd_block(0)

        NE = E0 + 1
        ffn_weights = ctx.enter_context(ExitStack())
        w1s = ffn_weights.enter_context(nc.sbuf_tensor("w1s", [P, NE, FF], F32))
        w2s = ffn_weights.enter_context(nc.sbuf_tensor("w2s", [P, NE, FK, D], F32))
        ld_f = sem("ld_f")

        with ExitStack() as tmp:
            def st(name, shape, dt=F32):
                return tmp.enter_context(nc.sbuf_tensor(name, shape, dt))

            xn = st("xn", [P, 2, 4, D])
            hT = st("hT", [P, 2, CHUNK])
            vp = st("vp", [P, 2, 4, H, 32])
            ex = st("ex", [P, 2, 2, CHUNK])
            qk = st("qk", [P, 4, 2, CHUNK])
            am = st("am", [P, 2, CHUNK])
            osb = st("osb", [P, 2, CHUNK])
            den = st("den", [P, CHUNK])
            on = st("on", [P, 2, CHUNK])

            xn_ready = sem("xn_ready")
            xnT_ready = sem("xnT_ready")
            hT_ready = sem("hT_ready")
            v_ps = sem("v_ps")
            v_ready = sem("v_ready")
            x_ready = sem("x_ready")
            e_ready = sem("e_ready")
            r_ready = sem("r_ready")
            feat_ready = sem("feat_ready")
            a_ready = sem("a_ready")
            am_ready = sem("am_ready")
            o_ready = sem("o_ready")
            osb_ready = sem("osb_ready")
            den_ps = sem("den_ps")
            den_sb = sem("den_sb")
            den_inv = sem("den_inv")
            on_ready = sem("on_ready")
            out_ps = sem("out_ps")
            x_added = sem("x_added")
            v_set = sem("v_set")

            def chunks(eng, body):
                body(0, 0, False, True)
                with eng.Fori(0, (NC - 2) // 2) as j:
                    body(j * 2 + 1, 1, True, True)
                    body(j * 2 + 2, 0, True, True)
                body(NC - 1, 1, True, False)

            with nc.Block() as block:
                @block.sync
                def _(eng):
                    eng.dma_start(w1s[:, 0:E0, :], t["L0_ffn_W1"].rearrange("e d f -> d e f")).then_inc(ld_f, 16)
                    eng.dma_start(w1s[:, E0, :], t["L0_ffn_Ws1"]).then_inc(ld_f, 16)
                    eng.dma_start(w2s[:, 0:E0, :, :],
                                  t["L0_ffn_W2"].rearrange("e (k p) d -> p e k d", p=P)).then_inc(ld_f, 16)
                    eng.dma_start(w2s[:, E0, :, :],
                                  t["L0_ffn_Ws2"].rearrange("(k p) d -> p k d", p=P)).then_inc(ld_f, 16)

                @block.gpsimd
                def _(eng):
                    eng.sem_inc(on_ready, 1)
                    eng.memset(vp[:, :, :, :, HD + 1:32], 0.0)
                    eng.memset(vp[:, :, :, :, HD:HD + 1], 1.0).then_inc(v_set, 1)

                    def normalize(i, g):
                        n = i * 2 + g
                        eng.wait_ge(den_inv, n * 2 + 2)
                        eng.wait_ge(osb_ready, n + 1)
                        eng.wait_ge(out_ps, i + 1)
                        eng.tensor_tensor(on[:, g, :], osb[:, g, :], den[:, :], ALU.mult).then_inc(on_ready, 1)

                    def body(i, u, prev, nxt):
                        for h in range(H):
                            if prev and h == 1:
                                normalize(i - 1, 0)
                            if prev and h == 4:
                                normalize(i - 1, 1)

                    chunks(eng, body)
                    normalize(NC - 1, 0)
                    normalize(NC - 1, 1)

                @block.scalar
                def _(eng):
                    def turn(i, u):
                        eng.wait_ge(xnT_ready, i + 1)
                        eng.activation(hT[:, u, :], bank(7), ACT.Identity, bias=shift[:, 0, 1, ds(i, 1)],
                                       scale=shift[:, 0, 0, ds(i, 1)]).then_inc(hT_ready, 1)

                    def keep_v(i, u):
                        eng.wait_ge(v_ps, i + 1)
                        eng.activation(vp[:, u, :, :, 0:HD].rearrange("p t h c -> p (t h) c"),
                                       bank(7).rearrange("p (a c) -> p a c", c=HD), ACT.Copy).then_inc(v_ready, 1)

                    def keep_o(i, g):
                        eng.wait_ge(o_ready, i * 2 + g + 1)
                        eng.wait_ge(on_ready, i * 2 + 1)
                        eng.activation(osb[:, g, :], bank(1), ACT.Copy).then_inc(osb_ready, 1)

                    def denominator(i, g):
                        eng.wait_ge(den_ps, i * 2 + g + 1)
                        eng.wait_ge(on_ready, i * 2 + g + 1)
                        eng.activation(den[:, :], bank(0), ACT.Copy, bias=1e-8).then_inc(den_sb, 1)

                    def body(i, u, prev, nxt):
                        for h in range(H):
                            q = i * H + h
                            if prev and h == 4:
                                denominator(i - 1, 1)
                            eng.wait_ge(x_ready, q + 1)
                            eng.wait_ge(feat_ready, q)
                            both = ex[:, h % 2, :, :].rearrange("p a n -> p (a n)")
                            eng.activation(both, ps[:, 2 + 2 * (h % 2):4 + 2 * (h % 2), :].rearrange("p a n -> p (a n)"),
                                           ACT.Relu, scale=-1.0).then_inc(r_ready, 1)
                            eng.wait_ge(r_ready, q + 1)
                            eng.activation(both, both, ACT.Exp, scale=-1.0).then_inc(e_ready, 1)
                            if prev and h == 0:
                                denominator(i - 1, 0)
                            if prev and h == 3:
                                keep_o(i - 1, 1)
                            if h == 6:
                                keep_o(i, 0)
                            if nxt and h == 5:
                                turn(i + 1, 1 - u)
                            if nxt and h == 7:
                                keep_v(i + 1, 1 - u)

                    eng.wait_ge(v_set, 1)
                    turn(0, 0)
                    keep_v(0, 0)
                    chunks(eng, body)
                    denominator(NC - 1, 0)
                    keep_o(NC - 1, 1)
                    denominator(NC - 1, 1)

                @block.vector
                def _(eng):
                    step = Chain(eng, vector_steps)
                    eng.sem_inc(feat_ready, 1)
                    eng.sem_inc(x_added, 1)

                    def normalize(i, u):
                        eng.wait_ge(xnT_ready, i)
                        normalized(eng, xn[:, u, :, :], i).then_inc(xn_ready, 1)

                    def inside_blocks(q, par):
                        eng.wait_ge(a_ready, q + 5)
                        eng.tensor_tensor(am[:, par, :].rearrange("p (t m) -> p t m", t=4),
                                          bank(6).rearrange("p (t m) -> p t m", t=4),
                                          blockmask[:, None, :].to_broadcast([P, 4, P]), ALU.mult).then_inc(am_ready, 1)

                    def invert(i, g, half):
                        if half == 0:
                            eng.wait_ge(den_sb, i * 2 + g + 1)
                        d = den[:, half * CHUNK // 2:(half + 1) * CHUNK // 2]
                        eng.reciprocal(d, d).then_inc(den_inv, 1)

                    def add(i):
                        eng.wait_ge(out_ps, i + 2)
                        xs = x_sb[:, ds(i * 4, 4), :]
                        eng.tensor_tensor(xs, xs, bank(0).rearrange("p (t d) -> p t d", t=4), ALU.add).then_inc(x_added, 1)
                        eng.wait_ge(x_added, i + 2)
                        step.body(i, 3)
                        token_moments(eng, step, i)

                    def body(i, u, prev, nxt):
                        for h in range(H):
                            q = i * H + h
                            if h >= 2 or prev:
                                inside_blocks(q - 2, h % 2)
                            eng.wait_ge(e_ready, q + 1)
                            eng.wait_ge(a_ready, q + 1)
                            eng.scalar_tensor_tensor(
                                qk[:, h % 4, :, :].rearrange("p a n -> p (a n)"),
                                ps[:, 2 + 2 * (h % 2):4 + 2 * (h % 2), :].rearrange("p a n -> p (a n)"), 0.0,
                                ex[:, h % 2, :, :].rearrange("p a n -> p (a n)"),
                                ALU.max, ALU.add).then_inc(feat_ready, 1)
                            if prev and h in (1, 2, 4, 5):
                                invert(i - 1, h // 4, 0 if h in (1, 4) else 1)
                            if nxt and h == 3:
                                normalize(i + 1, 1 - u)
                            if prev and h == 7:
                                add(i - 1)

                    normalize(0, 0)
                    chunks(eng, body)
                    inside_blocks(NC * H - 2, 0)
                    inside_blocks(NC * H - 1, 1)
                    for g in range(2):
                        for half in range(2):
                            invert(NC - 1, g, half)
                    add(NC - 1)
                    step.end(NC)

                @block.tensor
                def _(eng):
                    eng.sem_inc(out_ps, 1)
                    eng.sem_inc(a_ready, 4)
                    eng.sem_inc(am_ready, 1)

                    def turn(i, u):
                        eng.wait_ge(xn_ready, i + 1)
                        if not (type(i) is int and i == 0):
                            eng.wait_ge(v_ready, i)
                        for k in range(4):
                            last = eng.transpose(bank(7)[:, k * P:(k + 1) * P], xn[:, u, k, :], ident[:, :])
                        last.then_inc(xnT_ready, 1)

                    def values(i, u):
                        eng.wait_ge(hT_ready, i + 1)
                        for k in range(4):
                            last = eng.matmul(bank(7)[:, k * P:(k + 1) * P], hT[:, u, k * P:(k + 1) * P], wv[:, :],
                                              start=True, stop=True)
                        last.then_inc(v_ps, 1)

                    def features(i, u, h):
                        q = i * H + h
                        eng.wait_ge(feat_ready, q)
                        eng.matmul(bank(2 + 2 * (h % 2)), wf[:, 0, h, :], hT[:, u, :], start=True, stop=True)
                        eng.matmul(bank(3 + 2 * (h % 2)), wf[:, 1, h, :], hT[:, u, :], start=True,
                                   stop=True).then_inc(x_ready, 1)

                    def products(q, h):
                        eng.wait_ge(feat_ready, q + 2)
                        eng.wait_ge(am_ready, q + 1)
                        for k in range(4):
                            c = slice(k * P, (k + 1) * P)
                            last = eng.matmul(bank(6)[:, c], qk[:, h % 4, 1, c], qk[:, h % 4, 0, c], start=True, stop=True)
                        last.then_inc(a_ready, 1)

                    def outputs(q, i, u, h):
                        eng.wait_ge(am_ready, q + 2)
                        if h % 4 == 0:
                            eng.wait_ge(osb_ready, i * 2 + h // 4)
                            eng.wait_ge(v_ready, i + 1)
                        a = h % 4
                        for k in range(4):
                            last = eng.matmul(ps[32 * a:32 * a + 32, 1, k * P:(k + 1) * P], vp[:, u, k, h, :],
                                              am[:, h % 2, k * P:(k + 1) * P], start=True, stop=True)
                        if a == 3:
                            last.then_inc(o_ready, 1)

                    def denominator(i, g):
                        eng.wait_ge(osb_ready, i * 2 + g + 1)
                        eng.matmul(bank(0), dsel[:, :], osb[:, g, :], start=True, stop=True).then_inc(den_ps, 1)

                    def project(i):
                        eng.wait_ge(on_ready, i * 2 + 3)
                        for k in range(4):
                            c = slice(k * P, (k + 1) * P)
                            for g in range(2):
                                eng.matmul(bank(0)[:, c], on[:, g, c], wob[:, ds(i, 1), g, :].rearrange("p a d -> p (a d)"),
                                           start=(g == 0), stop=False)
                            last = eng.matmul(bank(0)[:, c], ones[0:1, :], bob[:, ds(i, 1), :].rearrange("p a d -> p (a d)"),
                                              start=False, stop=True)
                        last.then_inc(out_ps, 1)

                    def body(i, u, prev, nxt):
                        for h in range(H):
                            q = i * H + h
                            if prev and h == 4:
                                eng.wait_ge(den_sb, i * 2 - 1)
                                denominator(i - 1, 1)
                            features(i, u, h)
                            if prev and h == 7:
                                eng.wait_ge(den_sb, i * 2)
                                project(i - 1)
                            if h >= 2 or prev:
                                products(q - 2, (h - 2) % H)
                            if h >= 3:
                                outputs(q - 3, i, u, h - 3)
                            elif prev:
                                outputs(q - 3, i - 1, 1 - u, h + H - 3)
                            if prev and h == 0:
                                eng.wait_ge(x_added, i)
                                denominator(i - 1, 0)
                            if nxt and h == 4:
                                turn(i + 1, 1 - u)
                            if nxt and h == 6:
                                values(i + 1, 1 - u)

                    turn(0, 0)
                    values(0, 0)
                    chunks(eng, body)
                    last_q = NC * H - 1
                    products(last_q - 1, H - 2)
                    outputs(last_q - 2, NC - 1, 1, H - 3)
                    products(last_q, H - 1)
                    outputs(last_q - 1, NC - 1, 1, H - 2)
                    eng.wait_ge(x_added, NC)
                    denominator(NC - 1, 0)
                    outputs(last_q, NC - 1, 1, H - 1)
                    eng.wait_ge(den_sb, NC * 2 - 1)
                    denominator(NC - 1, 1)
                    eng.wait_ge(den_sb, NC * 2)
                    project(NC - 1)
        rstd_block(1)

        with ExitStack() as tmp:
            def st(name, shape, dt=F32):
                return tmp.enter_context(nc.sbuf_tensor(name, shape, dt))

            CAP0 = 2 * T
            h2T = st("h2T", [P, T])
            b2m = st("b2m", [P, NT // 2, D])
            bs2 = st("bs2", [P, D])
            gateT = st("gateT", [P, NT, E0])
            flag = st("flag", [P, 2 * P])
            emask = st("emask", [P, E0])
            crow = st("crow", [P, 1])
            hx0_stored = [sem(f"hx0_stored{u}") for u in range(2)]
            gflat = st("gflat", [P, 2 * P])
            N_LDF = 5 + E0
            with ExitStack() as tmp2:
                def st2(name, shape, dt=F32):
                    return tmp2.enter_context(nc.sbuf_tensor(name, shape, dt))

                pi = st2("pi", [P, 1], I32)
                scores = st2("scores", [P, NT, E0])
                smax = st2("smax", [P, NT])
                ssum = st2("ssum", [P, NT])
                sperm = st2("sperm", [P, 2, E0, NT // 2])
                sflat = st2("sflat", [P, 2 * P])
                above = st2("above", [P, 2 * P])
                equal = st2("equal", [P, 2 * P])
                rank = st2("rank", [P, 2 * P])
                b2r = st2("b2r", [P, D])
                cm3 = st2("cm3", [P, E0, NT // 2])
                cmask = st2("cmask", [P, NT // 2])
                cur = st2("cur", [P, 1], I32)
                BITS, DB = 30, 3
                NCAND, ROUNDS_T = (1 << DB) - 1, BITS // DB
                cand = st2("cand", [P, NCAND], I32)
                digit = st2("digit", [P, NCAND], I32)
                unit = st2("unit", [P, 1])
                hit = st2("hit", [P, NCAND, 2 * P], BF16)
                enough = st2("enough", [P, NCAND])
                chosen = st2("chosen", [P, 1])
                inc = st2("inc", [P, 1], I32)
                cnt = st2("cnt", [P, NCAND])
                n_above = st2("n_above", [P, 1])
                n_equal = st2("n_equal", [P, 1])
                need = st2("need", [P, 1])
                tmp3 = tmp2.enter_context(ExitStack())
                xn = tmp3.enter_context(nc.sbuf_tensor("xn2", [P, 2, 4, D], F32))
                rows = tmp3.enter_context(nc.sbuf_tensor("rows0", [P, 2, 4, D], F32))
                h2c = tmp3.enter_context(nc.sbuf_tensor("h2c", [P, 2, CHUNK], F32))

                bxn_ready = sem("bxn_ready")
                b_part = sem("b_part")
                rows_ready = sem("rows_ready")
                bxnT_ready = sem("bxnT_ready")
                bh_ready = sem("bh_ready")
                lg_ps = sem("lg_ps")
                lg_sb = sem("lg_sb")
                cm_ready = sem("cm_ready")
                with nc.Block() as block:
                    @block.sync
                    def _(eng):
                        for u in range(2):
                            eng.sem_inc(hx0_stored[u], 16)
                        eng.dma_start(bs2[:, :], t["L0_ffn_bs2"][None, :].to_broadcast([P, D])).then_inc(ld_f, 16)
                        n = P // E0
                        for e in range(E0):
                            eng.dma_start(b2r[e * n:(e + 1) * n, :],
                                          t["L0_ffn_b2"][e:e + 1, :].to_broadcast([n, D])).then_inc(ld_f, 16)
                        with eng.Fori(0, NC // 2) as j:
                            for u in range(2):
                                i = j * 2 + u
                                eng.wait_ge(rows_ready, i + 1)
                                eng.dma_start(hx0_v[:, ds(i * 4, 4), 0:D], rows[:, u, :, :]).then_inc(hx0_stored[u], 16)
                        for u in range(2):
                            eng.wait_ge(hx0_stored[u], 16 * (NC // 2) + 16)

                    @block.gpsimd
                    def _(eng):
                        step = Chain(eng, gpsimd_steps)
                        step.straight()
                        eng.iota(pi[:, :], pattern=[[1, 1]], base=0, channel_multiplier=1)
                        step(eng.memset(cm3[:, :, :], 0.0))
                        eng.affine_select(out=cm3[:, :, :], in_=cm3[:, :, :], compare_op=ALU.not_equal, fill=1.0, base=0,
                                          pattern=[[-NT // 2, E0], [-1, NT // 2]], channel_multiplier=1).then_inc(cm_ready, 1)
                        step.close()
                        with eng.Fori(0, NC // 2) as j:
                            for u in range(2):
                                i = j * 2 + u
                                eng.wait_ge(bxn_ready, i + 1)
                                eng.wait_ge(hx0_stored[u], 16 * j + 16)
                                r = rows[:, u, :, :]
                                eng.tensor_tensor(r, xn[:, u, :, :], schunk[:, 0, ds(i, 1), 1, :].to_broadcast([P, 4, D]),
                                                  ALU.mult).then_inc(b_part, 1)

                    @block.vector
                    def _(eng):
                        eng.sem_inc(b_part, 1)

                        def body(i, u, prev, nxt):
                            if nxt:
                                if prev:
                                    eng.wait_ge(bxnT_ready, i)
                                    eng.wait_ge(b_part, i + 1)
                                normalized(eng, xn[:, 1 - u, :, :], i + 1).then_inc(bxn_ready, 1)
                            eng.wait_ge(b_part, i + 2)
                            r = rows[:, u, :, :]
                            eng.tensor_tensor(r, r, schunk[:, 0, ds(i, 1), 0, :].to_broadcast([P, 4, D]),
                                              ALU.add).then_inc(rows_ready, 1)

                        normalized(eng, xn[:, 0, :, :], 0).then_inc(bxn_ready, 1)
                        chunks(eng, body)

                    @block.tensor
                    def _(eng):
                        def turn(i, u):
                            eng.wait_ge(bxn_ready, i + 1)
                            for k in range(4):
                                last = eng.transpose(bank(u)[:, k * P:(k + 1) * P], xn[:, u, k, :], ident[:, :])
                            last.then_inc(bxnT_ready, 1)

                        def body(i, u, prev, nxt):
                            if nxt:
                                turn(i + 1, 1 - u)
                            eng.wait_ge(bh_ready, i + 1)
                            eng.wait_ge(lg_sb, i + 1)
                            for k in range(4):
                                last = eng.matmul(ps[:, 2 + u, k * E0:(k + 1) * E0], h2c[:, u, k * P:(k + 1) * P],
                                                  gw0[:, :], start=True, stop=True)
                            last.then_inc(lg_ps, 1)

                        eng.sem_inc(lg_ps, 1)
                        turn(0, 0)
                        chunks(eng, body)

                    @block.scalar
                    def _(eng):
                        def keep(i, u):
                            eng.wait_ge(bxnT_ready, i + 1)
                            eng.wait_ge(lg_ps, i)
                            for dst in (h2T[:, ds(i * CHUNK, CHUNK)], h2c[:, u, :]):
                                last = eng.activation(dst, bank(u), ACT.Identity, bias=shift[:, 0, 3, ds(i, 1)],
                                                      scale=shift[:, 0, 2, ds(i, 1)])
                            last.then_inc(bh_ready, 1)

                        def body(i, u, prev, nxt):
                            if nxt:
                                keep(i + 1, 1 - u)
                            eng.wait_ge(lg_ps, i + 2)
                            eng.activation(scores[:, ds(i * 4, 4), :],
                                           ps[:, 2 + u, 0:4 * E0].rearrange("p (k e) -> p k e", k=4),
                                           ACT.Copy).then_inc(lg_sb, 1)

                        eng.sem_inc(lg_sb, 2)
                        keep(0, 0)
                        chunks(eng, body)

                ex_ready = sem("ex_ready")
                shifted = sem("shifted")
                perm_ready = sem("perm_ready")
                flat_ps = sem("flat_ps")
                cnt_ready = sem("cnt_ready")
                cnt_ps = sem("cnt_ps")
                gate_ready = sem("gate_ready")
                gate_ps = sem("gate_ps")
                tmp3.close()
                hid = st2("hid_s", [P, 2, FK, CHUNK])
                facc = st2("facc", [P, 4, D])
                sh1_ps = sem("sh1_ps")
                shid_ready = sem("shid_ready")
                sy_ps = sem("sy_ps")
                sy_used = sem("sy_used")
                assert NC < ROUNDS_T
                with nc.Block() as block:
                    @block.scalar
                    def _(eng):
                        eng.wait_ge(shifted, 1)
                        eng.activation(scores[:, :, :], scores[:, :, :], ACT.Exp).then_inc(ex_ready, 1)
                        eng.sem_inc(shid_ready, 1)
                        with eng.Fori(0, NC // 2) as j:
                            for u in range(2):
                                i = j * 2 + u
                                for k in range(FK):
                                    eng.wait_ge(sh1_ps, i * FK + k + 1)
                                    if k == 0:
                                        eng.wait_ge(sy_ps, i + 1)
                                    col = E0 * FK + k
                                    eng.activation(hid[:, u, k, :], bank(k), ACT.Gelu_apprx_tanh,
                                                   bias=b1c[:, col:col + 1]).then_inc(shid_ready, 1)

                    @block.vector
                    def _(eng):
                        step = Chain(eng, vector_steps)
                        step.straight()
                        step(eng.tensor_reduce(smax[:, :], scores[:, :, :], AX, ALU.max))
                        eng.tensor_tensor(scores[:, :, :], scores[:, :, :],
                                          smax[:, :, None].to_broadcast([P, NT, E0]), ALU.subtract).then_inc(shifted, 1)
                        eng.wait_ge(ex_ready, 1)
                        step(eng.tensor_reduce(ssum[:, :], scores[:, :, :], AX, ALU.add))
                        step(eng.reciprocal(ssum[:, :], ssum[:, :]))
                        for j in range(2):
                            last = eng.tensor_tensor(
                                sperm[:, j, :, :].rearrange("p e c -> p c e"),
                                scores[:, :, :].rearrange("p (c j) e -> p j c e", j=2)[:, j, :, :],
                                ssum[:, :].rearrange("p (c j) -> p j c", j=2)[:, j, :, None].to_broadcast([P, NT // 2, E0]),
                                ALU.mult)
                        last.then_inc(perm_ready, 1)
                        eng.memset(cur[:, :], 0)
                        for m in range(1, NCAND + 1):
                            eng.memset(digit[:, m - 1:m], m << (BITS - DB))
                            eng.memset(cand[:, m - 1:m], m << (BITS - DB))
                        step(eng.memset(unit[:, :], float(1 << (BITS - DB))))
                        eng.wait_ge(flat_ps, 1)
                        step(eng.tensor_copy(sflat[:, :], ps[:, 6, 0:2 * P]))
                        step.close()
                        def add_shared(i, u):
                            eng.wait_ge(sy_ps, i + 3)
                            fa = facc[:, :, :]
                            step(eng.tensor_tensor(fa, bank(4 + u).rearrange("p (k d) -> p k d", k=4),
                                                   bs2[:, None, :].to_broadcast([P, 4, D]), ALU.add))
                            eng.sem_inc(sy_used, 1)
                            step(eng.tensor_tensor(fa, fa, gchunk[:, 0, ds(i, 1), :].to_broadcast([P, 4, D]), ALU.mult))
                            xs = x_sb[:, ds(i * 4, 4), :]
                            step(eng.tensor_tensor(xs, xs, fa, ALU.add))

                        def search(k, shared):
                            for m in range(NCAND):
                                last = eng.tensor_scalar(hit[:, m, :], sflat[:, :], cand[:, m:m + 1].bitcast(F32), 0.0,
                                                         ALU.is_ge, ALU.add, accum_out=cnt[:, m:m + 1])
                            last.then_inc(cnt_ready, 1)
                            step(eng.tensor_scalar(digit[:, :], digit[:, :], DB, None, ALU.logical_shift_right))
                            shared()
                            eng.wait_ge(cnt_ps, k + 1)
                            step(eng.tensor_scalar(enough[:, :], ps[:, 7, 0:NCAND], float(CAP0), 0.0, ALU.is_ge, ALU.add,
                                                   accum_out=chosen[:, :]))
                            step(eng.tensor_scalar(inc[:, :], chosen[:, :], unit[:, :], None, ALU.mult))
                            eng.tensor_scalar(unit[:, :], unit[:, :], 1.0 / (1 << DB), None, ALU.mult)
                            step(eng.tensor_tensor(cur[:, :], cur[:, :], inc[:, :], ALU.bitwise_or))
                            step(eng.tensor_tensor(cand[:, :], cur[:, 0:1].to_broadcast([P, NCAND]), digit[:, :],
                                                   ALU.bitwise_or))

                        step.straight()
                        search(0, lambda: None)
                        step.close()
                        with eng.Fori(0, NC // 2) as j:
                            for u in range(2):
                                step.body(j * 2 + u, 8)
                                search(j * 2 + u + 1, lambda: add_shared(j * 2 + u, u))
                        step.end(NC)
                        step.straight()
                        for k in range(NC + 1, ROUNDS_T):
                            search(k, lambda: None)
                        step.close()
                        step.straight()
                        thr = cur[:, :].bitcast(F32)
                        eng.tensor_scalar(above[:, :], sflat[:, :], thr, 0.0, ALU.is_gt, ALU.add, accum_out=n_above[:, :])
                        step(eng.tensor_scalar(equal[:, :], sflat[:, :], thr, 0.0, ALU.is_equal, ALU.add,
                                               accum_out=n_equal[:, :]))
                        eng.sem_inc(cnt_ready, 1)
                        step(eng.tensor_tensor_scan(rank[:, :], ones[:, 0:1].to_broadcast([P, 2 * P]), equal[:, :], 0.0,
                                                    ALU.mult, ALU.add))
                        eng.wait_ge(cnt_ps, ROUNDS_T + 1)
                        step(eng.tensor_scalar(need[:, :], ps[:, 7, 0:1], -1.0, float(CAP0), ALU.mult, ALU.add))
                        step(eng.tensor_tensor(need[:, :], need[:, :], ps[:, 7, 1:2], ALU.subtract))
                        step(eng.scalar_tensor_tensor(rank[:, :], rank[:, :], need[:, :], equal[:, :], ALU.is_le, ALU.mult))
                        step(eng.tensor_tensor(flag[:, :], above[:, :], rank[:, :], ALU.add))
                        eng.tensor_tensor(gflat[:, :], flag[:, :], sflat[:, :], ALU.mult).then_inc(gate_ready, 1)
                        eng.wait_ge(cm_ready, 1)
                        eng.wait_ge(ld_f, 16 * N_LDF)
                        step(eng.tensor_reduce(cmask[:, :], cm3[:, :, :].rearrange("p e c -> p c e"), AX, ALU.add))
                        step(eng.tensor_tensor(b2m[:, :, :], b2r[:, None, :].to_broadcast([P, NT // 2, D]),
                                               cmask[:, :, None].to_broadcast([P, NT // 2, D]), ALU.mult))
                        step(eng.tensor_reduce(emask[:, :], cm3[:, :, :], AX, ALU.add))
                        step(eng.tensor_scalar(pi[:, :], pi[:, :], NT // 2 - 1, None, ALU.bitwise_and))
                        step(eng.tensor_copy(crow[:, :], pi[:, :]))
                        eng.wait_ge(gate_ps, 1)
                        for j in range(2):
                            eng.tensor_copy(gateT[:, :, :].rearrange("p (c j) e -> p e c j", j=2)[:, :, :, j],
                                            ps[:, 6, j * P:(j + 1) * P].rearrange("p (e c) -> p e c", e=E0))
                        step.close()

                    @block.tensor
                    def _(eng):
                        eng.wait_ge(perm_ready, 1)
                        for j in range(2):
                            last = eng.transpose(ps[:, 6, j * P:(j + 1) * P],
                                                 sperm[:, j, :, :].rearrange("p e c -> p (e c)"), ident[:, :])
                        last.then_inc(flat_ps, 1)
                        def count(k):
                            eng.wait_ge(cnt_ready, k + 1)
                            eng.matmul(ps[:, 7, 0:NCAND], ones[:, :], cnt[:, :], start=True, stop=True).then_inc(cnt_ps, 1)

                        def up(i):
                            for k in range(FK):
                                eng.wait_ge(shid_ready, (i - 1) * FK + k + 2)
                                eng.matmul(bank(k), w1s[:, E0, k * P:(k + 1) * P], h2T[:, ds(i * CHUNK, CHUNK)],
                                           start=True, stop=True).then_inc(sh1_ps, 1)

                        def down(i, u):
                            eng.wait_ge(shid_ready, (i + 1) * FK + 1)
                            eng.wait_ge(sy_used, i + 1)
                            for c in range(4):
                                for k in range(FK):
                                    last = eng.matmul(bank(4 + u)[:, c * P:(c + 1) * P],
                                                      hid[:, u, k, c * P:(c + 1) * P], w2s[:, E0, k, :],
                                                      start=(k == 0), stop=(k == FK - 1))
                            last.then_inc(sy_ps, 1)

                        def body(i, u, prev, nxt):
                            count(i)
                            if nxt:
                                up(i + 1)
                            down(i, u)

                        eng.sem_inc(sy_ps, 2)
                        eng.sem_inc(sy_used, 2)
                        eng.wait_ge(ld_f, 16 * N_LDF)
                        for k in range(FK):
                            eng.matmul(bank(k), w1s[:, E0, k * P:(k + 1) * P], h2T[:, 0:CHUNK],
                                       start=True, stop=True).then_inc(sh1_ps, 1)
                        chunks(eng, body)
                        for k in range(NC, ROUNDS_T):
                            count(k)
                        eng.wait_ge(cnt_ready, ROUNDS_T + 1)
                        eng.matmul(ps[:, 7, 0:1], ones[:, :], n_above[:, :], start=True, stop=True)
                        eng.matmul(ps[:, 7, 1:2], before[:, :], n_equal[:, :], start=True, stop=True).then_inc(cnt_ps, 1)
                        eng.wait_ge(gate_ready, 1)
                        for j in range(2):
                            last = eng.transpose(ps[:, 6, j * P:(j + 1) * P], gflat[:, j * P:(j + 1) * P], ident[:, :])
                        last.then_inc(gate_ps, 1)

            TS = 256
            NTL = CAP0 // TS + E0
            NG0 = NTL * TS // P
            NBL = NTL * TS // CHUNK
            W = 4 + E0
            idx0 = st("idx0", [P, NG0], I32)
            info = st("info", [P, NG0, W])
            tile_e = st("tile_e", [P, NTL], I32)
            hx0_gates = sem("hx0_gates")
            with ExitStack() as tmp2:
                def st2(name, shape, dt=F32):
                    return tmp2.enter_context(nc.sbuf_tensor(name, shape, dt))

                incl = st2("incl", [P, 2 * P], BF16)
                tot = st2("tot", [P, 1])
                tot_e = st2("tot_e", [P, E0])
                cnt_e = st2("cnt_e", [P, E0])
                tiles_i = st2("tiles_i", [P, E0], I32)
                tiles = st2("tiles", [P, E0])
                tiles_end = st2("tiles_end", [P, E0])
                cnt_end = st2("cnt_end", [P, E0])
                base = st2("base", [P, E0])
                row_start = st2("row_start", [P, 1])
                row_end = st2("row_end", [P, 1])
                rs_i = st2("rs_i", [P, 3], I32)
                blk_start = st2("blk_start", [P, NBL])
                blk_end = st2("blk_end", [P, NBL])
                pay = st2("pay0", [P, W], BF16)
                io_i = st2("io_i0", [P, CHUNK], I32)
                io512 = st2("io512", [P, CHUNK])
                bo_i = st2("bo_i", [P, NBL], I32)
                blk = st2("blk", [P, NBL])
                so_i = st2("so_i", [P, NG0 + 1], I32)
                slot = st2("slot", [P, NG0 + 1])
                inside = st2("inside", [P, NBL, CHUNK], BF16)
                phalf = st2("phalf", [P, NG0])
                scr_a = st2("scr_a", [P, 2, 2, 2 * P])
                oh = st2("oh0", [P, NBL, CHUNK], BF16)
                past = st2("past", [P, NTL, E0])
                tile_f = st2("tile_f", [P, NTL])
                place = st2("place", [P, NG0])
                scr = st2("scr", [P, 2, 2 * P])
                fi = st2("fi", [P, NG0])

                io_ready = sem("io_ready")
                tot_ready = sem("tot_ready")
                tot_ps = sem("tot_ps")
                oh_ready = sem("oh0_ready")
                info_ps = sem("info_ps")
                incl_ps = sem("incl_ps")
                incl_used = [sem(f"incl_used{a}") for a in range(2)]
                edges_ready = sem("edges_ready")
                inside_ready = sem("inside_ready")
                place_ready = sem("place_ready")
                LB = 6
                with nc.Block() as block:
                    @block.sync
                    def _(eng):
                        eng.dma_start(hx0_v[:, :, D:HW0], gateT[:, :, :]).then_inc(hx0_gates, 16)

                    @block.gpsimd
                    def _(eng):
                        step = Chain(eng, gpsimd_steps)
                        step.straight()
                        eng.iota(io_i[:, :], pattern=[[1, CHUNK]], base=0, channel_multiplier=0)
                        eng.iota(bo_i[:, :], pattern=[[CHUNK, NBL]], base=0, channel_multiplier=0)
                        step(eng.iota(so_i[:, 0:NG0], pattern=[[P, NG0]], base=0, channel_multiplier=1))
                        eng.tensor_copy(io512[:, :], io_i[:, :])
                        eng.tensor_copy(blk[:, :], bo_i[:, :])
                        step(eng.tensor_copy(slot[:, 0:NG0], so_i[:, 0:NG0]))
                        step.close()
                        eng.sem_inc(io_ready, 1)
                        eng.wait_ge(edges_ready, 1)
                        for b in range(2, NBL, 3):
                            eng.tensor_scalar(inside[:, b, :], io512[:, :], blk_start[:, b:b + 1], None,
                                              ALU.is_ge).then_inc(inside_ready, 1)

                    @block.tensor
                    def _(eng):
                        eng.wait_ge(tot_ready, 1)
                        eng.matmul(ps[:, 7, 0:E0], ones[:, :], tot_e[:, :], start=True, stop=True)
                        eng.matmul(ps[:, 7, E0:E0 + 1], before[:, :], tot[:, :], start=True, stop=True).then_inc(tot_ps, 1)
                        eng.wait_ge(oh_ready, 1)
                        for g in range(NG0):
                            b, c = divmod(g, NG0 // 2)
                            last = eng.matmul(ps[:, 6 + b, c * W:(c + 1) * W],
                                              oh[:, g // 4, (g % 4) * P:(g % 4 + 1) * P], pay[:, :],
                                              start=True, stop=True)
                        last.then_inc(info_ps, 1)
                        for n in range(NG0 // 2):
                            if n >= LB:
                                eng.wait_ge(incl_used[n % 2], (n - LB) // 2 + 1)
                            for a in range(2):
                                g = 2 * n + a
                                last = eng.matmul(bank(n % LB)[:, a * 256:(a + 1) * 256],
                                                  oh[:, g // 4, (g % 4) * P:(g % 4 + 1) * P], incl[:, :],
                                                  start=True, stop=True)
                            last.then_inc(incl_ps, 1)

                    @block.scalar
                    def _(eng):
                        eng.wait_ge(place_ready, 1)
                        for n in range(1, NG0 // 2, 2):
                            eng.wait_ge(incl_ps, n + 1)
                            if n >= 5:
                                eng.wait_ge(incl_used[1], n // 2 - 1)
                            for a in range(2):
                                g = 2 * n + a
                                last = eng.activation(scr_a[:, n // 2 % 2, a, :], bank(n % LB)[:, a * 256:(a + 1) * 256],
                                                      ACT.Sign, bias=phalf[:, g:g + 1], scale=-1.0,
                                                      accum_out=fi[:, g:g + 1])
                            last.then_inc(incl_used[1], 1)

                    @block.vector
                    def _(eng):
                        step = Chain(eng, vector_steps)
                        step.straight()
                        eng.wait_ge(io_ready, 1)
                        step(eng.tensor_tensor_scan(incl[:, :], ones[:, 0:1].to_broadcast([P, 2 * P]), flag[:, :], 0.0,
                                                    ALU.mult, ALU.add))
                        step(eng.tensor_copy(tot[:, :], incl[:, 2 * P - 1:2 * P]))
                        step(eng.tensor_scalar(tot_e[:, :], emask[:, :], tot[:, :], None, ALU.mult))
                        eng.sem_inc(tot_ready, 1)
                        eng.wait_ge(tot_ps, 1)
                        step(eng.tensor_copy(cnt_e[:, :], ps[:, 7, 0:E0]))
                        step(eng.tensor_scalar(tiles_i[:, :], cnt_e[:, :], float(TS - 1), None, ALU.add))
                        step(eng.tensor_scalar(tiles_i[:, :], tiles_i[:, :], 8, None, ALU.logical_shift_right))
                        step(eng.tensor_copy(tiles[:, :], tiles_i[:, :]))
                        one8 = ones[:, 0:1].to_broadcast([P, E0])
                        eng.tensor_tensor_scan(tiles_end[:, :], one8, tiles[:, :], 0.0, ALU.mult, ALU.add)
                        step(eng.tensor_tensor_scan(cnt_end[:, :], one8, cnt_e[:, :], 0.0, ALU.mult, ALU.add))
                        eng.tensor_tensor(base[:, :], tiles_end[:, :], tiles[:, :], ALU.subtract)
                        step(eng.tensor_tensor(cnt_end[:, :], cnt_end[:, :], cnt_e[:, :], ALU.subtract))
                        step(eng.scalar_tensor_tensor(base[:, :], base[:, :], float(TS), cnt_end[:, :],
                                                      ALU.mult, ALU.subtract))
                        step(eng.tensor_tensor(base[:, :], base[:, :], emask[:, :], ALU.mult))
                        step(eng.tensor_reduce(row_start[:, :], base[:, :], AX, ALU.add))
                        step(eng.tensor_tensor(row_start[:, :], row_start[:, :], ps[:, 7, E0:E0 + 1], ALU.add))
                        step(eng.tensor_tensor(row_end[:, :], row_start[:, :], tot[:, :], ALU.add))
                        step(eng.tensor_copy(rs_i[:, 0:1], row_start[:, :]))
                        eng.tensor_scalar(rs_i[:, 1:2], rs_i[:, 0:1], 8, None, ALU.logical_shift_right)
                        step(eng.tensor_scalar(rs_i[:, 2:3], rs_i[:, 0:1], 255, None, ALU.bitwise_and))
                        eng.tensor_copy(pay[:, 0:1], crow[:, :])
                        eng.tensor_copy(pay[:, 1:3], rs_i[:, 1:3])
                        eng.tensor_copy(pay[:, 3:4], ones[:, 0:1])
                        eng.tensor_copy(pay[:, 4:W], emask[:, :])
                        eng.tensor_scalar(blk_start[:, :], blk[:, :], -1.0, row_start[:, :], ALU.mult, ALU.add)
                        step(eng.tensor_scalar(blk_end[:, :], blk[:, :], -1.0, row_end[:, :], ALU.mult, ALU.add))
                        eng.sem_inc(edges_ready, 1)
                        step(eng.tensor_tensor(past[:, :, :], io512[:, 0:NTL, None].to_broadcast([P, NTL, E0]),
                                               tiles_end[:, None, :].to_broadcast([P, NTL, E0]), ALU.is_ge))
                        step(eng.tensor_reduce(tile_f[:, :], past[:, :, :], AX, ALU.add))
                        step(eng.tensor_scalar(tile_e[:, :], tile_f[:, :], float(E0 - 1), None, ALU.min))

                        for b in range(NBL):
                            if b % 3 == 2:
                                eng.wait_ge(inside_ready, b // 3 + 1)
                            else:
                                step(eng.tensor_scalar(inside[:, b, :], io512[:, :], blk_start[:, b:b + 1], None, ALU.is_ge))
                            last = eng.scalar_tensor_tensor(oh[:, b, :], io512[:, :], blk_end[:, b:b + 1],
                                                            inside[:, b, :], ALU.is_lt, ALU.mult)
                        step(last)
                        eng.sem_inc(oh_ready, 1)
                        eng.wait_ge(info_ps, 1)
                        for b in range(2):
                            last = eng.tensor_copy(info[:, b * (NG0 // 2):(b + 1) * (NG0 // 2), :].rearrange("p g w -> p (g w)"),
                                                   ps[:, 6 + b, 0:NG0 // 2 * W])
                        step(last)
                        step(eng.scalar_tensor_tensor(place[:, :], info[:, :, 1], -256.0, slot[:, 0:NG0], ALU.mult, ALU.add))
                        step(eng.tensor_tensor(place[:, :], place[:, :], info[:, :, 2], ALU.subtract))
                        step(eng.tensor_scalar(phalf[:, :], place[:, :], 0.5, None, ALU.add))
                        eng.sem_inc(place_ready, 1)

                        def look_up(n):
                            eng.wait_ge(incl_ps, n + 1)
                            for a in range(2):
                                g = 2 * n + a
                                last = eng.tensor_scalar(scr[:, a, :], bank(n % LB)[:, a * 256:(a + 1) * 256],
                                                         place[:, g:g + 1], 0.0, ALU.is_le, ALU.add,
                                                         accum_out=fi[:, g:g + 1])
                            step(last)
                            eng.sem_inc(incl_used[0], 1)

                        for n in range(0, NG0 // 2, 2):
                            look_up(n)
                        eng.wait_ge(incl_used[1], NG0 // 4)
                        odd = fi[:, :].rearrange("p (n h a) -> p n h a", h=2, a=2)[:, :, 1, :]
                        step(eng.tensor_scalar(odd, odd, 0.5, 128.0, ALU.mult, ALU.add))
                        step(eng.scalar_tensor_tensor(fi[:, :], info[:, :, 0], 256.0, fi[:, :], ALU.mult, ALU.add))
                        step(eng.tensor_scalar(row_end[:, :], slot[:, 0:1], float(T - 256), None, ALU.add))
                        step(eng.tensor_scalar(place[:, :], info[:, :, 3], -1.0, 1.0, ALU.mult, ALU.add))
                        step(eng.tensor_scalar(place[:, :], place[:, :], row_end[:, :], None, ALU.mult))
                        step(eng.tensor_tensor(idx0[:, :], fi[:, :], place[:, :], ALU.add))
                        step.close()

            with ExitStack() as tmp2:
                def st2(name, shape, dt=F32):
                    return tmp2.enter_context(nc.sbuf_tensor(name, shape, dt))

                KT = TS // P
                cell = st2("cell", [P, 4], I32)
                gath = st2("gath0", [P, 4, KT, HW0])
                gT = st2("gT0", [P, 2, TS])
                w1t = st2("w1t", [P, 2, FF])
                b1t = st2("b1t", [P, 2, FK])
                hid = st2("hid_e", [P, 2, FK, TS])
                gm = st2("gm", [P, 2, KT, E0])
                gv = st2("gv", [P, 2, KT])
                ysc = st2("ysc0", [P, 2, KT, D])
                f_gathered = [sem(f"f_gathered{s}") for s in range(4)]
                ft_ps = sem("ft_ps")
                fT_ready = sem("fT_ready")
                fw_cell = sem("fw_cell")
                fw_ready = sem("fw_ready")
                fu_ps = sem("fu_ps")
                fh_ready = sem("fh_ready")
                fy_ps = sem("fy_ps")
                fg_part = sem("fg_part")
                f_gated = sem("f_gated")
                fs_ready = sem("fs_ready")
                f_added = [sem(f"f_added{a}") for a in range(KT)]

                def early(n, k):
                    return type(n) is int and n < k

                def tile_rounds(eng, body):
                    for s in range(4):
                        body(s, s)
                    with eng.Fori(1, NTL // 4 - 1) as j:
                        for s in range(4):
                            body(j * 4 + s, s)
                    for s in range(4):
                        body(NTL - 4 + s, s)

                def late(n, k):
                    return type(n) is int and n + k >= NTL

                with nc.Block() as block:
                    @block.gpsimd
                    def _(eng):
                        eng.wait_ge(hx0_gates, 16)
                        eng.wait_ge(acc0_zeroed, 48)
                        for n in range(-3, NTL):
                            if n + 3 >= 4 and n + 3 < NTL:
                                eng.wait_ge(ft_ps, n)
                                eng.wait_ge(f_gated, n)
                            if n + 3 < NTL:
                                for k in range(KT):
                                    g = (n + 3) * KT + k
                                    eng.indirect_dma_start(out=gath[:, (n + 3) % 4, k, :], out_offset=None, in_=hx0,
                                                           in_offset=bass.IndirectOffsetOnAxis(ap=idx0[:, g:g + 1], axis=0)
                                                           ).then_inc(f_gathered[(n + 3) % 4], 16)
                            if n >= 0:
                                eng.wait_ge(fs_ready, n + 1)
                                for k in range(KT):
                                    if n >= 1:
                                        eng.wait_ge(f_added[k], n * 16)
                                    g = n * KT + k
                                    eng.indirect_dma_start(out=acc0[k],
                                                           out_offset=bass.IndirectOffsetOnAxis(ap=idx0[:, g:g + 1], axis=0),
                                                           in_=ysc[:, n % 2, k, :], in_offset=None,
                                                           compute_op=ALU.add).then_inc(f_added[k], 16)

                    @block.tensor
                    def _(eng):
                        def turn(n, s):
                            eng.wait_ge(f_gathered[s], (n - s) * (KT * 4) + KT * 16)
                            if not early(n, 1):
                                eng.wait_ge(fT_ready, n)
                            for k in range(KT):
                                last = eng.transpose(bank(0)[:, k * P:(k + 1) * P], gath[:, s, k, 0:D], ident[:, :])
                            last.then_inc(ft_ps, 1)

                        def up(n, s):
                            eng.wait_ge(fT_ready, n + 1)
                            eng.wait_ge(fw_ready, n + 1)
                            for k in range(FK):
                                if not early(n, 1):
                                    eng.wait_ge(fh_ready, n * FK - (FK - 1 - k))
                                eng.matmul(ps[:, 1 + k, 0:TS], w1t[:, s % 2, k * P:(k + 1) * P], gT[:, s % 2, :],
                                           start=True, stop=True).then_inc(fu_ps, 1)

                        def expert(s):
                            eng.nop(nofuse=True)
                            return eng.value_load(cell[0:1, s:s + 1], min_val=0, max_val=E0 - 1)

                        def down(n, s, e):
                            eng.wait_ge(fh_ready, (n + 1) * FK)
                            if not early(n, 2):
                                eng.wait_ge(fs_ready, n - 1)
                            for c in range(KT):
                                for k in range(FK):
                                    last = eng.matmul(ps[:, 5 + s % 2, c * P:(c + 1) * P],
                                                      hid[:, s % 2, k, c * P:(c + 1) * P],
                                                      w2s[:, ds(e, 1), k, :].rearrange("p a d -> p (a d)"),
                                                      start=(k == 0), stop=(k == FK - 1))
                            last.then_inc(fy_ps, 1)

                        def body(n, s):
                            up(n, s)
                            if not early(n, 1):
                                e = expert((s + 3) % 4)
                            if not late(n, 1):
                                turn(n + 1, (s + 1) % 4)
                            if not early(n, 1):
                                down(n - 1, (s + 3) % 4, e)

                        turn(0, 0)
                        tile_rounds(eng, body)
                        down(NTL - 1, 3, expert(3))

                    @block.scalar
                    def _(eng):
                        def keep(n, s):
                            eng.wait_ge(ft_ps, n + 1)
                            if not early(n, 2):
                                eng.wait_ge(fu_ps, (n - 1) * FK)
                            eng.activation(gT[:, s % 2, :], ps[:, 0, 0:TS], ACT.Copy).then_inc(fT_ready, 1)

                        def body(n, s):
                            if not early(n, 2):
                                eng.wait_ge(fy_ps, n - 1)
                            for k in range(FK):
                                eng.wait_ge(fu_ps, n * FK + k + 1)
                                eng.activation(hid[:, s % 2, k, :], ps[:, 1 + k, 0:TS], ACT.Gelu_apprx_tanh,
                                               bias=b1t[:, s % 2, k:k + 1]).then_inc(fh_ready, 1)
                            if not late(n, 1):
                                keep(n + 1, (s + 1) % 4)

                        keep(0, 0)
                        tile_rounds(eng, body)

                    @block.vector
                    def _(eng):
                        def weights(n, s):
                            if not early(n, 2):
                                eng.wait_ge(fu_ps, (n - 1) * FK)
                                eng.wait_ge(fh_ready, (n - 1) * FK)
                            eng.nop(nofuse=True)
                            eng.tensor_copy(cell[0:1, s:s + 1], tile_e[0:1, ds(n, 1)]).then_inc(fw_cell, 1)
                            eng.wait_ge(fw_cell, n + 1)
                            eng.nop(nofuse=True)
                            e = eng.value_load(cell[0:1, s:s + 1], min_val=0, max_val=E0 - 1)
                            eng.tensor_copy(w1t[:, s % 2, :], w1s[:, ds(e, 1), :].rearrange("p a f -> p (a f)"))
                            eng.tensor_copy(b1t[:, s % 2, :], b1c[:, ds(e * FK, FK)]).then_inc(fw_ready, 1)

                        def gates(n, s):
                            eng.wait_ge(f_gathered[s], (n - s) * (KT * 4) + KT * 16)
                            eng.tensor_tensor(gm[:, s % 2, :, :], gath[:, s, :, D:HW0], info[:, ds(n * KT, KT), 4:W],
                                              ALU.mult).then_inc(fg_part, 1)
                            eng.wait_ge(fg_part, n + 1)
                            eng.tensor_reduce(gv[:, s % 2, :], gm[:, s % 2, :, :], AX, ALU.add).then_inc(f_gated, 1)

                        def weigh(n, s):
                            eng.wait_ge(fy_ps, n + 1)
                            eng.wait_ge(f_gated, n + 1)
                            if not early(n, 2):
                                for a in range(KT):
                                    eng.wait_ge(f_added[a], (n - 1) * 16)
                            for k in range(KT):
                                last = eng.tensor_scalar(ysc[:, s % 2, k, :], ps[:, 5 + s % 2, k * P:(k + 1) * P],
                                                         gv[:, s % 2, k:k + 1], None, ALU.mult)
                            last.then_inc(fs_ready, 1)

                        def body(n, s):
                            if not late(n, 1):
                                weights(n + 1, (s + 1) % 4)
                            gates(n, s)
                            if not early(n, 1):
                                weigh(n - 1, (s + 3) % 4)

                        weights(0, 0)
                        tile_rounds(eng, body)
                        weigh(NTL - 1, 3)

            with ExitStack() as tmp2:
                accs = tmp2.enter_context(nc.sbuf_tensor("accs0", [P, 2, NT, D], F32))
                bias_ps = sem("bias_ps")
                both_added = sem("both_added")
                NQ0 = NT // 4
                with nc.Block() as block:
                    @block.sync
                    def _(eng):
                        for a in range(2):
                            eng.wait_ge(f_added[a], NTL * 16)
                        for q in range(4):
                            for a in range(2):
                                eng.dma_start(accs[:, a, q * NQ0:(q + 1) * NQ0, :],
                                              acc0[a][0:T, :].rearrange("(n p) d -> p n d", p=P)[:, q * NQ0:(q + 1) * NQ0, :]
                                              ).then_inc(ld_acc[q], 16)

                    @block.gpsimd
                    def _(eng):
                        for q in range(4):
                            eng.wait_ge(ld_acc[q], 32)
                            a0, a1 = (accs[:, a, q * NQ0:(q + 1) * NQ0, :] for a in range(2))
                            eng.tensor_tensor(a0, a0, a1, ALU.add).then_inc(both_added, 1)

                    @block.tensor
                    def _(eng):
                        for i in range(NC):
                            for c in range(4):
                                last = eng.matmul(bank(i)[:, c * P:(c + 1) * P], gflat[:, (c % 2) * P:(c % 2 + 1) * P],
                                                  b2m[:, 2 * i + c // 2, :], start=True, stop=True)
                            last.then_inc(bias_ps, 1)

                    @block.vector
                    def _(eng):
                        step = Chain(eng, vector_steps)
                        step.straight()
                        for q in range(4):
                            a0 = accs[:, 0, q * NQ0:(q + 1) * NQ0, :]
                            eng.wait_ge(bias_ps, (q + 1) * NC // 4)
                            eng.wait_ge(both_added, q + 1)
                            step(eng.tensor_tensor(a0, a0, ps[:, q * NC // 4:(q + 1) * NC // 4, :].rearrange(
                                "p b (k d) -> p (b k) d", k=4), ALU.add))
                            a0c = a0.rearrange("p (c k) d -> p c k d", k=4)
                            step(eng.tensor_tensor(a0c, a0c,
                                                   gchunk[:, 0, q * NQ0 // 4:(q + 1) * NQ0 // 4, None, :].to_broadcast(
                                                       [P, NQ0 // 4, 4, D]), ALU.mult))
                            xs = x_sb[:, q * NQ0:(q + 1) * NQ0, :]
                            step(eng.tensor_tensor(xs, xs, a0, ALU.add))
                            moments_of(eng, step, range(q * NQ0, (q + 1) * NQ0))
                        step.close()
        ffn_weights.close()
        rstd_block(2)

        GROUPS = E1 * NT // P
        EG = E1 // GROUPS
        keep = sb("keep", [P, E1, NT], BF16)
        selR = sb("selR", [P, P + 1], BF16)
        oneR = sb("oneR", [P, P + 1], BF16)
        io_i = sb("io_i", [P, P], I32)
        iota = sb("iota", [P, P])
        cc_i = sb("cc_i", [P, 1], I32)
        ccol = sb("ccol", [P, 1])
        pay = sb("pay", [P, EG, 2], BF16)
        inM = sb("inM", [P, GROUPS, EG, P], BF16)
        k_ready = sem("k_ready")
        w13T = sb("w13T", [P, E1, 2, F1])
        w2b = sb("w2b", [P, NPAIR, 2, D])
        w2_zero = sem("w2_zero")

        with ExitStack() as tmp:
            def st(name, shape, dt=F32):
                return tmp.enter_context(nc.sbuf_tensor(name, shape, dt))

            xn = st("xn3", [P, 2, B, 4, D])
            h3 = st("h3", [P, 2, B, CHUNK])
            fg = st("fg", [P, CHUNK])
            lam = st("lam", [P, CHUNK])
            state = st("state", [P, 2, CHUNK])
            cxn_ready = sem("cxn_ready")
            cxnT_ready = sem("cxnT_ready")
            ch_ready = sem("ch_ready")
            f_ps = sem("f_ps")
            u_ps = sem("u_ps")
            fg_ready = sem("fg_ready")
            lam_ps = sem("lam_ps")
            lam_ready = sem("lam_ready")
            s_ready = sem("s_ready")
            c_out = sem("c_out")
            cx_added = sem("cx_added")
            with nc.Block() as block:
                @block.gpsimd
                def _(eng):
                    step = Chain(eng, gpsimd_steps)
                    step.straight()
                    eng.memset(keep[:, :, :], 1.0)
                    eng.memset(oneR[:, :], 1.0)
                    eng.memset(pay[:, :, :], 0.0)
                    eng.memset(inM[:, :, :, :], 0.0)
                    eng.iota(io_i[:, :], pattern=[[1, P]], base=0, channel_multiplier=0)
                    eng.iota(cc_i[:, :], pattern=[[1, 1]], base=0, channel_multiplier=1)
                    step(eng.memset(selR[:, :], -1.0))
                    eng.memset(keep[:, :, 0:1], 0.0)
                    step(eng.affine_select(out=selR[:, 0:P], in_=selR[:, 0:P], compare_op=ALU.is_gt, fill=0.0, base=0,
                                           pattern=[[-1, P]], channel_multiplier=1))
                    eng.tensor_copy(iota[:, :], io_i[:, :])
                    step(eng.tensor_copy(ccol[:, :], cc_i[:, :]))
                    for a in range(EG):
                        r = slice(a * NT, (a + 1) * NT)
                        eng.tensor_scalar(pay[r, a, 0:1], ccol[r, :], float(-a * NT), None, ALU.add)
                        last = eng.tensor_copy(pay[r, a, 1:2], ones[r, 0:1])
                    step(last)
                    step.close()
                    eng.sem_inc(k_ready, 1)
                    eng.memset(w2b[:, :, :, :], 0.0).then_inc(w2_zero, 1)

                @block.vector
                def _(eng):
                    step = Chain(eng, vector_steps)
                    step.straight()
                    step(eng.memset(state[:, 1, CHUNK - 1:CHUNK], 0.0))

                    def norm(j):
                        if j >= 2:
                            eng.wait_ge(cxnT_ready, j - 1)
                        for b in range(B):
                            last = normalized(eng, xn[:, j % 2, b, :, :], j + b * CPB)
                        last.then_inc(cxn_ready, 1)

                    def add(j):
                        eng.wait_ge(c_out, j + 1)
                        for b in range(B):
                            xs = x_sb[:, (j + b * CPB) * 4:(j + b * CPB + 1) * 4, :]
                            last = eng.tensor_tensor(xs, xs, bank(6 + b).rearrange("p (k d) -> p k d", k=4), ALU.add)
                        last.then_inc(cx_added, 1)
                        eng.wait_ge(cx_added, j + 1)
                        moments_of(eng, step, [(j + b * CPB) * 4 + k for b in range(B) for k in range(4)])

                    norm(0)
                    for j in range(CPB):
                        u = j % 2
                        if j + 1 < CPB:
                            norm(j + 1)
                        eng.wait_ge(lam_ready, j + 1)
                        if j >= 1:
                            eng.wait_ge(s_ready, j)
                        if j >= 2:
                            eng.wait_ge(c_out, j - 1)
                        eng.tensor_tensor_scan(state[:, u, :], lam[:, :], bank(3 + u),
                                               state[:, 1 - u, CHUNK - 1:CHUNK], ALU.mult, ALU.add).then_inc(s_ready, 1)
                        if j >= 1:
                            add(j - 1)
                    add(CPB - 1)
                    step.close()

                @block.tensor
                def _(eng):
                    def front(j):
                        u = j % 2
                        eng.wait_ge(cxn_ready, j + 1)
                        if j >= 1:
                            eng.wait_ge(ch_ready, j)
                        for b in range(B):
                            for k in range(4):
                                last = eng.transpose(bank(b)[:, k * P:(k + 1) * P], xn[:, u, b, k, :], ident[:, :])
                        last.then_inc(cxnT_ready, 1)
                        eng.wait_ge(ch_ready, j + 1)
                        if j >= 1:
                            eng.wait_ge(fg_ready, j)
                        for b in range(B):
                            last = eng.matmul(ps[b * PR:(b + 1) * PR, 2, :], w_F[:, :], h3[:, u, b, :],
                                              start=True, stop=True)
                        last.then_inc(f_ps, 1)
                        if j >= 2:
                            eng.wait_ge(s_ready, j - 1)
                        for b in range(B):
                            last = eng.matmul(ps[b * PR:(b + 1) * PR, 3 + u, :], w_u[:, :], h3[:, u, b, :],
                                              start=True, stop=True)
                        last.then_inc(u_ps, 1)

                    def decay(j):
                        eng.wait_ge(fg_ready, j + 1)
                        if j >= 1:
                            eng.wait_ge(lam_ready, j)
                        eng.matmul(bank(5), lam_bd[:, :], fg[:, :], start=True, stop=True).then_inc(lam_ps, 1)

                    front(0)
                    decay(0)
                    for j in range(CPB):
                        u = j % 2
                        if j + 1 < CPB:
                            front(j + 1)
                        eng.wait_ge(s_ready, j + 1)
                        if j >= 1:
                            eng.wait_ge(cx_added, j)
                        for b in range(B):
                            for k in range(4):
                                c = slice(k * P, (k + 1) * P)
                                eng.matmul(bank(6 + b)[:, c], h3[:, u, b, c], whx[:, b, :], start=True, stop=False)
                                last = eng.matmul(bank(6 + b)[:, c], state[:, u, c], whs[:, b, :],
                                                  start=False, stop=True)
                        last.then_inc(c_out, 1)
                        if j + 1 < CPB:
                            decay(j + 1)

                @block.scalar
                def _(eng):
                    for j in range(CPB):
                        u = j % 2
                        eng.wait_ge(cxnT_ready, j + 1)
                        if j >= 2:
                            eng.wait_ge(c_out, j - 1)
                        for b in range(B):
                            c = j + b * CPB
                            last = eng.activation(h3[:, u, b, :], bank(b), ACT.Identity,
                                                  bias=shift[:, 1, 1, c:c + 1], scale=shift[:, 1, 0, c:c + 1])
                        last.then_inc(ch_ready, 1)
                        eng.wait_ge(f_ps, j + 1)
                        if j >= 1:
                            eng.wait_ge(lam_ps, j)
                        eng.activation(fg[:, :], bank(2), ACT.Sigmoid).then_inc(fg_ready, 1)
                        eng.wait_ge(lam_ps, j + 1)
                        eng.wait_ge(u_ps, j + 1)
                        if j >= 1:
                            eng.wait_ge(s_ready, j)
                        eng.activation(lam[:, :], bank(5), ACT.Sigmoid).then_inc(lam_ready, 1)
        rstd_block(3)

        PG = 4
        NG = 8
        GE = E1 // NG
        TG = 4
        SCALE = 2.5
        xe_sel = sb("xe_sel", [P, E1, NT], BF16)
        hx_stored = [sem(f"hx_stored{u}") for u in range(2)]
        with ExitStack() as tmp:
            def st(name, shape, dt=F32):
                return tmp.enter_context(nc.sbuf_tensor(name, shape, dt))

            e_bias = st("e_bias", [P, E1])
            w1n = st("w1n", [P, 2, PG, P])
            w3n = st("w3n", [P, 2, PG, P])
            w2n = st("w2n", [P, 2, 2 * PG, F1])
            wn_loaded = [sem(f"wn_loaded{u}") for u in range(2)]
            wn_turned = sem("wn_turned")
            wn_kept = sem("wn_kept")
            assert NPAIR // PG == NC
            w1_v = t["L1_ffn_w1"].rearrange("(n e) f h -> (e f) n h", e=2)
            w3_v = t["L1_ffn_w3"].rearrange("(n e) f h -> (e f) n h", e=2)
            w2_v = t["L1_ffn_w2"].rearrange("e h f -> h e f")
            lower = st("lower", [P, NG, NG])
            xn = st("xn4", [P, 2, 4, D])
            rows = st("rows", [P, 2, 4, HXW])
            h4 = st("h4", [P, 2, CHUNK])
            sc = st("sc", [P, 2, 4, E1])
            sgm = st("sgm", [P, CHUNK])
            hs = st("hs", [P, CHUNK])
            sfc = st("sfc", [P, 4, E1])
            tmpv = st("tmpv", [P, 4, E1])
            gt = tmpv[:, :, :].rearrange("p k (g h) -> p k g h", g=NG)
            rep = st("rep", [P, 4, E1])
            ge = rep[:, :, :].rearrange("p k (g h) -> p k g h", g=NG)
            sel = st("sel", [P, 2, 4, E1])
            top8 = st("top8", [P, 4, 8])
            hi = st("hi", [P, 4 * NG, GE // 2])
            lo = st("lo", [P, 4 * NG, GE // 2])
            mn = st("mn", [P, 4 * NG, GE // 4])
            gsum = st("gsum", [P, 4, NG])
            rank = st("rankg", [P, 4, NG])
            wsum = st("wsum", [P, 4])

            ld_b = sem("ld_b")
            z_ready = sem("z_ready")
            dn_ready = sem("dn_ready")
            d_part = sem("d_part")
            h4_ready = sem("h4_ready")
            h4_ps = sem("h4_ps")
            h4T_ready = sem("h4T_ready")
            lg4_ps = sem("lg4_ps")
            sc_ready = sem("sc_ready")
            sh_ps = sem("sh_ps")
            sgm_ready = sem("sgm_ready")
            hs_ready = sem("hs_ready")
            dn_ps = sem("dn_ps")
            dx_added = sem("dx_added")
            sel_ready = sem("sel_ready")
            sel_kept = sem("sel_kept")
            w_ready = sem("w_ready")
            NEVER = -3e38
            with nc.Block() as block:
                @block.sync
                def _(eng):
                    eng.dma_start(e_bias[:, :], t["L1_ffn_e_bias"][None, :].to_broadcast([P, E1])).then_inc(ld_b, 16)

                    def load_weights(r, u):
                        eng.dma_start(w1n[:, u, :, :], w1_v[:, ds(r * PG, PG), :]).then_inc(wn_loaded[u], 16)
                        eng.dma_start(w3n[:, u, :, :], w3_v[:, ds(r * PG, PG), :]).then_inc(wn_loaded[u], 16)
                        eng.dma_start(w2n[:, u, :, :], w2_v[:, ds(r * 2 * PG, 2 * PG), :]).then_inc(wn_loaded[u], 16)

                    def body(i, u, prev, nxt):
                        if nxt:
                            eng.wait_ge(wn_turned, i + 1)
                            load_weights(i + 1, 1 - u)
                        eng.wait_ge(w_ready, i + 3)
                        eng.dma_start(hx_v[:, ds(i * 4, 4), :], rows[:, u, :, :]).then_inc(hx_stored[u], 16)

                    load_weights(0, 0)
                    chunks(eng, body)
                    for u in range(2):
                        eng.wait_ge(hx_stored[u], 16 * (NC // 2))

                @block.gpsimd
                def _(eng):
                    eng.memset(lower[:, :, :], 1.0).then_inc(z_ready, 1)
                    eng.wait_ge(z_ready, 1)
                    eng.affine_select(out=lower[:, :, :], in_=lower[:, :, :], compare_op=ALU.is_gt, fill=0.0, base=0,
                                      pattern=[[1, NG], [-1, NG]], channel_multiplier=0).then_inc(z_ready, 1)

                    def modulate(i, u):
                        eng.wait_ge(dn_ready, i + 1)
                        eng.wait_ge(hx_stored[u], (i - u) * 8)
                        r = rows[:, u, :, 0:D]
                        eng.tensor_tensor(r, xn[:, u, :, :], schunk[:, 1, ds(i, 1), 1, :].to_broadcast([P, 4, D]),
                                          ALU.mult).then_inc(d_part, 1)
                        eng.wait_ge(d_part, i + 1)
                        eng.tensor_tensor(r, r, schunk[:, 1, ds(i, 1), 0, :].to_broadcast([P, 4, D]),
                                          ALU.add).then_inc(h4_ready, 1)

                    def body(i, u, prev, nxt):
                        if nxt:
                            modulate(i + 1, 1 - u)
                        eng.wait_ge(sel_ready, i + 1)
                        eng.tensor_copy(xe_sel[:, :, ds(i * 4, 4)],
                                        sel[:, u, :, :].rearrange("p k e -> p e k")).then_inc(sel_kept, 1)

                    modulate(0, 0)
                    chunks(eng, body)

                @block.tensor
                def _(eng):
                    eng.sem_inc(sh_ps, 1)
                    eng.sem_inc(lg4_ps, 1)
                    def score(i, u):
                        eng.wait_ge(h4_ready, i + 1)
                        eng.wait_ge(h4T_ready, i)
                        for k in range(4):
                            last = eng.transpose(bank(0)[:, k * P:(k + 1) * P], rows[:, u, k, 0:D], ident[:, :])
                        last.then_inc(h4_ps, 1)
                        eng.wait_ge(h4T_ready, i + 1)
                        eng.wait_ge(sc_ready, i)
                        for k in range(4):
                            last = eng.matmul(ps[:, 2, k * E1:(k + 1) * E1], h4[:, u, k * P:(k + 1) * P], gw1[:, :],
                                              start=True, stop=True)
                        last.then_inc(lg4_ps, 1)

                    def up(i, u):
                        eng.wait_ge(hs_ready, i + 1)
                        eng.matmul(bank(4), sgT[:, :], h4[:, u, :], start=True, stop=True)
                        eng.matmul(bank(5), suT[:, :], h4[:, u, :], start=True, stop=True).then_inc(sh_ps, 1)

                    def body(i, u, prev, nxt):
                        if nxt:
                            score(i + 1, 1 - u)
                        eng.wait_ge(wn_loaded[u], (i - u) * 24 + 48)
                        eng.wait_ge(wn_kept, i + 1)
                        for q in range(PG):
                            c = slice(q * P, (q + 1) * P)
                            eng.transpose(bank(1)[:, c], w1n[:, u, q, :], ident[:, :])
                            eng.transpose(bank(3)[:, c], w3n[:, u, q, :], ident[:, :])
                            last = eng.transpose(bank(7)[:, c], w2n[:, u, 2 * q:2 * q + 2, :].rearrange("p e f -> p (e f)"),
                                                 ident[:, :])
                        last.then_inc(wn_turned, 1)
                        eng.wait_ge(hs_ready, i + 2)
                        eng.wait_ge(dx_added, i)
                        for k in range(4):
                            last = eng.matmul(bank(6)[:, k * P:(k + 1) * P], hs[:, k * P:(k + 1) * P],
                                              sdg[:, ds(i, 1), :].rearrange("p a d -> p (a d)"), start=True, stop=True)
                        last.then_inc(dn_ps, 1)
                        if nxt:
                            up(i + 1, 1 - u)

                    eng.sem_inc(wn_turned, 1)
                    eng.sem_inc(wn_kept, 1)
                    score(0, 0)
                    up(0, 0)
                    chunks(eng, body)

                @block.scalar
                def _(eng):
                    def keep_weights(i, u):
                        eng.wait_ge(wn_turned, i + 2)
                        for a in range(2):
                            eng.activation(w13T[:, ds(i * 2 * PG, 2 * PG), a, :],
                                           bank(1 + 2 * a).rearrange("p (e f) -> p e f", f=F1), ACT.Copy)
                        for e in range(2):
                            r = slice(e * F1, (e + 1) * F1)
                            last = eng.activation(w2b[r, ds(i * PG, PG), e, :],
                                                  ps[r, 7, :].rearrange("p (q h) -> p q h", q=PG), ACT.Copy)
                        last.then_inc(wn_kept, 1)

                    def norm(i, u):
                        for k in range(4):
                            last = eng.activation(xn[:, u, k, :], x_sb[:, ds(i * 4 + k, 1), :].rearrange("p a d -> p (a d)"),
                                                  ACT.Identity, bias=nmr[:, ds(i * 4 + k, 1)],
                                                  scale=rstd[:, ds(i * 4 + k, 1)])
                        last.then_inc(dn_ready, 1)

                    def body(i, u, prev, nxt):
                        eng.wait_ge(h4_ps, i + 1)
                        eng.wait_ge(lg4_ps, i + 1)
                        eng.wait_ge(sh_ps, i + 1)
                        eng.activation(h4[:, u, :], bank(0), ACT.Copy).then_inc(h4T_ready, 1)
                        eng.wait_ge(lg4_ps, i + 2)
                        eng.wait_ge(w_ready, i + 1)
                        eng.activation(sc[:, u, :, :], ps[:, 2, 0:4 * E1].rearrange("p (k e) -> p k e", k=4),
                                       ACT.Sigmoid).then_inc(sc_ready, 1)
                        if nxt:
                            if prev:
                                eng.wait_ge(h4_ready, i)
                            norm(i + 1, 1 - u)
                        eng.wait_ge(sh_ps, i + 2)
                        eng.wait_ge(hs_ready, i + 1)
                        eng.activation(sgm[:, :], bank(4), ACT.Sigmoid).then_inc(sgm_ready, 1)
                        if prev:
                            keep_weights(i - 1, 1 - u)

                    norm(0, 0)
                    eng.wait_ge(w2_zero, 1)
                    chunks(eng, body)
                    keep_weights(NC - 1, 1)

                @block.vector
                def _(eng):
                    eng.sem_inc(hs_ready, 1)
                    step = Chain(eng, vector_steps)
                    eng.sem_inc(w_ready, 2)
                    eng.wait_ge(ld_b, 16)
                    eng.wait_ge(z_ready, 2)
                    def add(i):
                        eng.wait_ge(dn_ps, i + 1)
                        xs = x_sb[:, ds(i * 4, 4), :]
                        eng.tensor_tensor(xs, xs, bank(6).rearrange("p (k d) -> p k d", k=4), ALU.add).then_inc(dx_added, 1)

                    def body(i, u, prev, nxt):
                        step.body(i, 20)
                        eng.wait_ge(sc_ready, i + 1)
                        s = sc[:, u, :, :]
                        step(eng.tensor_tensor(sfc[:, :, :], s, e_bias[:, None, :].to_broadcast([P, 4, E1]), ALU.add))
                        v = sfc[:, :, :].rearrange("p k (g x) -> p (k g) x", g=NG)
                        q, r = GE // 2, GE // 4
                        eng.tensor_tensor(hi[:, :, :], v[:, :, 0:q], v[:, :, q:GE], ALU.max)
                        step(eng.tensor_tensor(lo[:, :, :], v[:, :, 0:q], v[:, :, q:GE], ALU.min))
                        for w in (r, r // 2):
                            eng.tensor_tensor(mn[:, :, 0:w], hi[:, :, 0:w], hi[:, :, w:2 * w], ALU.min)
                            step(eng.tensor_tensor(lo[:, :, 0:w], lo[:, :, 0:w], lo[:, :, w:2 * w], ALU.max))
                            eng.tensor_tensor(lo[:, :, 0:w], lo[:, :, 0:w], mn[:, :, 0:w], ALU.max)
                            step(eng.tensor_tensor(hi[:, :, 0:w], hi[:, :, 0:w], hi[:, :, w:2 * w], ALU.max))
                        step(eng.tensor_tensor(gsum[:, :, :].rearrange("p k g -> p (k g)"), hi[:, :, 0], lo[:, :, 0],
                                               ALU.add))
                        other = gsum[:, :, None, :].to_broadcast([P, 4, NG, NG])
                        mine = gsum[:, :, :, None].to_broadcast([P, 4, NG, NG])
                        eng.tensor_tensor(gt[:, :, :, :], other, mine, ALU.is_gt)
                        step(eng.tensor_tensor(ge[:, :, :, :], other, mine, ALU.is_equal))
                        step(eng.tensor_tensor(ge[:, :, :, :], ge[:, :, :, :],
                                               lower[:, None, :, :].to_broadcast([P, 4, NG, NG]), ALU.mult))
                        step(eng.tensor_tensor(gt[:, :, :, :], gt[:, :, :, :], ge[:, :, :, :], ALU.add))
                        step(eng.tensor_reduce(rank[:, :, :], gt[:, :, :, :], AX, ALU.add))
                        step(eng.scalar_tensor_tensor(tmpv[:, :, :].rearrange("p k (g x) -> p (k g) x", g=NG),
                                                      rank[:, :, :].rearrange("p k g -> p (k g)")[:, :, None].to_broadcast(
                                                          [P, 4 * NG, GE]), float(TG),
                                                      sfc[:, :, :].rearrange("p k (g x) -> p (k g) x", g=NG),
                                                      ALU.is_lt, ALU.mult))
                        step(eng.tensor_scalar(tmpv[:, :, :], tmpv[:, :, :], 0.0, None, ALU.add))
                        eng.nop(nofuse=True)
                        for k in range(4):
                            last = eng.max(top8[:, k, :], tmpv[:, k, :])
                        step(last)
                        eng.nop(nofuse=True)
                        for k in range(4):
                            last = eng.match_replace(rep[:, k, :], top8[:, k, :], tmpv[:, k, :], NEVER)
                        step(last)
                        eng.wait_ge(sel_kept, i)
                        eng.tensor_scalar(sel[:, u, :, :], rep[:, :, :], NEVER, None, ALU.is_equal).then_inc(sel_ready, 1)
                        step(eng.scalar_tensor_tensor(tmpv[:, :, :], rep[:, :, :], NEVER, s, ALU.is_equal, ALU.mult))
                        step(eng.tensor_reduce(wsum[:, :], tmpv[:, :, :], AX, ALU.add))
                        step(eng.tensor_scalar(wsum[:, :], wsum[:, :], 1e-20, None, ALU.add))
                        step(eng.reciprocal(wsum[:, :], wsum[:, :]))
                        eng.wait_ge(h4_ready, i + 1)
                        eng.scalar_tensor_tensor(rows[:, u, :, D:HXW], tmpv[:, :, :], SCALE,
                                                 wsum[:, :, None].to_broadcast([P, 4, E1]),
                                                 ALU.mult, ALU.mult).then_inc(w_ready, 1)
                        if prev:
                            add(i - 1)
                        eng.wait_ge(sgm_ready, i + 1)
                        step(eng.tensor_tensor(sgm[:, :], sgm[:, :], bank(4), ALU.mult))
                        eng.tensor_tensor(hs[:, :], sgm[:, :], bank(5), ALU.mult).then_inc(hs_ready, 1)

                    chunks(eng, body)
                    step.end(NC)
                    add(NC - 1)

        idx = sb("idx", [P, E1], I32)
        with ExitStack() as tmp:
            def st(name, shape, dt=F32):
                return tmp.enter_context(nc.sbuf_tensor(name, shape, dt))

            rinc = st("rinc", [P, E1, NT], BF16)
            edge = st("edge", [P, GROUPS, 2])
            oh = st("oh", [P, GROUPS, P])
            oh_b = st("oh_b", [P, GROUPS, P])
            ohb = st("ohb", [P, GROUPS, P], BF16)
            le = st("le", [P, EG, P])
            sg_scr = st("sg_scr", [P, 2, EG, P])
            chalf = st("chalf", [P, 1])
            cnt = st("cnt4", [P, E1])
            nv = st("nv", [P, E1, 2])
            spare = st("spare", [P, 1])
            f1 = st("f1", [P, E1])
            r_done = sem("r_done")
            in_ps = sem("in_ps")
            in_act = sem("in_act")
            edge_read = sem("edge_read")
            oh_ready = sem("oh_ready")
            slot_ps = sem("slot_ps")
            slot_used = [sem(f"slot_used{a}") for a in range(2)]
            with nc.Block() as block:
                @block.tensor
                def _(eng):
                    eng.wait_ge(r_done, 1)
                    for g in range(GROUPS):
                        e = slice(g * EG, (g + 1) * EG)
                        o = ps[:, g // 2, (g % 2) * 256:(g % 2) * 256 + P + 1]
                        eng.matmul(o, xe_sel[:, e, :].rearrange("p e n -> p (e n)"), selR[:, :], start=True, stop=False)
                        last = eng.matmul(o, rinc[:, e, :].rearrange("p e n -> p (e n)"), oneR[:, :], start=False, stop=True)
                    last.then_inc(in_ps, 1)
                    eng.wait_ge(oh_ready, 1)
                    eng.wait_ge(in_act, 1)
                    for g in range(GROUPS):
                        if g >= 4:
                            eng.wait_ge(slot_used[g % 2], (g - 4) // 2 + 1)
                        eng.matmul(bank(g % 4), ohb[:, g, :], inM[:, g, :, :].rearrange("p e m -> p (e m)"),
                                   start=True, stop=True)
                        eng.matmul(ps[:, 4 + g % 4, 0:2 * EG], ohb[:, g, :], pay[:, :, :].rearrange("p e a -> p (e a)"),
                                   start=True, stop=True).then_inc(slot_ps, 1)

                @block.scalar
                def _(eng):
                    eng.wait_ge(edge_read, 1)
                    eng.wait_ge(k_ready, 1)
                    wide = ps[:, :, :].rearrange("p b (h c) -> p (b h) c", h=2)
                    for a in range(EG):
                        r = slice(a * NT, (a + 1) * NT)
                        last = eng.activation(inM[r, :, a, :], wide[r, :, 0:P], ACT.Copy)
                    last.then_inc(in_act, 1)
                    for g in range(1, GROUPS, 2):
                        eng.wait_ge(slot_ps, g + 1)
                        if g >= 5:
                            eng.wait_ge(slot_used[1], g // 2 - 1)
                        eng.activation(nv[:, g * EG:(g + 1) * EG, :].rearrange("p e a -> p (e a)"),
                                       ps[:, 4 + g % 4, 0:2 * EG], ACT.Copy)
                        for a in range(EG):
                            last = eng.activation(sg_scr[:, g // 2 % 2, a, :], bank(g % 4)[:, a * P:(a + 1) * P], ACT.Sign,
                                                  bias=chalf[:, :], scale=-1.0,
                                                  accum_out=cnt[:, g * EG + a:g * EG + a + 1])
                        last.then_inc(slot_used[1], 1)

                @block.vector
                def _(eng):
                    step = Chain(eng, vector_steps)
                    step.straight()
                    eng.wait_ge(k_ready, 1)
                    eng.tensor_scalar(chalf[:, :], ccol[:, :], 0.5, None, ALU.add)
                    eng.tensor_tensor_scan(rinc[:, :, :].rearrange("p e n -> p (e n)"),
                                           keep[:, :, :].rearrange("p e n -> p (e n)"),
                                           xe_sel[:, :, :].rearrange("p e n -> p (e n)"), 0.0,
                                           ALU.mult, ALU.add).then_inc(r_done, 1)
                    eng.wait_ge(in_ps, 1)
                    wide = ps[:, :, :].rearrange("p b (h c) -> p (b h) c", h=2)
                    eng.tensor_copy(edge[:, :, 0], wide[:, :, P])
                    step(eng.tensor_copy(edge[:, :, 1], wide[:, :, P - 1]))
                    eng.sem_inc(edge_read, 1)
                    io = iota[:, None, :].to_broadcast([P, GROUPS, P])
                    eng.tensor_tensor(oh[:, :, :], io, edge[:, :, 0:1].to_broadcast([P, GROUPS, P]), ALU.is_ge)
                    step(eng.tensor_tensor(oh_b[:, :, :], io, edge[:, :, 1:2].to_broadcast([P, GROUPS, P]), ALU.is_ge))
                    step(eng.tensor_tensor(ohb[:, :, :], oh[:, :, :], oh_b[:, :, :], ALU.subtract))
                    eng.sem_inc(oh_ready, 1)
                    for g in range(0, GROUPS, 2):
                        eng.wait_ge(slot_ps, g + 1)
                        eng.tensor_copy(nv[:, g * EG:(g + 1) * EG, :].rearrange("p e a -> p (e a)"),
                                        ps[:, 4 + g % 4, 0:2 * EG])
                        for a in range(EG):
                            last = eng.tensor_scalar(le[:, a, :], bank(g % 4)[:, a * P:(a + 1) * P], ccol[:, :], 0.0,
                                                     ALU.is_le, ALU.add, accum_out=cnt[:, g * EG + a:g * EG + a + 1])
                        step(last)
                        eng.sem_inc(slot_used[0], 1)
                    eng.wait_ge(slot_used[1], GROUPS // 2)
                    odd = cnt[:, :].rearrange("p (g h a) -> p g h a", h=2, a=EG)[:, :, 1, :]
                    step(eng.tensor_scalar(odd, odd, 0.5, float(P // 2), ALU.mult, ALU.add))
                    step(eng.tensor_scalar(spare[:, :], ccol[:, :], float(T - P), None, ALU.add))
                    step(eng.scalar_tensor_tensor(f1[:, :], nv[:, :, 0], float(P), cnt[:, :], ALU.mult, ALU.add))
                    step(eng.tensor_scalar(f1[:, :], f1[:, :], spare[:, :], None, ALU.add))
                    step(eng.tensor_scalar(nv[:, :, 1], nv[:, :, 1], spare[:, :], None, ALU.mult))
                    step(eng.tensor_tensor(idx[:, :], f1[:, :], nv[:, :, 1], ALU.subtract))
                    step.close()

        with ExitStack() as tmp:
            def st(name, shape, dt=F32):
                return tmp.enter_context(nc.sbuf_tensor(name, shape, dt))

            KE = 4
            RE = E1 // KE
            PER_ROUND = KE // 2 * 16
            gath = st("gath", [P, 4, KE, HXW])
            gT = st("gT", [P, 2, KE, P])
            sl = st("sl", [P, 2, KE, F1])
            hh = st("hh", [P, 2, KE, F1])
            hhT = st("hhT", [P, 2, KE // 2, P])
            ysc = st("ysc", [P, 2, KE, D])
            gathered = [sem(f"gathered{s}") for s in range(4)]
            g_ps = sem("g_ps")
            gT_ready = sem("gT_ready")
            up_ps = sem("up_ps")
            sl_ready = sem("sl_ready")
            hh_ready = sem("hh_ready")
            hh_ps = sem("hh_ps")
            hhT_ready = sem("hhT_ready")
            y_ps = sem("y_ps")
            ysc_ready = sem("ysc_ready")
            added = [sem(f"added{a}") for a in range(2)]
            with nc.Block() as block:
                @block.gpsimd
                def _(eng):
                    eng.wait_ge(acc_zeroed, 48)
                    for r in range(-3, RE):
                        if r >= 0:
                            eng.wait_ge(ysc_ready, r + 2)
                        for k in range(KE):
                            if r + 3 < RE:
                                e = (r + 3) * KE + k
                                eng.indirect_dma_start(out=gath[:, (r + 3) % 4, k, :], out_offset=None, in_=hx,
                                                       in_offset=bass.IndirectOffsetOnAxis(ap=idx[:, e:e + 1], axis=0)
                                                       ).then_inc(gathered[(r + 3) % 4], 16)
                            if r >= 0:
                                if r or k >= 2:
                                    eng.wait_ge(added[k % 2], r * PER_ROUND + k // 2 * 16)
                                e = r * KE + k
                                eng.indirect_dma_start(out=acc[k % 2],
                                                       out_offset=bass.IndirectOffsetOnAxis(ap=idx[:, e:e + 1], axis=0),
                                                       in_=ysc[:, r % 2, k, :], in_offset=None,
                                                       compute_op=ALU.add).then_inc(added[k % 2], 16)

                @block.tensor
                def _(eng):
                    eng.sem_inc(y_ps, 1)
                    eng.sem_inc(up_ps, 1)
                    with eng.Fori(0, RE // 4) as j:
                        for s in range(4):
                            r, u = j * 4 + s, s % 2
                            eng.wait_ge(gathered[s], (j + 1) * 16 * KE)
                            eng.wait_ge(gT_ready, r + 1)
                            for k in range(KE):
                                last = eng.transpose(bank(0)[:, k * P:(k + 1) * P], gath[:, s, k, 0:D], ident[:, :])
                            last.then_inc(g_ps, 1)
                            eng.wait_ge(gT_ready, r + 2)
                            eng.wait_ge(hh_ready, r + 1)
                            for k in range(KE):
                                last = eng.matmul(bank(1)[:, k * P:(k + 1) * P], gT[:, u, k, :],
                                                  w13T[:, ds(r * KE + k, 1), :, :].rearrange("p e a f -> p (e a f)"),
                                                  start=True, stop=True)
                            last.then_inc(up_ps, 1)
                            eng.wait_ge(hh_ready, r + 2)
                            eng.wait_ge(hhT_ready, r + 1)
                            for q in range(KE // 2):
                                last = eng.transpose(ps[:, 2, q * P:(q + 1) * P],
                                                     hh[:, u, 2 * q:2 * q + 2, :].rearrange("p e f -> p (e f)"), ident[:, :])
                            last.then_inc(hh_ps, 1)
                            eng.wait_ge(hhT_ready, r + 2)
                            eng.wait_ge(ysc_ready, r + 1)
                            for q in range(KE // 2):
                                last = eng.matmul(bank(3)[:, q * 256:(q + 1) * 256], hhT[:, u, q, :],
                                                  w2b[:, ds(r * (KE // 2) + q, 1), :, :].rearrange("p a e h -> p (a e h)"),
                                                  start=True, stop=True)
                            last.then_inc(y_ps, 1)

                @block.scalar
                def _(eng):
                    eng.sem_inc(hhT_ready, 1)
                    eng.sem_inc(gT_ready, 1)
                    with eng.Fori(0, RE // 2) as j:
                        for u in range(2):
                            r = j * 2 + u
                            eng.wait_ge(g_ps, r + 1)
                            eng.wait_ge(up_ps, r + 1)
                            eng.activation(gT[:, u, :, :].rearrange("p k c -> p (k c)"), bank(0),
                                           ACT.Copy).then_inc(gT_ready, 1)
                            eng.wait_ge(up_ps, r + 2)
                            eng.wait_ge(hh_ready, r + 1)
                            eng.activation(sl[:, u, :, :], bank(1).rearrange("p (k a f) -> p k a f", k=KE, a=2)[:, :, 0, :],
                                           ACT.Silu).then_inc(sl_ready, 1)
                            eng.wait_ge(hh_ps, r + 1)
                            eng.wait_ge(y_ps, r + 1)
                            eng.activation(hhT[:, u, :, :].rearrange("p q c -> p (q c)"), ps[:, 2, 0:2 * P],
                                           ACT.Copy).then_inc(hhT_ready, 1)

                @block.vector
                def _(eng):
                    eng.sem_inc(ysc_ready, 1)
                    eng.sem_inc(hh_ready, 1)
                    def body(r, s):
                        u = s % 2
                        eng.wait_ge(sl_ready, r + 1)
                        eng.wait_ge(hh_ps, r)
                        eng.tensor_tensor(hh[:, u, :, :], sl[:, u, :, :],
                                          bank(1).rearrange("p (k a f) -> p k a f", k=KE, a=2)[:, :, 1, :],
                                          ALU.mult).then_inc(hh_ready, 1)
                        eng.wait_ge(y_ps, r + 2)
                        if type(r) is not int or r >= 2:
                            for a in range(2):
                                eng.wait_ge(added[a], (r - 1) * PER_ROUND)
                        for k in range(KE):
                            last = eng.tensor_scalar(ysc[:, u, k, :], bank(3)[:, k * P:(k + 1) * P],
                                                     gath[:, s, k, ds(D + r * KE + k, 1)], None, ALU.mult)
                        last.then_inc(ysc_ready, 1)

                    for s in range(4):
                        body(s, s)
                    with eng.Fori(1, RE // 4) as j:
                        for s in range(4):
                            body(j * 4 + s, s)

        with ExitStack() as tmp:
            accs = tmp.enter_context(nc.sbuf_tensor("accs", [P, 2, NT, D], F32))
            res_ready = sem("res_ready")
            st_out = sem("st_out")
            NQ = NT // 4
            with nc.Block() as block:
                @block.sync
                def _(eng):
                    for a in range(2):
                        eng.wait_ge(added[a], E1 // 2 * 16)
                    for q in range(4):
                        for a in range(2):
                            eng.dma_start(accs[:, a, q * NQ:(q + 1) * NQ, :],
                                          acc[a][0:T, :].rearrange("(n p) d -> p n d", p=P)[:, q * NQ:(q + 1) * NQ, :]
                                          ).then_inc(ld_acc[q], 16)
                    for q in range(4):
                        eng.wait_ge(res_ready, q + 1)
                        eng.dma_start(out_v[:, q * NQ:(q + 1) * NQ, :], x_sb[:, q * NQ:(q + 1) * NQ, :]).then_inc(st_out, 16)
                    eng.wait_ge(st_out, 64)

                @block.vector
                def _(eng):
                    step = Chain(eng, vector_steps)
                    step.straight()
                    for q in range(4):
                        eng.wait_ge(ld_acc[q], 64)
                        a0, a1 = (accs[:, a, q * NQ:(q + 1) * NQ, :] for a in range(2))
                        step(eng.tensor_tensor(a0, a0, a1, ALU.add))
                        step(eng.tensor_tensor(a0.rearrange("p (c k) d -> p c k d", k=4), a0.rearrange("p (c k) d -> p c k d", k=4),
                                               gchunk[:, 1, q * NQ // 4:(q + 1) * NQ // 4, None, :].to_broadcast([P, NQ // 4, 4, D]),
                                               ALU.mult))
                        xs = x_sb[:, q * NQ:(q + 1) * NQ, :]
                        eng.tensor_tensor(xs, xs, a0, ALU.add).then_inc(res_ready, 1)


_INS = [
    'L0_attn_x', 'L0_attn_w_qkv', 'L0_attn_w_out', 'L0_attn_b_out', 'L0_attn_proj', 'L0_ffn_gate_weight',
    'L0_ffn_W1', 'L0_ffn_b1', 'L0_ffn_W2', 'L0_ffn_b2', 'L0_ffn_Ws1', 'L0_ffn_bs1', 'L0_ffn_Ws2',
    'L0_ffn_bs2', 'L0_c', 'L0_wmod', 'L1_attn_W_toP', 'L1_attn_W_U', 'L1_attn_W_F', 'L1_attn_W_V',
    'L1_attn_W_lam', 'L1_attn_B_mat', 'L1_attn_C_mat', 'L1_attn_W_fromP', 'L1_ffn_gate_weight',
    'L1_ffn_e_bias', 'L1_ffn_w1', 'L1_ffn_w2', 'L1_ffn_w3', 'L1_ffn_shared_gate', 'L1_ffn_shared_up',
    'L1_ffn_shared_down', 'L1_c', 'L1_wmod',
]
_OUTS = [((2, 2048, 128), "float32")]


def kernel(**inputs):
    import numpy as _np
    import concourse.bacc as _bacc
    from concourse import mybir as _mybir
    from concourse.bass_utils import run_bass_kernel_spmd as _run

    nc = _bacc.Bacc("TRN2", target_bir_lowering=False, num_devices=1)
    arrays, args, outs = {}, {}, []
    for name in _INS:
        a = _np.ascontiguousarray(inputs[name])
        arrays[f"in_{name}_dram"] = a
        args[name] = nc.dram_tensor(f"in_{name}_dram", a.shape, _mybir.dt.from_np(a.dtype), kind="ExternalInput").ap()
    for i, (shape, dtype) in enumerate(_OUTS):
        dt = _mybir.dt.from_np(_np.dtype(dtype))
        outs.append(nc.dram_tensor(f"out_{i}_dram", shape, dt, kind="ExternalOutput").ap())
    build(nc, args, outs[0])
    r = _run(nc, [arrays], core_ids=[0])
    return r.results[0]["out_0_dram"]
```
